# Optimizing a Trainium2 kernel written in Bass

```python
import numpy as np
import jax
import jax.numpy as jnp

def _softmax(x, axis=-1):
    return jax.nn.softmax(x, axis=axis)
def _gelu(x):
    return jax.nn.gelu(x, approximate=True)
def _silu(x):
    return jax.nn.silu(x)
def _sigmoid(x):
    return jax.nn.sigmoid(x)
def _layernorm(x, axis=-1, eps=1e-5):
    m = jnp.mean(x, axis=axis, keepdims=True)
    v = jnp.var(x, axis=axis, keepdims=True)
    return (x - m) / jnp.sqrt(v + eps)
def _scatter_add(tgt, idx, src, axis=0):
    return tgt.at[idx].add(src)
def _segment_sum(src, seg, n):
    return jax.ops.segment_sum(src, seg, n)

kernel_name = 'mk_conv_preact_d2_conv_nhwc128_6751e1'

def setup_inputs(seed: int = 0):
    np.random.seed(seed)
    _w = jnp.asarray
    def _rec_inputs():
        import jax
        import jax.numpy as jnp
        _gk = jax.random.key(seed)
        x = -0.000125 + 0.9999 * jax.random.normal(jax.random.fold_in(_gk, 1), (1, 512, 512, 128), jnp.float32)
        return x
    x = _rec_inputs()
    def _L0_conv_setup():
        import jax, jax.numpy as jnp
        import numpy as np
        EPS = 1e-05

        def _ln(x, g, b):
            m = jnp.mean(x, axis=-1, keepdims=True)
            v = jnp.var(x, axis=-1, keepdims=True)
            return (x - m) / jnp.sqrt(v + EPS) * g + b
        key = jax.random.key(seed)
        ks = jax.random.split(key, 16)
        B, N, CZ, C = (1, 512, 128, 16)
        s_cz = 1.0 / np.sqrt(CZ)
        s_c = 1.0 / np.sqrt(C)

        def lin(k, fan_in, shape):
            return jax.random.uniform(k, shape, jnp.float32, -1.0, 1.0) / np.sqrt(fan_in)
        return {'x': jax.random.normal(ks[0], (B, N, N, CZ), jnp.float32), 'Wa1': lin(ks[1], CZ, (CZ, C)), 'ba1': lin(ks[2], CZ, (C,)), 'Wa2': lin(ks[3], CZ, (CZ, C)), 'ba2': lin(ks[4], CZ, (C,)), 'Wb1': lin(ks[5], CZ, (CZ, C)), 'bb1': lin(ks[6], CZ, (C,)), 'Wb2': lin(ks[7], CZ, (CZ, C)), 'bb2': lin(ks[8], CZ, (C,)), 'ln2_g': jnp.ones((C,), jnp.float32), 'ln2_b': jnp.zeros((C,), jnp.float32), 'Wg': lin(ks[9], CZ, (CZ, CZ)), 'bg': lin(ks[10], CZ, (CZ,)), 'Wz': lin(ks[11], C, (C, CZ)), 'bz': lin(ks[12], C, (CZ,))}
    _L0_conv_all = _L0_conv_setup()
    _L0_conv_in = {k: v for k, v in _L0_conv_all.items() if k in ('Wa1', 'ba1', 'Wa2', 'ba2', 'Wb1', 'bb1', 'Wb2', 'bb2', 'ln2_g', 'ln2_b', 'Wg', 'bg', 'Wz', 'bz', )}
    del _L0_conv_all

    def _L1_conv_setup():
        import jax, jax.numpy as jnp
        import numpy as np
        EPS = 1e-05

        def _layernorm(x, w, b):
            m = jnp.mean(x, axis=-1, keepdims=True)
            v = jnp.mean(jnp.square(x - m), axis=-1, keepdims=True)
            return (x - m) * jax.lax.rsqrt(v + EPS) * w + b

        def _linear(x, w, b):
            return jnp.einsum('...i,oi->...o', x, w) + b
        key = jax.random.key(seed)
        ks = jax.random.split(key, 8)
        B, N, D = (1, 512, 128)
        H = D // 2
        x = jax.random.normal(ks[0], (B, N, N, D), dtype=jnp.float32)
        mask = jax.random.uniform(ks[1], (B, N, N), dtype=jnp.float32)
        s = 0.02
        return {'x': x, 'mask': mask, 'ln1_w': jnp.ones((D,), jnp.float32), 'ln1_b': jnp.zeros((D,), jnp.float32), 'pi_w': jax.random.normal(ks[2], (D, D), jnp.float32) * s, 'pi_b': jnp.zeros((D,), jnp.float32), 'gi_w': jax.random.normal(ks[3], (D, D), jnp.float32) * s, 'gi_b': jnp.ones((D,), jnp.float32), 'ln2_w': jnp.ones((H,), jnp.float32), 'ln2_b': jnp.zeros((H,), jnp.float32), 'po_w': jax.random.normal(ks[4], (D, H), jnp.float32) * s, 'po_b': jnp.zeros((D,), jnp.float32), 'go_w': jax.random.normal(ks[5], (D, H), jnp.float32) * s, 'go_b': jnp.ones((D,), jnp.float32)}
    _L1_conv_all = _L1_conv_setup()
    _L1_conv_in = {k: v for k, v in _L1_conv_all.items() if k in ('mask', 'ln1_w', 'ln1_b', 'pi_w', 'pi_b', 'gi_w', 'gi_b', 'ln2_w', 'ln2_b', 'po_w', 'po_b', 'go_w', 'go_b', )}
    del _L1_conv_all

    return {
        "x": x,
        "L0_conv_Wa1": _L0_conv_in["Wa1"],
        "L0_conv_ba1": _L0_conv_in["ba1"],
        "L0_conv_Wa2": _L0_conv_in["Wa2"],
        "L0_conv_ba2": _L0_conv_in["ba2"],
        "L0_conv_Wb1": _L0_conv_in["Wb1"],
        "L0_conv_bb1": _L0_conv_in["bb1"],
        "L0_conv_Wb2": _L0_conv_in["Wb2"],
        "L0_conv_bb2": _L0_conv_in["bb2"],
        "L0_conv_ln2_g": _L0_conv_in["ln2_g"],
        "L0_conv_ln2_b": _L0_conv_in["ln2_b"],
        "L0_conv_Wg": _L0_conv_in["Wg"],
        "L0_conv_bg": _L0_conv_in["bg"],
        "L0_conv_Wz": _L0_conv_in["Wz"],
        "L0_conv_bz": _L0_conv_in["bz"],
        "L1_conv_mask": _L1_conv_in["mask"],
        "L1_conv_ln1_w": _L1_conv_in["ln1_w"],
        "L1_conv_ln1_b": _L1_conv_in["ln1_b"],
        "L1_conv_pi_w": _L1_conv_in["pi_w"],
        "L1_conv_pi_b": _L1_conv_in["pi_b"],
        "L1_conv_gi_w": _L1_conv_in["gi_w"],
        "L1_conv_gi_b": _L1_conv_in["gi_b"],
        "L1_conv_ln2_w": _L1_conv_in["ln2_w"],
        "L1_conv_ln2_b": _L1_conv_in["ln2_b"],
        "L1_conv_po_w": _L1_conv_in["po_w"],
        "L1_conv_po_b": _L1_conv_in["po_b"],
        "L1_conv_go_w": _L1_conv_in["go_w"],
        "L1_conv_go_b": _L1_conv_in["go_b"],
    }

def reference(x, L0_conv_Wa1, L0_conv_ba1, L0_conv_Wa2, L0_conv_ba2, L0_conv_Wb1, L0_conv_bb1, L0_conv_Wb2, L0_conv_bb2, L0_conv_ln2_g, L0_conv_ln2_b, L0_conv_Wg, L0_conv_bg, L0_conv_Wz, L0_conv_bz, L1_conv_mask, L1_conv_ln1_w, L1_conv_ln1_b, L1_conv_pi_w, L1_conv_pi_b, L1_conv_gi_w, L1_conv_gi_b, L1_conv_ln2_w, L1_conv_ln2_b, L1_conv_po_w, L1_conv_po_b, L1_conv_go_w, L1_conv_go_b):
    import jax
    import jax.numpy as jnp
    def _L0_conv_ref(x, Wa1, ba1, Wa2, ba2, Wb1, bb1, Wb2, bb2, ln2_g, ln2_b, Wg, bg, Wz, bz):
        import jax, jax.numpy as jnp
        import numpy as np
        EPS = 1e-05

        def _ln(x, g, b):
            m = jnp.mean(x, axis=-1, keepdims=True)
            v = jnp.var(x, axis=-1, keepdims=True)
            return (x - m) / jnp.sqrt(v + EPS) * g + b
        direction = 'outgoing'
        a = jax.nn.sigmoid((x @ Wa1 + ba1) * (x @ Wa2 + ba2))
        b = jax.nn.sigmoid((x @ Wb1 + bb1) * (x @ Wb2 + bb2))
        if direction == 'incoming':
            a = jnp.swapaxes(a, 1, 2)
            b = jnp.swapaxes(b, 1, 2)
        g = jax.nn.sigmoid(x @ Wg + bg)
        z = jnp.einsum('bikc,bkjc->bijc', a, b)
        return g * (_ln(z, ln2_g, ln2_b) @ Wz + bz)

    def _L1_conv_ref(x, mask, ln1_w, ln1_b, pi_w, pi_b, gi_w, gi_b, ln2_w, ln2_b, po_w, po_b, go_w, go_b):
        import jax, jax.numpy as jnp
        import numpy as np
        EPS = 1e-05

        def _layernorm(x, w, b):
            m = jnp.mean(x, axis=-1, keepdims=True)
            v = jnp.mean(jnp.square(x - m), axis=-1, keepdims=True)
            return (x - m) * jax.lax.rsqrt(v + EPS) * w + b

        def _linear(x, w, b):
            return jnp.einsum('...i,oi->...o', x, w) + b
        xn = _layernorm(x, ln1_w, ln1_b)
        p = _linear(xn, pi_w, pi_b)
        g = jax.nn.sigmoid(_linear(xn, gi_w, gi_b))
        h = p * g * mask[..., None]
        a1, b1, a2, b2 = jnp.split(h, 4, axis=-1)
        x1 = jnp.einsum('bikd,bjkd->bijd', a1, b1)
        x2 = jnp.einsum('bkid,bkjd->bijd', a2, b2)
        y = jnp.concatenate([x1, x2], axis=-1)
        yn = _layernorm(y, ln2_w, ln2_b)
        return _linear(yn, po_w, po_b) * jax.nn.sigmoid(_linear(yn, go_w, go_b))

    def _gn(v, G=32, eps=1e-5):
        B_, H_, W_, C_ = v.shape
        g = v.reshape(B_, H_, W_, G, C_ // G)
        m = jnp.mean(g, axis=(1, 2, 4), keepdims=True)
        s = jnp.var(g, axis=(1, 2, 4), keepdims=True)
        return ((g - m) / jnp.sqrt(s + eps)).reshape(v.shape)

    def _ln_c(v, eps=1e-6):
        m = jnp.mean(v, axis=-1, keepdims=True)
        s = jnp.var(v, axis=-1, keepdims=True)
        return (v - m) / jnp.sqrt(s + eps)

    def _ln_t(v, eps=1e-5):
        m = jnp.mean(v, axis=-1, keepdims=True)
        s = jnp.var(v, axis=-1, keepdims=True)
        return (v - m) / jnp.sqrt(s + eps)

    def _to_tokens(v):
        B_, H_, W_, C_ = v.shape
        return v.reshape(B_, H_ * W_, C_)
    def _from_tokens(t, like):
        return t.reshape(like.shape)

    x = x + _L0_conv_ref(_gn(x), L0_conv_Wa1, L0_conv_ba1, L0_conv_Wa2, L0_conv_ba2, L0_conv_Wb1, L0_conv_bb1, L0_conv_Wb2, L0_conv_bb2, L0_conv_ln2_g, L0_conv_ln2_b, L0_conv_Wg, L0_conv_bg, L0_conv_Wz, L0_conv_bz)
    x = x + _L1_conv_ref(_gn(x), L1_conv_mask, L1_conv_ln1_w, L1_conv_ln1_b, L1_conv_pi_w, L1_conv_pi_b, L1_conv_gi_w, L1_conv_gi_b, L1_conv_ln2_w, L1_conv_ln2_b, L1_conv_po_w, L1_conv_po_b, L1_conv_go_w, L1_conv_go_b)
    return x


_drawn_inputs = setup_inputs


def setup_inputs(seed=0):
    import zlib

    import numpy as np

    out = dict(_drawn_inputs(seed))
    spreads = {'L0_conv_ln2_g': (1.0, 0.2),
     'L0_conv_ln2_b': (0.0, 0.319),
     'L1_conv_ln1_w': (1.0, 0.6),
     'L1_conv_ln1_b': (0.0, 0.1),
     'L1_conv_pi_b': (0.0, 0.1),
     'L1_conv_gi_b': (1.0, 0.6),
     'L1_conv_ln2_w': (1.0, 0.6),
     'L1_conv_ln2_b': (0.0, 0.777),
     'L1_conv_po_b': (0.0, 0.1),
     'L1_conv_go_b': (1.0, 0.6)}
    factors = {'L0_conv_ba2': 3.306,
     'L0_conv_bb2': 3.336,
     'L0_conv_bg': 7.894,
     'L1_conv_gi_w': 8.0,
     'L1_conv_go_w': 8.0}
    for name, (base, spread) in spreads.items():
        noise = np.random.default_rng([zlib.crc32(name.encode()), seed]).standard_normal(out[name].shape)
        drawn = base * np.exp(spread * noise) if base else spread * noise
        out[name] = jnp.asarray(drawn.astype(out[name].dtype))
    for name, factor in factors.items():
        out[name] = (out[name] * factor).astype(out[name].dtype)
    return out
```

```python
import concourse.bass as bass
from concourse import mybir
from contextlib import ExitStack

FP32 = mybir.dt.float32
BF16 = mybir.dt.bfloat16
ALU = mybir.AluOpType
ACT = mybir.ActivationFunctionType
AX = mybir.AxisListType

P = 128
BANK = 512
GN_EPS = 1e-5
LN_EPS = 1e-5


class Scope:

    def __init__(self, nc, stack, tag):
        self.nc, self.stack, self.tag = nc, stack, tag

    def sbuf(self, name, shape, dtype=FP32):
        return self.stack.enter_context(self.nc.sbuf_tensor(f"{self.tag}_{name}", shape, dtype))

    def psum(self, name, shape, dtype=FP32):
        return self.stack.enter_context(self.nc.psum_tensor(f"{self.tag}_{name}", shape, dtype))

    def sem(self, name):
        return self.stack.enter_context(self.nc.semaphore(f"{self.tag}_{name}"))

    def sems(self, name, n):
        return [self.sem(f"{name}{i}") for i in range(n)]


def column(vector):
    return vector.rearrange("(p a) -> p a", a=1)


def prepare(nc, K, W):
    with ExitStack() as stack:
        s = Scope(nc, stack, "w")
        pi, gi = s.sbuf("pi", [P, P]), s.sbuf("gi", [P, P])
        po, go = s.sbuf("po", [P, 64]), s.sbuf("go", [P, 64])
        cols = s.sbuf("cols", [P, 12])
        transposed = s.sbuf("transposed", [P, 4, P])
        center = s.sbuf("center", [P, P])
        center64 = s.sbuf("center64", [64, P])
        ps_t = s.psum("ps_t", [P, 4, P])
        ps_b = s.psum("ps_b", [P, BANK])
        ps_c = s.psum("ps_c", [P, 4, P])
        loaded, built, turned, kept = s.sem("loaded"), s.sem("built"), s.sem("turned"), s.sem("kept")
        biased, centred, done = s.sem("biased"), s.sem("centred"), s.sem("done")
        loads = [
            (K.Wa[:, 0:16], W["Wa1"]), (K.Wa[:, 16:32], W["Wa2"]),
            (K.Wb[:, 0:16], W["Wb1"]), (K.Wb[:, 16:32], W["Wb2"]),
            (K.bias_a[:, 0:16], W["ba1"].partition_broadcast(P)), (K.bias_a[:, 16:32], W["ba2"].partition_broadcast(P)),
            (K.bias_b[:, 0:16], W["bb1"].partition_broadcast(P)), (K.bias_b[:, 16:32], W["bb2"].partition_broadcast(P)),
            (K.Wg[:], W["Wg"]), (K.bg[:], column(W["bg"])), (K.Wz_raw[:], W["Wz"]),
            (pi[:], W["pi_w"]), (gi[:], W["gi_w"]), (po[:], W["po_w"]), (go[:], W["go_w"]),
            (cols[:, 0:1], column(W["bz"])), (cols[:, 1:2], column(W["pi_b"])), (cols[:, 2:3], column(W["gi_b"])),
            (cols[:, 3:4], column(W["po_b"])), (cols[:, 4:5], column(W["go_b"])),
            (cols[:, 5:6], column(W["ln1_w"])), (cols[:, 6:7], column(W["ln1_b"])),
            (cols[0:64, 7:8], column(W["ln2_w"])), (cols[64:128, 7:8], column(W["ln2_w"])),
            (cols[0:64, 8:9], column(W["ln2_b"])),
            (cols[0:16, 9:10], column(W["ln2_g0"])), (cols[0:16, 10:11], column(W["ln2_b0"])),
        ]
        with nc.Block() as block:
            @block.sync
            def _(sp):
                for dst, src in loads:
                    sp.dma_start(dst, src).then_inc(loaded, 16)
                sp.wait_ge(loaded, 16 * len(loads))

            @block.gpsimd
            def _(pool):
                n = 0

                def step(ins):
                    nonlocal n
                    ins.then_inc(built, 1)
                    n += 1
                    pool.wait_ge(built, n)

                def diagonal(tile, pattern, base=0):
                    step(pool.affine_select(out=tile, in_=tile, compare_op=ALU.not_equal, fill=1.0, base=base,
                                            pattern=pattern, channel_multiplier=1))

                step(pool.memset(K.ident[:], 0.0))
                diagonal(K.ident[:], [[-1, P]])
                step(pool.memset(K.ident_bf[:], 0.0))
                diagonal(K.ident_bf[:], [[-1, P]])
                step(pool.memset(K.group_mean[:], 0.25))
                view = K.group_mean[:].rearrange("p (g c) -> p g c", c=4)
                step(pool.affine_select(out=view, in_=view, compare_op=ALU.is_ge, fill=0.0, base=0,
                                        pattern=[[-4, 32], [0, 4]], channel_multiplier=1))
                step(pool.affine_select(out=view, in_=view, compare_op=ALU.is_ge, fill=0.0, base=3,
                                        pattern=[[4, 32], [0, 4]], channel_multiplier=-1))
                step(pool.memset(K.select16[:], 0.0))
                for part in range(3):
                    diagonal(K.select16[:], [[-1, 16], [0, P]], base=-16 * part)
                step(pool.memset(K.halves[:], 1.0))
                step(pool.affine_select(out=K.halves[:, 0:64], in_=K.halves[:, 0:64], compare_op=ALU.is_ge, fill=0.0,
                                        base=2, pattern=[[0, 64]], channel_multiplier=-1))
                step(pool.affine_select(out=K.halves[:, 64:128], in_=K.halves[:, 64:128], compare_op=ALU.is_ge,
                                        fill=0.0, base=-3, pattern=[[0, 64]], channel_multiplier=1))
                step(pool.memset(K.mean_col[:], 1.0 / P))
                step(pool.memset(K.mean_square[:], 1.0 / P))
                pool.memset(K.minus_half[:], -0.5).then_inc(built, 1)

            BUILT = 17

            @block.tensor
            def _(pe):
                pe.wait_ge(built, BUILT)
                pe.wait_ge(loaded, 16 * len(loads))
                pe.transpose(ps_t[:, 0, :], pi[:], K.ident[:]).then_inc(turned, 1)
                pe.transpose(ps_t[:, 1, :], gi[:], K.ident[:]).then_inc(turned, 1)
                pe.transpose(ps_t[0:64, 2, :], po[:], K.ident[:]).then_inc(turned, 1)
                pe.transpose(ps_t[0:64, 3, :], go[:], K.ident[:]).then_inc(turned, 1)
                pe.wait_ge(kept, 1)
                for n, (w, rows, b) in enumerate([(transposed[:, 0, :], P, 6), (transposed[:, 1, :], P, 6),
                                                  (transposed[0:64, 2, :], 64, 8), (transposed[0:64, 3, :], 64, 8),
                                                  (K.Wz_raw[:], 16, 10)]):
                    pe.matmul(ps_b[:, n:n + 1], w, cols[0:rows, b:b + 1], start=True, stop=True).then_inc(biased, 1)
                pe.wait_ge(kept, 2)
                pe.matmul(ps_c[:, 0, :], center[:], transposed[:, 0, :], start=True, stop=True).then_inc(centred, 1)
                pe.matmul(ps_c[:, 1, :], center[:], transposed[:, 1, :], start=True, stop=True).then_inc(centred, 1)
                pe.matmul(ps_c[:, 2, :], center64[:], transposed[0:64, 2, :], start=True, stop=True).then_inc(centred, 1)
                pe.matmul(ps_c[:, 3, :], center64[:], transposed[0:64, 3, :], start=True, stop=True).then_inc(centred, 1)

            @block.vector
            def _(dve):
                dve.wait_ge(turned, 4)
                for n in range(4):
                    rows = P if n < 2 else 64
                    last = dve.tensor_copy(transposed[0:rows, n, :], ps_t[0:rows, n, :])
                last.then_inc(kept, 1)
                dve.wait_ge(built, BUILT)
                dve.tensor_scalar(center[:], K.ident[:], -1.0 / P, None, ALU.add)
                dve.tensor_scalar(center64[:, 0:64], K.ident[0:64, 0:64], -1.0 / 64, None, ALU.add)
                dve.tensor_scalar(center64[:, 64:128], K.ident[0:64, 0:64], -1.0 / 64, None, ALU.add)
                dve.wait_ge(biased, 5)
                for n, col in ((0, 5), (1, 5), (2, 7), (3, 7)):
                    rows = P if n < 2 else 64
                    last = dve.tensor_scalar(transposed[0:rows, n, :], transposed[0:rows, n, :],
                                             cols[0:rows, col:col + 1], None, ALU.mult)
                last.then_inc(kept, 1)
                dve.tensor_tensor(K.pi_bias[:], ps_b[:, 0:1], cols[:, 1:2], ALU.add)
                dve.tensor_tensor(K.gi_bias[:], ps_b[:, 1:2], cols[:, 2:3], ALU.add)
                dve.tensor_tensor(K.po_bias[:], ps_b[:, 2:3], cols[:, 3:4], ALU.add)
                dve.tensor_tensor(K.go_bias[:], ps_b[:, 3:4], cols[:, 4:5], ALU.add)
                dve.tensor_tensor(K.z_bias[:], ps_b[:, 4:5], cols[:, 0:1], ALU.add)
                dve.tensor_scalar(K.Wz[:], K.Wz_raw[:], cols[0:16, 9:10], None, ALU.mult)
                dve.wait_ge(centred, 4)
                dve.tensor_copy(K.Wpi[:], ps_c[:, 0, :])
                dve.tensor_copy(K.Wgi[:], ps_c[:, 1, :])
                for n, w in ((2, K.Wpo), (3, K.Wgo)):
                    for e in range(2):
                        own, other = slice(64 * e, 64 * e + 64), slice(64 - 64 * e, 128 - 64 * e)
                        dve.memset(w[other, e, :], 0.0)
                        last = dve.tensor_copy(w[own, e, :], ps_c[own, n, :])
                last.then_inc(done, 1)


def norm_from_moments(nc, s, block, K, moments, moments_ready):
    var, deviation = s.sbuf("gn_var", [P, 1]), s.sbuf("gn_dev", [P, 1])
    chain, var_ready, dev_ready = s.sem("gn_chain"), s.sem("gn_var_ready"), s.sem("gn_dev_ready")

    def vector_part(dve):
        dve.wait_ge(moments_ready, 2)
        dve.tensor_copy(K.gn_mean[:], moments[:, 0:1]).then_inc(chain, 1)
        dve.wait_ge(chain, 1)
        dve.tensor_tensor(var[:], K.gn_mean[:], K.gn_mean[:], ALU.mult).then_inc(chain, 1)
        dve.wait_ge(chain, 2)
        dve.tensor_tensor(var[:], moments[:, 1:2], var[:], ALU.subtract).then_inc(chain, 1)
        dve.wait_ge(chain, 3)
        dve.tensor_scalar(var[:], var[:], GN_EPS, None, ALU.add).then_inc(var_ready, 1)
        dve.wait_ge(dev_ready, 1)
        dve.reciprocal(K.gn_scale[:], deviation[:]).then_inc(chain, 1)
        dve.wait_ge(chain, 4)
        dve.scalar_tensor_tensor(K.gn_shift[:], K.gn_mean[:], -1.0, K.gn_scale[:], ALU.mult, ALU.mult).then_inc(chain, 1)
        dve.wait_ge(chain, 5)

    def scalar_part(act):
        act.wait_ge(var_ready, 1)
        act.activation(deviation[:], var[:], ACT.Sqrt).then_inc(dev_ready, 1)

    return vector_part, scalar_part


def stage1_statistics(nc, K, x, N):
    T = 128
    chunks = N * N // P // T
    x_v = x.rearrange("(p n t) c -> n p t c", p=P, t=T)
    with ExitStack() as stack:
        s = Scope(nc, stack, "s1")
        xt = s.sbuf("xt", [P, 2, T, P])
        stats = s.sbuf("stats", [P, 32, chunks, 6])
        mv = s.sbuf("mv", [P, 32, 2])
        square = s.sbuf("square", [P, 32])
        wide = s.sbuf("wide", [P, 2, 32, 4])
        moments = s.psum("moments", [P, 2])
        loaded = s.sems("loaded", 2)
        used, aggregated, wide_ready, moments_ready = s.sem("used"), s.sem("aggregated"), s.sem("wide_ready"), s.sem("moments_ready")
        with nc.Block() as block:
            norm_vector, norm_scalar = norm_from_moments(nc, s, block, K, moments, moments_ready)

            @block.sync
            def _(sp):
                with sp.Fori(0, chunks // 2) as r:
                    for u in range(2):
                        sp.wait_ge(used, r * 2 + (u + 1))
                        sp.dma_start(xt[:, u, :, :], x_v[bass.ds(r * 2 + u, 1)].rearrange("a p t c -> p (a t) c")).then_inc(loaded[u], 16)

            @block.vector
            def _(dve):
                dve.sem_inc(used, 2)
                with dve.Fori(0, chunks // 2) as r:
                    for u in range(2):
                        dve.wait_ge(loaded[u], r * 16 + 16)
                        for g in range(32):
                            last = dve.bn_stats(stats[:, g, bass.ds(r * 2 + u, 1), :].rearrange("p a s -> p (a s)"),
                                                xt[:, u, :, 4 * g:4 * g + 4])
                        last.then_inc(used, 1)
                dve.wait_ge(used, chunks + 2)
                for g in range(32):
                    dve.bn_aggr(mv[:, g, :], stats[:, g, :, :].rearrange("p n s -> p (n s)")).then_inc(aggregated, 1)
                dve.wait_ge(aggregated, 32)
                dve.tensor_tensor(square[:], mv[:, :, 0], mv[:, :, 0], ALU.mult).then_inc(aggregated, 1)
                dve.tensor_copy(wide[:, 0, :, :], mv[:, :, 0:1].to_broadcast([P, 32, 4]))
                dve.wait_ge(aggregated, 33)
                dve.tensor_tensor(square[:], square[:], mv[:, :, 1], ALU.add).then_inc(aggregated, 1)
                dve.wait_ge(aggregated, 34)
                dve.tensor_copy(wide[:, 1, :, :], square[:].rearrange("p (g a) -> p g a", a=1).to_broadcast([P, 32, 4])).then_inc(wide_ready, 1)
                norm_vector(dve)

            @block.tensor
            def _(pe):
                pe.wait_ge(wide_ready, 1)
                for m in range(2):
                    pe.matmul(moments[:, m:m + 1], wide[:, m, :, :].rearrange("p g c -> p (g c)"), K.mean_col[:],
                              start=True, stop=True).then_inc(moments_ready, 1)

            @block.scalar
            def _(act):
                norm_scalar(act)


def stage2_gates(nc, K, x, a_d, b_d, N):
    RB = N // P
    ROWS, UNITS = 8, 32
    x_v = x.rearrange("(rb n r j) c -> rb n j r c", rb=RB, r=ROWS, j=N)
    with ExitStack() as stack:
        s = Scope(nc, stack, "s2")
        xt = s.sbuf("xt", [P, 4, ROWS, P])
        xh = s.sbuf("xh", [P, P, P])
        pre = s.sbuf("pre", [P, 2, 16, 32])
        gate = s.sbuf("gate", [P, 2, 16, 16])
        ab = s.sbuf("ab", [P, 2, 16, P])
        turned_ps = s.psum("turned_ps", [P, 4, BANK])
        proj_ps = s.psum("proj_ps", [P, 4, BANK])
        loaded = s.sems("loaded", 4)
        turned, normed, projected = s.sem("turned"), s.sem("normed"), s.sem("projected")
        biased, gated, sig, stored, left = s.sem("biased"), s.sem("gated"), s.sem("sig"), s.sem("stored"), s.sem("left")

        @block_of(nc)
        def _(block):
            @block.sync
            def _(sp):
                with sp.Fori(0, RB) as rb:
                    with sp.Fori(0, RB) as cb:
                        g = rb * RB + cb
                        for n in range(16):
                            sp.wait_ge(turned, g * UNITS + (2 * n + 2))
                            src = x_v[bass.ds(rb, 1), n, bass.ds(cb * P, P)].rearrange("a j r c -> (a j) r c")
                            sp.dma_start(xt[:, n % 4, :, :], src).then_inc(loaded[n % 4], 16)

            @block.tensor
            def _(pe):
                pe.sem_inc(turned, 8)
                pe.sem_inc(projected, 16)
                with pe.Fori(0, RB * RB) as g:
                    for q in range(8):
                        for u in range(4 * q, 4 * q + 4):
                            if u % 2 == 0:
                                pe.wait_ge(loaded[u // 2 % 4], g * 64 + 16 * (u // 8 + 1))
                            pe.wait_ge(normed, g * UNITS + (u + 1))
                            for r in range(4):
                                last = pe.transpose(turned_ps[:, u % 4, r * P:(r + 1) * P],
                                                    xt[:, u // 2 % 4, 4 * (u % 2) + r, :], K.ident[:])
                            last.then_inc(turned, 1)
                        pe.wait_ge(biased, g * 16 + (q + 1))
                        for u in range(4 * q, 4 * q + 4):
                            pe.wait_ge(normed, g * UNITS + (u + 5))
                            for r in range(4 * u, 4 * u + 4):
                                last = pe.matmul(proj_ps[:, q % 4, 32 * (r % 16):32 * (r % 16) + 32], xh[:, r, :],
                                                 K.Wa[:], start=True, stop=True)
                        last.then_inc(projected, 1)
                    for q in range(8):
                        pe.wait_ge(biased, g * 16 + (q + 9))
                        for j in range(16 * q, 16 * q + 16):
                            last = pe.matmul(proj_ps[:, q % 4, 32 * (j % 16):32 * (j % 16) + 32], xh[:, :, j],
                                             K.Wb[:], start=True, stop=True)
                        last.then_inc(projected, 1)

            def finish_sigmoid(act, g, q):
                act.wait_ge(gated, g * 16 + (q + 1))
                if q % 8 == 0:
                    act.wait_ge(left, g * 2 + (q // 8 + 1))
                act.activation(ab[:, q // 8, :, 16 * (q % 8):16 * (q % 8) + 16], gate[:, q % 2, :, :].rearrange("p r c -> p c r"),
                               ACT.Sigmoid).then_inc(sig, 1)

            @block.scalar
            def _(act):
                act.sem_inc(normed, 4)
                act.sem_inc(sig, 2)
                with act.Fori(0, RB * RB) as g:
                    act.wait_ge(projected, g * 16 + 16)
                    for q in range(8):
                        for u in range(4 * q, 4 * q + 4):
                            act.wait_ge(turned, g * UNITS + (u + 9))
                            act.activation(xh[:, 4 * u:4 * u + 4, :], turned_ps[:, u % 4, :].rearrange("p (r j) -> p r j", j=P),
                                           ACT.Identity, bias=K.gn_shift[:], scale=K.gn_scale[:]).then_inc(normed, 1)
                        if q >= 1:
                            finish_sigmoid(act, g, q - 1)
                    for q in range(7, 16):
                        finish_sigmoid(act, g, q)

            @block.vector
            def _(dve):
                dve.sem_inc(biased, 4)
                with dve.Fori(0, RB * RB) as g:
                    for q in range(16):
                        bias = K.bias_a if q < 8 else K.bias_b
                        dve.wait_ge(projected, g * 16 + (q + 17))
                        dve.wait_ge(sig, g * 16 + (q + 1))
                        dve.tensor_tensor(pre[:, q % 2, :, :], proj_ps[:, q % 4, :].rearrange("p (r c) -> p r c", c=32),
                                          bias[:].rearrange("p (a c) -> p a c", a=1).to_broadcast([P, 16, 32]),
                                          ALU.add).then_inc(biased, 1)
                        dve.wait_ge(biased, g * 16 + (q + 5))
                        dve.tensor_tensor(gate[:, q % 2, :, :], pre[:, q % 2, :, 0:16], pre[:, q % 2, :, 16:32],
                                          ALU.mult).then_inc(gated, 1)

            @block.gpsimd
            def _(pool):
                pool.sem_inc(left, 2)
                with pool.Fori(0, RB) as rb:
                    with pool.Fori(0, RB) as cb:
                        g = rb * RB + cb
                        pool.wait_ge(sig, g * 16 + 10)
                        pool.dma_start(a_d[bass.ds(cb, 1), :, :, bass.ds(rb * P, P)].rearrange("a p c i -> (a p) c i"),
                                       ab[:, 0, :, :]).then_inc(stored, 16)
                        pool.wait_ge(stored, g * 32 + 16)
                        pool.sem_inc(left, 1)
                        pool.wait_ge(sig, g * 16 + 18)
                        pool.dma_start(b_d[bass.ds(rb, 1), :, :, bass.ds(cb * P, P)].rearrange("a p c i -> (a p) c i"),
                                       ab[:, 1, :, :]).then_inc(stored, 16)
                        pool.wait_ge(stored, g * 32 + 32)
                        pool.sem_inc(left, 1)


def block_of(nc):
    def run(build):
        with nc.Block() as block:
            build(block)
    return run


def stage3_triangle(nc, K, a_d, b_d, z_d, N):
    RB, C, SLOTS = N // P, 16, 4
    with ExitStack() as stack:
        s = Scope(nc, stack, "s3")
        at = s.sbuf("at", [P, SLOTS, RB, P])
        bt = s.sbuf("bt", [P, SLOTS, RB, N])
        z = s.sbuf("z", [P, C, N])
        centred = s.sbuf("centred", [P, C, N])
        squares = s.sbuf("squares", [P, C, N])
        mean, var, dev = s.sbuf("mean", [P, N]), s.sbuf("var", [P, N]), s.sbuf("dev", [P, N])
        z_ps = s.psum("z_ps", [P, 8, BANK])
        loaded = s.sems("loaded", SLOTS)
        product, copied, chain, cent, sq, var_ready, dev_ready, z_ready, stored, left = [
            s.sem(n) for n in ("product", "copied", "chain", "cent", "sq", "var_ready", "dev_ready", "z_ready", "stored", "left")]
        CHAIN = 4

        @block_of(nc)
        def _(block):
            @block.sync
            def _(sp):
                with sp.Fori(0, RB) as ib:
                    for c in range(C):
                        sp.wait_ge(product, ib * C + (c + 1))
                        sp.dma_start(at[:, c % SLOTS, :, :], a_d[:, :, c, bass.ds(ib * P, P)].rearrange("k p i -> p k i")).then_inc(loaded[c % SLOTS], 16)
                        sp.dma_start(bt[:, c % SLOTS, :, :], b_d[:, :, c, :].rearrange("k p j -> p k j")).then_inc(loaded[c % SLOTS], 16)

            @block.tensor
            def _(pe):
                pe.sem_inc(product, SLOTS)
                with pe.Fori(0, RB) as ib:
                    for c in range(C):
                        pe.wait_ge(loaded[c % SLOTS], ib * (32 * C // SLOTS) + 32 * (c // SLOTS + 1))
                        pe.wait_ge(copied, ib * C + (c + 1))
                        for kb in range(RB):
                            last = pe.matmul(z_ps[:, c % 8, 0:N], at[:, c % SLOTS, kb, :], bt[:, c % SLOTS, kb, :],
                                             start=kb == 0, stop=kb == RB - 1)
                        last.then_inc(product, 1)

            @block.scalar
            def _(act):
                act.sem_inc(copied, 8)
                with act.Fori(0, RB) as ib:
                    act.wait_ge(cent, ib + 1)
                    for c in range(C):
                        act.wait_ge(product, ib * C + (c + 1 + SLOTS))
                        act.activation(z[:, c, :], z_ps[:, c % 8, 0:N], ACT.Copy).then_inc(copied, 1)
                    act.wait_ge(cent, ib + 2)
                    act.activation(squares[:], centred[:], ACT.Square).then_inc(sq, 1)
                    act.wait_ge(var_ready, ib + 1)
                    act.activation(dev[:], var[:], ACT.Sqrt).then_inc(dev_ready, 1)

            @block.vector
            def _(dve):
                dve.sem_inc(cent, 1)

                def over_channels(tile):
                    return tile[:].rearrange("p c j -> p j c")

                def every_channel(tile):
                    return tile[:].rearrange("p (a j) -> p a j", a=1).to_broadcast([P, C, N])

                with dve.Fori(0, RB) as ib:
                    dve.wait_ge(copied, ib * C + (C + 8))
                    dve.tensor_reduce(mean[:], over_channels(z), AX.X, ALU.add).then_inc(chain, 1)
                    dve.wait_ge(chain, ib * CHAIN + 1)
                    dve.tensor_scalar(mean[:], mean[:], 1.0 / C, None, ALU.mult).then_inc(chain, 1)
                    dve.wait_ge(chain, ib * CHAIN + 2)
                    dve.wait_ge(left, ib + 1)
                    dve.tensor_tensor(centred[:], z[:], every_channel(mean), ALU.subtract).then_inc(cent, 1)
                    dve.wait_ge(sq, ib + 1)
                    dve.tensor_reduce(var[:], over_channels(squares), AX.X, ALU.add).then_inc(chain, 1)
                    dve.wait_ge(chain, ib * CHAIN + 3)
                    dve.tensor_scalar(var[:], var[:], 1.0 / C, LN_EPS, ALU.mult, ALU.add).then_inc(var_ready, 1)
                    dve.wait_ge(dev_ready, ib + 1)
                    dve.reciprocal(dev[:], dev[:]).then_inc(chain, 1)
                    dve.wait_ge(chain, ib * CHAIN + 4)
                    dve.tensor_tensor(centred[:], centred[:], every_channel(dev), ALU.mult).then_inc(z_ready, 1)

            @block.gpsimd
            def _(pool):
                pool.sem_inc(left, 1)
                with pool.Fori(0, RB) as ib:
                    pool.wait_ge(z_ready, ib + 1)
                    pool.dma_start(z_d[:, bass.ds(ib * P, P), :].rearrange("c i j -> i c j"), centred[:]).then_inc(stored, 16)
                    pool.wait_ge(stored, ib * 16 + 16)
                    pool.sem_inc(left, 1)


def stage4_layer0(nc, K, x, z_d, x1_d, N):
    CB, U = N // P, 4
    x_v = x.rearrange("(i q p) c -> p i q c", q=CB, p=P)
    with ExitStack() as stack:
        s = Scope(nc, stack, "s4")
        xt = s.sbuf("xt", [P, 4, 2, CB, P])
        zt = s.sbuf("zt", [16, 2, U, N])
        xT = s.sbuf("xT", [P, U, N])
        g = s.sbuf("g", [P, 2, N])
        gz = s.sbuf("gz", [P, 2, N])
        x1T = s.sbuf("x1T", [P, 4, 2, N])
        stats = s.sbuf("stats", [P, N, 6])
        mv = s.sbuf("mv", [P, 2])
        pair = s.sbuf("pair", [P, 2])
        Wg = s.sbuf("Wg", [P, P])
        bg = s.sbuf("bg", [P, 1])
        x_ps = s.psum("x_ps", [P, 4, BANK])
        g_ps = s.psum("g_ps", [P, 2, BANK])
        z_ps = s.psum("z_ps", [P, 2, BANK])
        loaded, z_loaded, stored = s.sems("loaded", 4), s.sems("z_loaded", 2), s.sems("stored", 4)
        turned, kept, g_prod, z_prod, sig, mixed, added, counted = [
            s.sem(n) for n in ("turned", "kept", "g_prod", "z_prod", "sig", "mixed", "added", "counted")]
        folded, shifted, moments_ready, chain = s.sem("folded"), s.sem("shifted"), s.sem("moments_ready"), s.sem("chain")

        @block_of(nc)
        def _(block):
            moments = g_ps[:, 0, 0:2]
            norm_vector, norm_scalar = norm_from_moments(nc, s, block, K, moments, moments_ready)

            @block.sync
            def _(sp):
                def load(r, n):
                    sp.wait_ge(turned, r * 8 + (2 * n + 2))
                    sp.dma_start(xt[:, n, :, :, :], x_v[:, bass.ds(r * 8 + 2 * n, 2)]).then_inc(loaded[n], 16)
                    if n % 2 == 0:
                        sp.wait_ge(z_prod, r * 8 + (2 * n + 4))
                        sp.dma_start(zt[:, n // 2, :, :], z_d[:, bass.ds(r * 8 + 2 * n, U), :]).then_inc(z_loaded[n // 2], 16)

                def store(r, n):
                    sp.wait_ge(added, r * 8 + (2 * n + 6))
                    sp.dma_start(x1_d[:, bass.ds(r * 8 + 2 * n, 2), :], x1T[:, n, :, :]).then_inc(stored[n], 16)

                for n in range(4):
                    sp.sem_inc(stored[n], 16)
                    load(0, n)
                with sp.Fori(0, N // 8 - 1) as r:
                    for n in range(4):
                        store(r, n)
                        load(r + 1, n)
                for n in range(4):
                    store(N // 8 - 1, n)
                for n in range(4):
                    sp.wait_ge(stored[n], 2 * N + 16)

            @block.tensor
            def _(pe):
                pe.sem_inc(turned, 8)
                pe.sem_inc(z_prod, 8)
                pe.matmul(g_ps[:, 0, 0:1], K.Wg[:], K.gn_shift[:], start=True, stop=True).then_inc(shifted, 1)
                pe.wait_ge(folded, 2)
                with pe.Fori(0, N // 8) as r:
                    for h in range(2):
                        for u in range(U):
                            i = 4 * h + u
                            if u % 2 == 0:
                                pe.wait_ge(loaded[i // 2], r * 16 + 16)
                            pe.wait_ge(kept, r * 8 + (i + 1))
                            for q in range(CB):
                                last = pe.transpose(x_ps[:, u, q * P:(q + 1) * P], xt[:, i // 2, i % 2, q, :], K.ident[:])
                            last.then_inc(turned, 1)
                        pe.wait_ge(z_loaded[h], r * 16 + 16)
                        for u in range(U):
                            i = 4 * h + u
                            pe.wait_ge(mixed, r * 8 + (i + 1))
                            pe.matmul(z_ps[:, u % 2, 0:N], K.Wz[:], zt[:, h, u, :], start=True, stop=True).then_inc(z_prod, 1)
                            pe.wait_ge(kept, r * 8 + (i + 5))
                            pe.matmul(g_ps[:, u % 2, 0:N], Wg[:], xT[:, u, :], start=True, stop=True).then_inc(g_prod, 1)
                pe.wait_ge(chain, 3)
                for m in range(2):
                    pe.matmul(moments[:, m:m + 1], K.group_mean[:], pair[:, m:m + 1], start=True, stop=True).then_inc(moments_ready, 1)

            @block.scalar
            def _(act):
                act.sem_inc(kept, 4)
                with act.Fori(0, N // 8) as r:
                    for h in range(2):
                        for step in range(U + 1):
                            if step < U:
                                i = 4 * h + step
                                act.wait_ge(turned, r * 8 + (i + 9))
                                act.wait_ge(added, r * 8 + (i + 1))
                                act.activation(xT[:, step, :], x_ps[:, step, 0:N], ACT.Copy).then_inc(kept, 1)
                            if step >= 1:
                                i = 4 * h + step - 1
                                act.wait_ge(g_prod, r * 8 + (i + 1))
                                act.activation(g[:, i % 2, :], g_ps[:, i % 2, 0:N], ACT.Sigmoid, bias=bg[:]).then_inc(sig, 1)
                norm_scalar(act)

            @block.vector
            def _(dve):
                dve.sem_inc(mixed, 2)
                dve.tensor_scalar(Wg[:], K.Wg[:], K.gn_scale[:], None, ALU.mult).then_inc(folded, 1)
                dve.wait_ge(shifted, 1)
                dve.tensor_tensor(bg[:], g_ps[:, 0, 0:1], K.bg[:], ALU.add).then_inc(folded, 1)

                def statistics(r, i):
                    dve.wait_ge(added, r * 8 + (i + 5))
                    dve.bn_stats(stats[:, bass.ds(r * 8 + i, 1), :].rearrange("p a s -> p (a s)"),
                                 x1T[:, i // 2, i % 2, :]).then_inc(counted, 1)

                dve.sem_inc(counted, 8)
                with dve.Fori(0, N // 8) as r:
                    for i in range(8):
                        dve.wait_ge(sig, r * 8 + (i + 1))
                        dve.wait_ge(z_prod, r * 8 + (i + 9))
                        dve.wait_ge(added, r * 8 + (i + 3))
                        dve.scalar_tensor_tensor(gz[:, i % 2, :], z_ps[:, i % 2, 0:N], K.z_bias[:], g[:, i % 2, :],
                                                 ALU.add, ALU.mult).then_inc(mixed, 1)
                        if i >= 1:
                            statistics(r, i - 1)
                    statistics(r, 7)
                dve.wait_ge(counted, N + 8)
                dve.bn_aggr(mv[:], stats[:].rearrange("p n s -> p (n s)")).then_inc(chain, 1)
                dve.wait_ge(chain, 1)
                dve.tensor_copy(pair[:, 0:1], mv[:, 0:1])
                dve.tensor_tensor(pair[:, 1:2], mv[:, 0:1], mv[:, 0:1], ALU.mult).then_inc(chain, 1)
                dve.wait_ge(chain, 2)
                dve.tensor_tensor(pair[:, 1:2], pair[:, 1:2], mv[:, 1:2], ALU.add).then_inc(chain, 1)
                norm_vector(dve)

            @block.gpsimd
            def _(pool):
                pool.sem_inc(added, 4)
                with pool.Fori(0, N // 8) as r:
                    for i in range(8):
                        if i % 2 == 0:
                            pool.wait_ge(stored[i // 2], r * 16 + 16)
                        pool.wait_ge(counted, r * 8 + (i + 1))
                        pool.wait_ge(mixed, r * 8 + (i + 3))
                        pool.tensor_tensor(x1T[:, i // 2, i % 2, :], gz[:, i % 2, :], xT[:, i % 4, :], ALU.add).then_inc(added, 1)


def stage5_project(nc, K, x1_d, mask, h_d, N):
    RB, GROUPS = N // P, 8
    last_region = RB * RB
    with ExitStack() as stack:
        s = Scope(nc, stack, "s5")
        xg = s.sbuf("xg", [P, 2, 16, P])
        xh = s.sbuf("xh", [P, 2, 16, P])
        xc = s.sbuf("xc", [P, 2, BANK])
        gate = s.sbuf("gate", [P, 2, BANK])
        h = s.sbuf("h", [P, P, P])
        out1 = s.sbuf("out1", [P, 64, P])
        out2 = s.sbuf("out2", [P, 64, P])
        mask_n = s.sbuf("mask_n", [P, RB, N])
        mask_t = s.sbuf("mask_t", [P, RB, N])
        stats = s.sbuf("stats", [P, 16, 6])
        spread_m, within, var, rstd, rest = [s.sbuf(n, [P, 16]) for n in ("spread_m", "within", "var", "rstd", "rest")]
        parts = s.sbuf("parts", [P, 48], BF16)
        rows = s.sbuf("rows", [48, 2, P], BF16)
        x_ps = s.psum("x_ps", [P, 2, BANK])
        rstd_ps = s.psum("rstd_ps", [P, BANK])
        p_ps = s.psum("p_ps", [P, 2, BANK])
        g_ps = s.psum("g_ps", [P, BANK])
        t_ps = s.psum("t_ps", [P, 2, BANK])
        parts_ps = x_ps[0:48, 0, 0:64].bitcast(BF16)
        loaded = s.sems("loaded", 2)
        mask_loaded, mask_turned, mask_kept = [s.sem(n) for n in ("mask_loaded", "mask_turned", "mask_kept")]
        normed, x_turned, counted, var_ready, rstd_ready, parts_ready, parts_turned, rows_ready, chain = [
            s.sem(n) for n in ("normed", "x_turned", "counted", "var_ready", "rstd_ready", "parts_ready", "parts_turned", "rows_ready", "chain")]
        spread, scaled, p_done, g_done, sig, h_ready, h_turned, h_kept = [
            s.sem(n) for n in ("spread", "scaled", "p_done", "g_done", "sig", "h_ready", "h_turned", "h_kept")]
        stored, met = s.sems("stored", 2), s.sem("met")
        CHAIN = 8

        @block_of(nc)
        def _(block):
            @block.sync
            def _(sp):
                sp.dma_start(mask_n[:], mask.rearrange("(b p) j -> p b j", p=P)).then_inc(mask_loaded, 16)

                def load(g, q):
                    place = g % last_region
                    sp.wait_ge(normed, g * 8 + (q + 1))
                    src = x1_d[:, bass.ds(place // RB * P + 16 * q, 16), bass.ds(place % RB * P, P)]
                    sp.dma_start(xg[:, q % 2, :, :], src).then_inc(loaded[q % 2], 16)

                for m in range(2):
                    sp.sem_inc(stored[m], 16)
                for q in range(2):
                    load(0, q)
                with sp.Fori(0, last_region) as g:
                    for q in range(2, 8):
                        load(g, q)
                    for q in range(2):
                        load(g + 1, q)
                    sp.wait_ge(h_kept, g * 32 + 18)
                    sp.dma_start(h_d[0, bass.ds(g % RB, 1), :, :, bass.ds(g // RB * P, P)].rearrange("a p c i -> (a p) c i"),
                                 out1[:]).then_inc(stored[0], 16)
                    sp.wait_ge(h_kept, g * 32 + 34)
                    sp.dma_start(h_d[1, bass.ds(g // RB, 1), :, :, bass.ds(g % RB * P, P)].rearrange("a p c i -> (a p) c i"),
                                 out2[:]).then_inc(stored[1], 16)
                for m in range(2):
                    sp.wait_ge(stored[m], 16 * last_region + 16)
                for q in range(2):
                    sp.wait_ge(loaded[q], last_region * 64 + 16)

            @block.scalar
            def _(act):
                act.sem_inc(normed, 2)

                def norm(g, q):
                    act.wait_ge(loaded[q % 2], g * 64 + 16 * (q // 2 + 1))
                    act.wait_ge(scaled, g * 32 + 4 * (q + 1))
                    act.activation(xh[:, q % 2, :, :], xg[:, q % 2, :, :], ACT.Identity, bias=K.gn_shift[:],
                                   scale=K.gn_scale[:]).then_inc(normed, 1)

                def keep_rows(g, q):
                    act.wait_ge(parts_turned, g * 8 + (q + 1))
                    act.activation(rows[:, q % 2, :], parts_ps, ACT.Copy).then_inc(rows_ready, 1)

                act.sem_inc(sig, 1)
                norm(0, 0)
                keep_rows(0, 0)
                with act.Fori(0, last_region) as g:
                    for q in range(GROUPS):
                        norm(g, q + 1)
                        for n in range(4):
                            unit = 4 * q + n
                            act.wait_ge(g_done, g * 32 + (unit + 1))
                            act.wait_ge(h_ready, g * 32 + (unit + 1))
                            act.activation(gate[:, unit % 2, :], g_ps[:], ACT.Sigmoid, bias=K.gi_bias[:]).then_inc(sig, 1)
                            if n == 2:
                                keep_rows(g, q + 1)

            @block.gpsimd
            def _(pool):
                def power(g, q):
                    pool.wait_ge(var_ready, g * 8 + (q + 1))
                    pool.tensor_tensor(rstd[:], var[:], K.minus_half[:], ALU.pow).then_inc(rstd_ready, 1)

                power(0, 0)
                with pool.Fori(0, last_region) as g:
                    for q in range(GROUPS):
                        power(g, q + 1)

            @block.vector
            def _(dve):
                dve.sem_inc(scaled, 8)
                dve.sem_inc(counted, 2)
                dve.sem_inc(h_ready, 2)
                dve.sem_inc(h_kept, 2)
                for b in range(RB):
                    dve.wait_ge(mask_turned, b + 1)
                    dve.tensor_copy(mask_t[:, b, :], t_ps[:, b % 2, 0:N]).then_inc(mask_kept, 1)

                def statistics(g, unit):
                    dve.wait_ge(x_turned, g * 32 + (unit + 1))
                    for r in range(4):
                        last = dve.bn_stats(stats[:, 4 * (unit % 4) + r, :], x_ps[:, unit % 2, r * P:(r + 1) * P])
                    last.then_inc(counted, 1)

                def variance(g, q):
                    base = (g * 8 + q) * CHAIN
                    dve.wait_ge(counted, g * 32 + (4 * q + 6))
                    dve.tensor_tensor(spread_m[:], stats[:, :, 1], stats[:, :, 4], ALU.subtract).then_inc(chain, 1)
                    dve.tensor_tensor(within[:], stats[:, :, 2], stats[:, :, 5], ALU.add).then_inc(chain, 1)
                    dve.wait_ge(chain, base + 2)
                    dve.scalar_tensor_tensor(spread_m[:], spread_m[:], 0.25, spread_m[:], ALU.mult, ALU.mult).then_inc(chain, 1)
                    dve.wait_ge(chain, base + 3)
                    dve.scalar_tensor_tensor(var[:], within[:], 1.0 / P, spread_m[:], ALU.mult, ALU.add).then_inc(chain, 1)
                    dve.wait_ge(chain, base + 4)
                    dve.tensor_scalar(var[:], var[:], LN_EPS, None, ALU.add).then_inc(var_ready, 1)

                def split(g, q):
                    dve.wait_ge(rstd_ready, g * 8 + (q + 1))
                    dve.tensor_copy(parts[:, 0:16], rstd[:]).then_inc(chain, 1)
                    dve.wait_ge(chain, (g * 8 + q) * CHAIN + 5)
                    dve.tensor_tensor(rest[:], rstd[:], parts[:, 0:16], ALU.subtract).then_inc(chain, 1)
                    dve.wait_ge(chain, (g * 8 + q) * CHAIN + 6)
                    dve.tensor_copy(parts[:, 16:32], rest[:]).then_inc(chain, 1)
                    dve.wait_ge(chain, (g * 8 + q) * CHAIN + 7)
                    dve.tensor_tensor(rest[:], rest[:], parts[:, 16:32], ALU.subtract).then_inc(chain, 1)
                    dve.wait_ge(chain, (g * 8 + q) * CHAIN + 8)
                    dve.tensor_copy(parts[:, 32:48], rest[:]).then_inc(parts_ready, 1)

                def scale(g, unit):
                    dve.wait_ge(spread, g * 32 + (unit + 1))
                    x = xh[:, unit // 4 % 2, 4 * (unit % 4):4 * (unit % 4) + 4, :].rearrange("p r j -> p (r j)")
                    dve.tensor_tensor(xc[:, unit % 2, :], x, rstd_ps[:], ALU.mult).then_inc(scaled, 1)

                def gate_h(g, unit):
                    if unit == 0:
                        dve.wait_ge(h_turned, g * 32 + 32)
                    dve.wait_ge(sig, g * 32 + (unit + 2))
                    dve.wait_ge(p_done, g * 32 + (unit + 1))
                    dve.scalar_tensor_tensor(h[:, 4 * unit:4 * unit + 4, :].rearrange("p r j -> p (r j)"), p_ps[:, unit % 2, :],
                                             K.pi_bias[:], gate[:, unit % 2, :], ALU.add, ALU.mult).then_inc(h_ready, 1)

                def keep(g, rb, cb, n):
                    i0 = 8 * (n % 16)
                    dst = (out1 if n < 16 else out2)[:, :, i0:i0 + 8].rearrange("p c i -> p i c")
                    if n % 16 == 0:
                        dve.wait_ge(stored[n // 16], g * 16 + 16)
                    m = (mask_t[:, bass.ds(cb, 1), bass.ds(rb * P + i0, 8)] if n < 16 else
                         mask_n[:, bass.ds(rb, 1), bass.ds(cb * P + i0, 8)])
                    dve.wait_ge(h_turned, g * 32 + (n + 33))
                    dve.tensor_tensor(dst, t_ps[:, n % 2, :].rearrange("p (i c) -> p i c", c=64),
                                      m.rearrange("p a i -> p i a").to_broadcast([P, 8, 64]), ALU.mult).then_inc(h_kept, 1)

                for unit in range(4):
                    statistics(0, unit)
                variance(0, 0)
                split(0, 0)
                scale(0, 0)
                with dve.Fori(0, RB) as rb:
                    with dve.Fori(0, RB) as cb:
                        g = rb * RB + cb
                        for q in range(GROUPS):
                            for n in range(4):
                                unit = 4 * q + n
                                if n == 3:
                                    split(g, q + 1)
                                scale(g, unit + 1)
                                gate_h(g, unit)
                                if n < 2:
                                    statistics(g, 4 * (q + 1) + 2 * n)
                                    statistics(g, 4 * (q + 1) + 2 * n + 1)
                                if n == 1:
                                    variance(g, q + 1)
                                if unit % 2 == 0 and unit >= 2:
                                    keep(g, rb, cb, unit // 2 - 1)
                        for n in range(15, 32):
                            keep(g, rb, cb, n)

            @block.tensor
            def _(pe):
                pe.sem_inc(h_turned, 32)
                pe.wait_ge(mask_loaded, 16)
                for cb in range(RB):
                    if cb >= 2:
                        pe.wait_ge(mask_kept, cb - 1)
                    for rb in range(RB):
                        last = pe.transpose(t_ps[:, cb % 2, rb * P:(rb + 1) * P], mask_n[:, rb, cb * P:(cb + 1) * P], K.ident[:])
                    last.then_inc(mask_turned, 1)
                pe.wait_ge(mask_kept, RB)

                def wait_apart(semaphore, value):
                    pe.wait_ge(semaphore, value)
                    pe.sem_inc(met, 1)

                def turn_tokens(g, unit):
                    if unit % 4 == 0:
                        pe.wait_ge(normed, g * 8 + (unit // 4 + 3))
                    pe.wait_ge(counted, g * 32 + (unit + 1))
                    for r in range(4):
                        last = pe.transpose(x_ps[:, unit % 2, r * P:(r + 1) * P], xh[:, unit // 4 % 2, 4 * (unit % 4) + r, :], K.ident[:])
                    last.then_inc(x_turned, 1)

                def turn_parts(g, q):
                    wait_apart(parts_ready, g * 8 + (q + 1))
                    pe.transpose(parts_ps, parts[:], K.ident_bf[:]).then_inc(parts_turned, 1)

                def spread_scale(g, unit):
                    if unit % 4 == 0:
                        pe.wait_ge(rows_ready, g * 8 + (unit // 4 + 1))
                    pe.wait_ge(scaled, g * 32 + (unit + 8))
                    for r in range(4):
                        t = 4 * (unit % 4) + r
                        last = pe.matmul(rstd_ps[:, r * P:(r + 1) * P], K.select16[:, t, :], rows[:, unit // 4 % 2, :], start=True, stop=True)
                    last.then_inc(spread, 1)

                def project(g, unit):
                    pe.wait_ge(scaled, g * 32 + (unit + 9))
                    pe.wait_ge(sig, g * 32 + (unit + 1))
                    pe.matmul(g_ps[:], K.Wgi[:], xc[:, unit % 2, :], start=True, stop=True).then_inc(g_done, 1)
                    if unit % 4 == 3:
                        spread_scale(g, unit + 1)
                    pe.wait_ge(h_ready, g * 32 + (unit + 2))
                    pe.matmul(p_ps[:, unit % 2, :], K.Wpi[:], xc[:, unit % 2, :], start=True, stop=True).then_inc(p_done, 1)

                def turn_rows(g, unit):
                    n = unit // 2
                    for r in range(4 * unit, 4 * unit + 4):
                        last = pe.transpose(t_ps[:, n % 2, 64 * (r % 8):64 * (r % 8) + 64], h[0:64, r, :], K.ident[0:64, 0:64])
                    if unit % 2 == 1:
                        last.then_inc(h_turned, 1)

                def turn_columns(g, n):
                    wait_apart(h_kept, g * 32 + (n + 17))
                    for j in range(8 * n, 8 * n + 8):
                        last = pe.transpose(t_ps[:, n % 2, 64 * (j % 8):64 * (j % 8) + 64], h[64:128, :, j], K.ident[64:128, 64:128])
                    last.then_inc(h_turned, 1)

                for unit in range(4):
                    turn_tokens(0, unit)
                turn_parts(0, 0)
                spread_scale(0, 0)
                with pe.Fori(0, last_region) as g:
                    for q in range(GROUPS):
                        for n in range(4):
                            unit = 4 * q + n
                            if n == 3:
                                turn_parts(g, q + 1)
                            if n < 3:
                                spread_scale(g, unit + 1)
                            if unit % 2 == 1:
                                pe.wait_ge(h_kept, g * 32 + (unit // 2 + 1))
                            project(g, unit)
                            if n < 2:
                                turn_tokens(g, 4 * (q + 1) + 2 * n)
                                turn_tokens(g, 4 * (q + 1) + 2 * n + 1)
                            if unit >= 1:
                                turn_rows(g, unit - 1)
                    wait_apart(h_ready, g * 32 + 34)
                    turn_rows(g, 31)
                    for n in range(16):
                        turn_columns(g, n)


def stage6_triangles(nc, K, h_d, y_d, r_d, N):
    RB, D, SLOTS = N // P, 64, 4
    with ExitStack() as stack:
        s = Scope(nc, stack, "s6")
        at, bt = s.sbuf("at", [P, SLOTS, RB, N]), s.sbuf("bt", [P, SLOTS, RB, N])
        y = s.sbuf("y", [P, 4, RB, N])
        square = s.sbuf("square", [P, 2, RB, N])
        total, total2 = s.sbuf("total", [P, RB, N]), s.sbuf("total2", [P, RB, N])
        parts = s.sbuf("parts", [P, RB, 3, N], BF16)
        y_ps = s.psum("y_ps", [P, 8, BANK])
        loaded, stored, left = s.sems("loaded", SLOTS), s.sem("stored"), s.sem("left")
        zeroed, product, copied, squared, summed, chain, var_ready, dev_ready, parts_ready, parts_stored = [
            s.sem(n) for n in ("zeroed", "product", "copied", "squared", "summed", "chain", "var_ready", "dev_ready", "parts_ready", "parts_stored")]
        GROUP = 4

        @block_of(nc)
        def _(block):
            @block.sync
            def _(sp):
                for t in range(2):
                    with sp.Fori(0, 32 // GROUP) as r:
                        for u in range(GROUP):
                            sp.wait_ge(product, r * (GROUP * RB) + ((32 * t + u + 1) * RB))
                            sp.dma_start(at[:, u, :, :], h_d[t, :, :, bass.ds(r * GROUP + u, 1), :].rearrange("k p a i -> p k (a i)")).then_inc(loaded[u], 16)
                            sp.dma_start(bt[:, u, :, :], h_d[t, :, :, bass.ds(r * GROUP + (32 + u), 1), :].rearrange("k p a i -> p k (a i)")).then_inc(loaded[u], 16)

            @block.tensor
            def _(pe):
                pe.sem_inc(product, SLOTS * RB)
                with pe.Fori(0, D // GROUP) as r:
                    for u in range(GROUP):
                        pe.wait_ge(loaded[u], r * 32 + 32)
                        for ib in range(RB):
                            n = u * RB + ib
                            pe.wait_ge(copied, r * (GROUP * RB) + (n + 1))
                            for kb in range(RB):
                                last = pe.matmul(y_ps[:, n % 8, 0:N], at[:, u, kb, ib * P:(ib + 1) * P], bt[:, u, kb, :],
                                                 start=kb == 0, stop=kb == RB - 1)
                            last.then_inc(product, 1)

            @block.scalar
            def _(act):
                act.sem_inc(copied, 8)
                with act.Fori(0, D // GROUP) as r:
                    for u in range(GROUP):
                        act.wait_ge(left, r * GROUP + (u + 1))
                        act.wait_ge(summed, r * (2 * GROUP) + (2 * u + 2))
                        for ib in range(RB):
                            n = u * RB + ib
                            act.wait_ge(product, r * (GROUP * RB) + (n + 1 + SLOTS * RB))
                            act.activation(y[:, u, ib, :], y_ps[:, n % 8, 0:N], ACT.Copy).then_inc(copied, 1)
                        act.wait_ge(copied, r * (GROUP * RB) + ((u + 1) * RB + 8))
                        act.wait_ge(summed, r * (2 * GROUP) + (2 * u + 6))
                        act.activation(square[:, u % 2, :, :], y[:, u, :, :], ACT.Square).then_inc(squared, 1)
                act.wait_ge(var_ready, 1)
                act.activation(total2[:], total[:], ACT.Sqrt).then_inc(dev_ready, 1)

            @block.gpsimd
            def _(pool):
                pool.sem_inc(left, 4)
                with pool.Fori(0, D // GROUP) as r:
                    for u in range(GROUP):
                        pool.wait_ge(copied, r * (GROUP * RB) + ((u + 1) * RB + 8))
                        pool.dma_start(y_d[bass.ds(r * GROUP + u, 1)].rearrange("a (b p) j -> p (a b) j", p=P),
                                       y[:, u, :, :]).then_inc(stored, 16)
                        pool.wait_ge(stored, r * (GROUP * 16) + (u + 1) * 16)
                        pool.sem_inc(left, 1)
                pool.wait_ge(parts_ready, 1)
                pool.dma_start(r_d.rearrange("(b p) k j -> p b k j", p=P), parts[:]).then_inc(parts_stored, 16)
                pool.wait_ge(parts_stored, 16)

            @block.vector
            def _(dve):
                dve.memset(total[:], 0.0).then_inc(zeroed, 1)
                dve.memset(total2[:], 0.0).then_inc(zeroed, 1)
                dve.wait_ge(zeroed, 2)
                dve.sem_inc(summed, 8)
                with dve.Fori(0, D // GROUP) as r:
                    for u in range(GROUP):
                        dve.wait_ge(summed, r * (2 * GROUP) + (2 * u + 8))
                        dve.wait_ge(squared, r * GROUP + (u + 1))
                        dve.tensor_tensor(total[:], total[:], y[:, u, :, :], ALU.add).then_inc(summed, 1)
                        dve.tensor_tensor(total2[:], total2[:], square[:, u % 2, :, :], ALU.add).then_inc(summed, 1)
                dve.wait_ge(summed, 2 * D + 8)
                n = 0

                def step(ins):
                    nonlocal n
                    ins.then_inc(chain, 1)
                    n += 1
                    dve.wait_ge(chain, n)

                step(dve.tensor_scalar(total[:], total[:], 1.0 / D, None, ALU.mult))
                step(dve.tensor_tensor(total[:], total[:], total[:], ALU.mult))
                step(dve.scalar_tensor_tensor(total[:], total2[:], 1.0 / D, total[:], ALU.mult, ALU.subtract))
                dve.tensor_scalar(total[:], total[:], LN_EPS, None, ALU.add).then_inc(var_ready, 1)
                dve.wait_ge(dev_ready, 1)
                step(dve.reciprocal(total[:], total2[:]))
                for part in range(3):
                    step(dve.tensor_copy(parts[:, :, part, :], total[:]))
                    if part < 2:
                        step(dve.tensor_tensor(total[:], total[:], parts[:, :, part, :], ALU.subtract))
                dve.nop().then_inc(parts_ready, 1)


def stage7_layer1(nc, K, y_d, r_d, x1_d, out, N):
    CB, PAIRS = N // P, 4
    y_v = y_d.rearrange("d (r e) j -> e d r j", e=2)
    r_v = r_d.rearrange("(r e) k j -> (e k) r j", e=2)
    out_v = out.rearrange("(i q p) c -> p i q c", q=CB, p=P)
    with ExitStack() as stack:
        s = Scope(nc, stack, "s7")
        yt = s.sbuf("yt", [P, 2, 2, N])
        rt = s.sbuf("rt", [6, 2, PAIRS // 2, N], BF16)
        x1t = s.sbuf("x1t", [P, 4, 2, N])
        yn = s.sbuf("yn", [P, 2, N])
        gate = s.sbuf("gate", [P, 2, N])
        gated = s.sbuf("gated", [P, 2, N])
        oT = s.sbuf("oT", [P, 4, N])
        ot = s.sbuf("ot", [P, 4, 2, CB, P])
        r_ps = s.psum("r_ps", [P, BANK])
        p_ps = s.psum("p_ps", [P, 2, BANK])
        g_ps = s.psum("g_ps", [P, 2, BANK])
        o_ps = s.psum("o_ps", [P, 2, BANK])
        y_loaded, x_loaded, stored = s.sems("y_loaded", 2), s.sems("x_loaded", 4), s.sems("stored", 4)
        spread, scaled, p_done, g_done, sig, mixed, added, turned, kept = [
            s.sem(n) for n in ("spread", "scaled", "p_done", "g_done", "sig", "mixed", "added", "turned", "kept")]
        ROWS = 2 * PAIRS

        @block_of(nc)
        def _(block):
            @block.sync
            def _(sp):
                with sp.Fori(0, N // ROWS) as r:
                    for n in range(PAIRS):
                        if n % 2 == 0:
                            sp.wait_ge(scaled, r * PAIRS + (n + 2))
                            for e in range(2):
                                sp.dma_start(yt[64 * e:64 * e + 64, n // 2, :, :],
                                             y_v[e, :, bass.ds(r * PAIRS + n, 2), :]).then_inc(y_loaded[n // 2], 16)
                            sp.dma_start(rt[:, n // 2, :, :], r_v[:, bass.ds(r * PAIRS + n, 2), :]).then_inc(y_loaded[n // 2], 16)
                        sp.wait_ge(added, r * ROWS + (2 * n + 2))
                        sp.dma_start(x1t[:, n, :, :], x1_d[:, bass.ds(r * ROWS + 2 * n, 2), :]).then_inc(x_loaded[n], 16)

            @block.tensor
            def _(pe):
                pe.sem_inc(turned, 4)

                def spread_scale(r, n):
                    if n % 2 == 0:
                        pe.wait_ge(y_loaded[n // 2], r * 48 + 48)
                    pe.wait_ge(scaled, r * PAIRS + (n + 4))
                    pe.matmul(r_ps[:, 0:N], K.halves[:], rt[:, n // 2, n % 2, :], start=True, stop=True).then_inc(spread, 1)

                def project(r, row):
                    n, e = row // 2, row % 2
                    if e == 0:
                        pe.wait_ge(scaled, r * PAIRS + (n + 5))
                    pe.wait_ge(mixed, r * ROWS + (row + 1))
                    pe.matmul(g_ps[:, e, 0:N], K.Wgo[:, e, :], yn[:, n % 2, :], start=True, stop=True).then_inc(g_done, 1)
                    pe.matmul(p_ps[:, e, 0:N], K.Wpo[:, e, :], yn[:, n % 2, :], start=True, stop=True).then_inc(p_done, 1)

                def turn(r, row):
                    pe.wait_ge(kept, r * ROWS + (row + 1))
                    pe.wait_ge(added, r * ROWS + (row + 9))
                    for q in range(CB):
                        last = pe.transpose(o_ps[:, row % 2, q * P:(q + 1) * P], oT[:, row % 4, q * P:(q + 1) * P], K.ident[:])
                    last.then_inc(turned, 1)

                with pe.Fori(0, N // ROWS) as r:
                    spread_scale(r, 0)
                    for row in range(ROWS + 2):
                        if row % 2 == 0 and row // 2 + 1 < PAIRS:
                            spread_scale(r, row // 2 + 1)
                        if row < ROWS:
                            project(r, row)
                        if row >= 2:
                            turn(r, row - 2)

            @block.vector
            def _(dve):
                dve.sem_inc(scaled, 4)
                dve.sem_inc(mixed, 2)

                def scale(r, n):
                    dve.wait_ge(spread, r * PAIRS + (n + 1))
                    dve.tensor_tensor(yn[:, n % 2, :], yt[:, n // 2, n % 2, :], r_ps[:, 0:N], ALU.mult).then_inc(scaled, 1)

                with dve.Fori(0, N // ROWS) as r:
                    scale(r, 0)
                    for row in range(ROWS):
                        if row % 2 == 0 and row // 2 + 1 < PAIRS:
                            scale(r, row // 2 + 1)
                        dve.wait_ge(sig, r * ROWS + (row + 1))
                        dve.wait_ge(p_done, r * ROWS + (row + 1))
                        dve.wait_ge(added, r * ROWS + (row + 7))
                        dve.scalar_tensor_tensor(gated[:, row % 2, :], p_ps[:, row % 2, 0:N], K.po_bias[:], gate[:, row % 2, :],
                                                 ALU.add, ALU.mult).then_inc(mixed, 1)

            @block.scalar
            def _(act):
                act.sem_inc(kept, 2)

                def keep(r, row):
                    act.wait_ge(turned, r * ROWS + (row + 5))
                    if row % 2 == 0:
                        act.wait_ge(stored[row // 2], r * 16 + 16)
                    act.activation(ot[:, row // 2, row % 2, :, :], o_ps[:, row % 2, 0:N].rearrange("p (q c) -> p q c", c=P),
                                   ACT.Copy).then_inc(kept, 1)
                    if row % 2 == 1:
                        act.wait_ge(kept, r * ROWS + (row + 3))
                        act.dma_start(out_v[:, bass.ds(r * ROWS + row - 1, 2)], ot[:, row // 2, :, :, :]).then_inc(stored[row // 2], 16)

                for n in range(4):
                    act.sem_inc(stored[n], 16)
                with act.Fori(0, N // ROWS) as r:
                    for row in range(ROWS + 2):
                        if row < ROWS:
                            act.wait_ge(g_done, r * ROWS + (row + 1))
                            act.wait_ge(mixed, r * ROWS + (row + 1))
                            act.activation(gate[:, row % 2, :], g_ps[:, row % 2, 0:N], ACT.Sigmoid, bias=K.go_bias[:]).then_inc(sig, 1)
                        if row >= 2:
                            keep(r, row - 2)
                for n in range(4):
                    act.wait_ge(stored[n], N // ROWS * 16 + 16)

            @block.gpsimd
            def _(pool):
                pool.sem_inc(added, 8)
                with pool.Fori(0, N // ROWS) as r:
                    for row in range(ROWS):
                        if row % 2 == 0:
                            pool.wait_ge(x_loaded[row // 2], r * 16 + 16)
                        pool.wait_ge(mixed, r * ROWS + (row + 3))
                        pool.wait_ge(turned, r * ROWS + (row + 1))
                        pool.tensor_tensor(oT[:, row % 4, :], gated[:, row % 2, :], x1t[:, row // 2, row % 2, :], ALU.add).then_inc(added, 1)


class Constants:
    pass


def pair_layers(nc, x, W, out):
    N = x.shape[0]
    x_flat = x.rearrange("i j c -> (i j) c")
    out_flat = out.rearrange("i j c -> (i j) c")
    RB = N // P
    a_d = nc.dram_tensor("a_d", [RB, P, 16, N], FP32, kind="Internal").ap()
    b_d = nc.dram_tensor("b_d", [RB, P, 16, N], FP32, kind="Internal").ap()
    z_d = nc.dram_tensor("z_d", [16, N, N], FP32, kind="Internal").ap()
    x1_d = nc.dram_tensor("x1_d", [P, N, N], FP32, kind="Internal").ap()
    h_d = nc.dram_tensor("h_d", [2, RB, P, 64, N], FP32, kind="Internal").ap()
    y_d = nc.dram_tensor("y_d", [64, N, N], FP32, kind="Internal").ap()
    r_d = nc.dram_tensor("r_d", [N, 3, N], BF16, kind="Internal").ap()
    with ExitStack() as stack:
        s = Scope(nc, stack, "k")
        K = Constants()
        K.ident, K.ident_bf = s.sbuf("ident", [P, P]), s.sbuf("ident_bf", [P, P], BF16)
        K.group_mean = s.sbuf("group_mean", [P, P])
        K.select16, K.halves = s.sbuf("select16", [48, 16, P], BF16), s.sbuf("halves", [6, P], BF16)
        K.mean_col, K.mean_square = s.sbuf("mean_col", [P, 1]), s.sbuf("mean_square", [P, 1])
        K.minus_half = s.sbuf("minus_half", [P, 16])
        K.Wa, K.Wb = s.sbuf("Wa", [P, 32]), s.sbuf("Wb", [P, 32])
        K.bias_a, K.bias_b = s.sbuf("bias_a", [P, 32]), s.sbuf("bias_b", [P, 32])
        K.Wg, K.bg = s.sbuf("Wg", [P, P]), s.sbuf("bg", [P, 1])
        K.Wz_raw, K.Wz, K.z_bias = s.sbuf("Wz_raw", [16, P]), s.sbuf("Wz", [16, P]), s.sbuf("z_bias", [P, 1])
        K.Wpi, K.Wgi, K.pi_bias, K.gi_bias = s.sbuf("Wpi", [P, P]), s.sbuf("Wgi", [P, P]), s.sbuf("pi_bias", [P, 1]), s.sbuf("gi_bias", [P, 1])
        K.Wpo, K.Wgo, K.po_bias, K.go_bias = s.sbuf("Wpo", [P, 2, P]), s.sbuf("Wgo", [P, 2, P]), s.sbuf("po_bias", [P, 1]), s.sbuf("go_bias", [P, 1])
        K.gn_mean, K.gn_scale, K.gn_shift = s.sbuf("gn_mean", [P, 1]), s.sbuf("gn_scale", [P, 1]), s.sbuf("gn_shift", [P, 1])
        prepare(nc, K, W)
        stage1_statistics(nc, K, x_flat, N)
        stage2_gates(nc, K, x_flat, a_d, b_d, N)
        stage3_triangle(nc, K, a_d, b_d, z_d, N)
        stage4_layer0(nc, K, x_flat, z_d, x1_d, N)
        stage5_project(nc, K, x1_d, W["mask"], h_d, N)
        stage6_triangles(nc, K, h_d, y_d, r_d, N)
        stage7_layer1(nc, K, y_d, r_d, x1_d, out_flat, N)


_WEIGHTS = {
    "Wa1": "L0_conv_Wa1", "ba1": "L0_conv_ba1", "Wa2": "L0_conv_Wa2", "ba2": "L0_conv_ba2",
    "Wb1": "L0_conv_Wb1", "bb1": "L0_conv_bb1", "Wb2": "L0_conv_Wb2", "bb2": "L0_conv_bb2",
    "ln2_g0": "L0_conv_ln2_g", "ln2_b0": "L0_conv_ln2_b", "Wg": "L0_conv_Wg", "bg": "L0_conv_bg",
    "Wz": "L0_conv_Wz", "bz": "L0_conv_bz", "mask": "L1_conv_mask", "ln1_w": "L1_conv_ln1_w",
    "ln1_b": "L1_conv_ln1_b", "pi_w": "L1_conv_pi_w", "pi_b": "L1_conv_pi_b", "gi_w": "L1_conv_gi_w",
    "gi_b": "L1_conv_gi_b", "ln2_w": "L1_conv_ln2_w", "ln2_b": "L1_conv_ln2_b", "po_w": "L1_conv_po_w",
    "po_b": "L1_conv_po_b", "go_w": "L1_conv_go_w", "go_b": "L1_conv_go_b",
}


def kernel(**inputs):
    import numpy as np
    import concourse.bacc as bacc
    from concourse.bass_utils import run_bass_kernel_spmd

    nc = bacc.Bacc("TRN2", target_bir_lowering=False, num_devices=1)
    arrays, weights = {}, {}

    def give(name, array):
        array = np.ascontiguousarray(array)
        arrays[f"in_{name}"] = array
        return nc.dram_tensor(f"in_{name}", array.shape, FP32, kind="ExternalInput").ap()

    x = give("x", inputs["x"][0])
    for short, name in _WEIGHTS.items():
        weights[short] = give(short, inputs[name][0] if short == "mask" else inputs[name])
    out = nc.dram_tensor("out", arrays["in_x"].shape, FP32, kind="ExternalOutput").ap()
    pair_layers(nc, x, weights, out)
    result = run_bass_kernel_spmd(nc, [arrays], core_ids=[0]).results[0]["out"]
    return result[None]
```

```python
import concourse.bass as bass
from concourse import mybir
from contextlib import ExitStack

FP32 = mybir.dt.float32
BF16 = mybir.dt.bfloat16
FP16 = mybir.dt.float16
ALU = mybir.AluOpType
ACT = mybir.ActivationFunctionType
AX = mybir.AxisListType

P = 128
BANK = 512
GN_EPS = 1e-5
LN_EPS = 1e-5


class Scope:

    def __init__(self, nc, stack, tag):
        self.nc, self.stack, self.tag = nc, stack, tag

    def sbuf(self, name, shape, dtype=FP32):
        return self.stack.enter_context(self.nc.sbuf_tensor(f"{self.tag}_{name}", shape, dtype))

    def psum(self, name, shape, dtype=FP32):
        return self.stack.enter_context(self.nc.psum_tensor(f"{self.tag}_{name}", shape, dtype))

    def sem(self, name):
        return self.stack.enter_context(self.nc.semaphore(f"{self.tag}_{name}"))

    def sems(self, name, n):
        return [self.sem(f"{name}{i}") for i in range(n)]


def column(vector):
    return vector.rearrange("(p a) -> p a", a=1)


def prepare(nc, K, W):
    with ExitStack() as stack:
        s = Scope(nc, stack, "w")
        pi, gi = s.sbuf("pi", [P, P]), s.sbuf("gi", [P, P])
        po, go = s.sbuf("po", [P, 64]), s.sbuf("go", [P, 64])
        cols = s.sbuf("cols", [P, 12])
        transposed = s.sbuf("transposed", [P, 4, P])
        Wab = s.sbuf("Wab", [P, 64])
        center = s.sbuf("center", [P, P])
        center64 = s.sbuf("center64", [64, P])
        ps_t = s.psum("ps_t", [P, 4, P])
        ps_b = s.psum("ps_b", [P, BANK])
        ps_c = s.psum("ps_c", [P, 4, P])
        loaded, built, turned, kept = s.sem("loaded"), s.sem("built"), s.sem("turned"), s.sem("kept")
        biased, centred, done = s.sem("biased"), s.sem("centred"), s.sem("done")
        rounded = s.sem("rounded")
        loads = [
            (Wab[:, 0:16], W["Wa1"]), (Wab[:, 16:32], W["Wb1"]), (Wab[:, 32:48], W["Wa2"]), (Wab[:, 48:64], W["Wb2"]),
            (K.bias_ab[:, 0:16], W["ba1"].partition_broadcast(P)), (K.bias_ab[:, 16:32], W["bb1"].partition_broadcast(P)),
            (K.bias_ab[:, 32:48], W["ba2"].partition_broadcast(P)), (K.bias_ab[:, 48:64], W["bb2"].partition_broadcast(P)),
            (K.Wg[:], W["Wg"]), (K.bg[:], column(W["bg"])), (K.Wz_raw[:], W["Wz"]),
            (pi[:], W["pi_w"]), (gi[:], W["gi_w"]), (po[:], W["po_w"]), (go[:], W["go_w"]),
            (cols[:, 0:1], column(W["bz"])), (cols[:, 1:2], column(W["pi_b"])), (cols[:, 2:3], column(W["gi_b"])),
            (cols[:, 3:4], column(W["po_b"])), (cols[:, 4:5], column(W["go_b"])),
            (cols[:, 5:6], column(W["ln1_w"])), (cols[:, 6:7], column(W["ln1_b"])),
            (cols[0:64, 7:8], column(W["ln2_w"])), (cols[64:128, 7:8], column(W["ln2_w"])),
            (cols[0:64, 8:9], column(W["ln2_b"])),
            (cols[0:16, 9:10], column(W["ln2_g0"])), (cols[0:16, 10:11], column(W["ln2_b0"])),
        ]
        with nc.Block() as block:
            @block.sync
            def _(sp):
                for dst, src in loads:
                    sp.dma_start(dst, src).then_inc(loaded, 16)
                sp.wait_ge(loaded, 16 * len(loads))

            @block.gpsimd
            def _(pool):
                n = 0

                def step(ins):
                    nonlocal n
                    ins.then_inc(built, 1)
                    n += 1
                    pool.wait_ge(built, n)

                def diagonal(tile, pattern, base=0):
                    step(pool.affine_select(out=tile, in_=tile, compare_op=ALU.not_equal, fill=1.0, base=base,
                                            pattern=pattern, channel_multiplier=1))

                step(pool.memset(K.ident[:], 0.0))
                diagonal(K.ident[:], [[-1, P]])
                step(pool.memset(K.ident_bf[:], 0.0))
                diagonal(K.ident_bf[:], [[-1, P]])
                step(pool.memset(K.group_mean[:], 0.25))
                view = K.group_mean[:].rearrange("p (g c) -> p g c", c=4)
                step(pool.affine_select(out=view, in_=view, compare_op=ALU.is_ge, fill=0.0, base=0,
                                        pattern=[[-4, 32], [0, 4]], channel_multiplier=1))
                step(pool.affine_select(out=view, in_=view, compare_op=ALU.is_ge, fill=0.0, base=3,
                                        pattern=[[4, 32], [0, 4]], channel_multiplier=-1))
                step(pool.memset(K.select16[:], 0.0))
                for part in range(3):
                    diagonal(K.select16[:], [[-1, 16], [0, P]], base=-16 * part)
                step(pool.memset(K.halves[:], 1.0))
                step(pool.affine_select(out=K.halves[:, 0:64], in_=K.halves[:, 0:64], compare_op=ALU.is_ge, fill=0.0,
                                        base=2, pattern=[[0, 64]], channel_multiplier=-1))
                step(pool.affine_select(out=K.halves[:, 64:128], in_=K.halves[:, 64:128], compare_op=ALU.is_ge,
                                        fill=0.0, base=-3, pattern=[[0, 64]], channel_multiplier=1))
                step(pool.memset(K.mean_col[:], 1.0 / P))
                step(pool.memset(K.mean_square[:], 1.0 / P))
                pool.memset(K.minus_half[:], -0.5).then_inc(built, 1)

            BUILT = 17

            @block.tensor
            def _(pe):
                pe.wait_ge(built, BUILT)
                pe.wait_ge(loaded, 16 * len(loads))
                pe.transpose(ps_t[:, 0, :], pi[:], K.ident[:]).then_inc(turned, 1)
                pe.transpose(ps_t[:, 1, :], gi[:], K.ident[:]).then_inc(turned, 1)
                pe.transpose(ps_t[0:64, 2, :], po[:], K.ident[:]).then_inc(turned, 1)
                pe.transpose(ps_t[0:64, 3, :], go[:], K.ident[:]).then_inc(turned, 1)
                pe.wait_ge(kept, 1)
                for n, (w, rows, b) in enumerate([(transposed[:, 0, :], P, 6), (transposed[:, 1, :], P, 6),
                                                  (transposed[0:64, 2, :], 64, 8), (transposed[0:64, 3, :], 64, 8),
                                                  (K.Wz_raw[:], 16, 10)]):
                    pe.matmul(ps_b[:, n:n + 1], w, cols[0:rows, b:b + 1], start=True, stop=True).then_inc(biased, 1)
                pe.wait_ge(kept, 2)
                pe.matmul(ps_c[:, 0, :], center[:], transposed[:, 0, :], start=True, stop=True).then_inc(centred, 1)
                pe.matmul(ps_c[:, 1, :], center[:], transposed[:, 1, :], start=True, stop=True).then_inc(centred, 1)
                pe.matmul(ps_c[:, 2, :], center64[:], transposed[0:64, 2, :], start=True, stop=True).then_inc(centred, 1)
                pe.matmul(ps_c[:, 3, :], center64[:], transposed[0:64, 3, :], start=True, stop=True).then_inc(centred, 1)

            @block.vector
            def _(dve):
                dve.wait_ge(loaded, 16 * len(loads))
                dve.tensor_copy(K.Wab_high[:], Wab[:]).then_inc(rounded, 1)
                dve.wait_ge(rounded, 1)
                dve.tensor_tensor(K.Wab_low[:], Wab[:], K.Wab_high[:], ALU.subtract)
                dve.wait_ge(turned, 4)
                for n in range(4):
                    rows = P if n < 2 else 64
                    last = dve.tensor_copy(transposed[0:rows, n, :], ps_t[0:rows, n, :])
                last.then_inc(kept, 1)
                dve.wait_ge(built, BUILT)
                dve.tensor_scalar(center[:], K.ident[:], -1.0 / P, None, ALU.add)
                dve.tensor_scalar(center64[:, 0:64], K.ident[0:64, 0:64], -1.0 / 64, None, ALU.add)
                dve.tensor_scalar(center64[:, 64:128], K.ident[0:64, 0:64], -1.0 / 64, None, ALU.add)
                dve.wait_ge(biased, 5)
                for n, col in ((0, 5), (1, 5), (2, 7), (3, 7)):
                    rows = P if n < 2 else 64
                    last = dve.tensor_scalar(transposed[0:rows, n, :], transposed[0:rows, n, :],
                                             cols[0:rows, col:col + 1], None, ALU.mult)
                last.then_inc(kept, 1)
                dve.tensor_tensor(K.pi_bias[:], ps_b[:, 0:1], cols[:, 1:2], ALU.add)
                dve.tensor_tensor(K.gi_bias[:], ps_b[:, 1:2], cols[:, 2:3], ALU.add)
                dve.tensor_tensor(K.po_bias[:], ps_b[:, 2:3], cols[:, 3:4], ALU.add)
                dve.tensor_tensor(K.go_bias[:], ps_b[:, 3:4], cols[:, 4:5], ALU.add)
                dve.tensor_tensor(K.z_bias[:], ps_b[:, 4:5], cols[:, 0:1], ALU.add)
                dve.tensor_scalar(K.Wz[:], K.Wz_raw[:], cols[0:16, 9:10], None, ALU.mult)
                dve.wait_ge(centred, 4)
                dve.tensor_copy(K.Wpi[:], ps_c[:, 0, :])
                dve.tensor_copy(K.Wgi[:], ps_c[:, 1, :])
                for n, w in ((2, K.Wpo), (3, K.Wgo)):
                    for e in range(2):
                        own, other = slice(64 * e, 64 * e + 64), slice(64 - 64 * e, 128 - 64 * e)
                        dve.memset(w[other, e, :], 0.0)
                        last = dve.tensor_copy(w[own, e, :], ps_c[own, n, :])
                last.then_inc(done, 1)


def norm_from_moments(nc, s, block, K, moments, moments_ready):
    var, deviation = s.sbuf("gn_var", [P, 1]), s.sbuf("gn_dev", [P, 1])
    chain, var_ready, dev_ready = s.sem("gn_chain"), s.sem("gn_var_ready"), s.sem("gn_dev_ready")

    def vector_part(dve):
        dve.wait_ge(moments_ready, 2)
        dve.tensor_copy(K.gn_mean[:], moments[:, 0:1]).then_inc(chain, 1)
        dve.wait_ge(chain, 1)
        dve.tensor_tensor(var[:], K.gn_mean[:], K.gn_mean[:], ALU.mult).then_inc(chain, 1)
        dve.wait_ge(chain, 2)
        dve.tensor_tensor(var[:], moments[:, 1:2], var[:], ALU.subtract).then_inc(chain, 1)
        dve.wait_ge(chain, 3)
        dve.tensor_scalar(var[:], var[:], GN_EPS, None, ALU.add).then_inc(var_ready, 1)
        dve.wait_ge(dev_ready, 1)
        dve.reciprocal(K.gn_scale[:], deviation[:]).then_inc(chain, 1)
        dve.wait_ge(chain, 4)
        dve.scalar_tensor_tensor(K.gn_shift[:], K.gn_mean[:], -1.0, K.gn_scale[:], ALU.mult, ALU.mult).then_inc(chain, 1)
        dve.wait_ge(chain, 5)

    def scalar_part(act):
        act.wait_ge(var_ready, 1)
        act.activation(deviation[:], var[:], ACT.Sqrt).then_inc(dev_ready, 1)

    return vector_part, scalar_part


def stage1_statistics(nc, K, x, N):
    T = 128
    chunks = N * N // P // T
    x_v = x.rearrange("(p n t) c -> n p t c", p=P, t=T)
    with ExitStack() as stack:
        s = Scope(nc, stack, "s1")
        xt = s.sbuf("xt", [P, 2, T, P])
        stats = s.sbuf("stats", [P, 32, chunks, 6])
        mv = s.sbuf("mv", [P, 32, 2])
        square = s.sbuf("square", [P, 32])
        wide = s.sbuf("wide", [P, 2, 32, 4])
        moments = s.psum("moments", [P, 2])
        loaded = s.sems("loaded", 2)
        used, aggregated, wide_ready, moments_ready = s.sem("used"), s.sem("aggregated"), s.sem("wide_ready"), s.sem("moments_ready")
        with nc.Block() as block:
            norm_vector, norm_scalar = norm_from_moments(nc, s, block, K, moments, moments_ready)

            @block.sync
            def _(sp):
                with sp.Fori(0, chunks // 2) as r:
                    for u in range(2):
                        sp.wait_ge(used, r * 2 + (u + 1))
                        sp.dma_start(xt[:, u, :, :], x_v[bass.ds(r * 2 + u, 1)].rearrange("a p t c -> p (a t) c")).then_inc(loaded[u], 16)

            @block.vector
            def _(dve):
                dve.sem_inc(used, 2)
                with dve.Fori(0, chunks // 2) as r:
                    for u in range(2):
                        dve.wait_ge(loaded[u], r * 16 + 16)
                        for g in range(32):
                            last = dve.bn_stats(stats[:, g, bass.ds(r * 2 + u, 1), :].rearrange("p a s -> p (a s)"),
                                                xt[:, u, :, 4 * g:4 * g + 4])
                        last.then_inc(used, 1)
                dve.wait_ge(used, chunks + 2)
                for g in range(32):
                    dve.bn_aggr(mv[:, g, :], stats[:, g, :, :].rearrange("p n s -> p (n s)")).then_inc(aggregated, 1)
                dve.wait_ge(aggregated, 32)
                dve.tensor_tensor(square[:], mv[:, :, 0], mv[:, :, 0], ALU.mult).then_inc(aggregated, 1)
                dve.tensor_copy(wide[:, 0, :, :], mv[:, :, 0:1].to_broadcast([P, 32, 4]))
                dve.wait_ge(aggregated, 33)
                dve.tensor_tensor(square[:], square[:], mv[:, :, 1], ALU.add).then_inc(aggregated, 1)
                dve.wait_ge(aggregated, 34)
                dve.tensor_copy(wide[:, 1, :, :], square[:].rearrange("p (g a) -> p g a", a=1).to_broadcast([P, 32, 4])).then_inc(wide_ready, 1)
                norm_vector(dve)

            @block.tensor
            def _(pe):
                pe.wait_ge(wide_ready, 1)
                for m in range(2):
                    pe.matmul(moments[:, m:m + 1], wide[:, m, :, :].rearrange("p g c -> p (g c)"), K.mean_col[:],
                              start=True, stop=True).then_inc(moments_ready, 1)

            @block.scalar
            def _(act):
                norm_scalar(act)


def block_of(nc):
    def run(build):
        with nc.Block() as block:
            build(block)
    return run


def stage2_gates(nc, K, x, a_d, b_d, N):
    RB = N // P
    ROWS, UNITS = 8, 64
    PAIRS = UNITS // 2
    LAG = 4
    x_v = x.rearrange("(rb n r j) c -> rb n j r c", rb=RB, r=ROWS, j=N)
    with ExitStack() as stack:
        s = Scope(nc, stack, "s2")
        xt = s.sbuf("xt", [P, 4, ROWS, P])
        xh = s.sbuf("xh", [P, 4, BANK])
        high, low = s.sbuf("high", [P, 8, BANK], FP16), s.sbuf("low", [P, 8, BANK], FP16)
        pre = s.sbuf("pre", [P, 2, 8, 64])
        gate = s.sbuf("gate", [P, 2, 8, 32])
        ab = s.sbuf("ab", [P, 2, 32, P])
        b_out = s.sbuf("b_out", [P, 16, P])
        turned_ps = s.psum("turned_ps", [P, 4, BANK])
        proj_ps = s.psum("proj_ps", [P, 2, BANK])
        b_ps = s.psum("b_ps", [P, 2, BANK])
        loaded = s.sems("loaded", 4)
        turned, normed, multiplied = s.sem("turned"), s.sem("normed"), s.sem("multiplied")
        rounded, rest_ready = s.sems("rounded", 2), s.sems("rest_ready", 2)
        biased, gated, sig = s.sem("biased"), s.sem("gated"), s.sem("sig")
        b_turned, b_kept = s.sem("b_turned"), s.sem("b_kept")
        a_stored, b_stored = s.sems("a_stored", 2), s.sem("b_stored")

        @block_of(nc)
        def _(block):
            @block.sync
            def _(sp):
                with sp.Fori(0, RB) as rb:
                    with sp.Fori(0, RB // 2) as c2:
                        r = rb * (RB // 2) + c2
                        for n in range(32):
                            sp.wait_ge(turned, r * UNITS + (2 * n + 2))
                            src = x_v[bass.ds(rb, 1), n % 16, bass.ds((c2 * 2 + n // 16) * P, P)].rearrange("a j r c -> (a j) r c")
                            sp.dma_start(xt[:, n % 4, :, :], src).then_inc(loaded[n % 4], 16)

            @block.tensor
            def _(pe):
                pe.sem_inc(turned, 8)
                pe.sem_inc(multiplied, 8)

                def turn(r, u):
                    if u % 2 == 0:
                        pe.wait_ge(loaded[u // 2 % 4], r * 128 + 16 * (u // 8 + 1))
                    pe.wait_ge(normed, r * UNITS + (u + 1))
                    for k in range(4):
                        last = pe.transpose(turned_ps[:, u % 4, k * P:(k + 1) * P],
                                            xt[:, u // 2 % 4, 4 * (u % 2) + k, :], K.ident[:])
                    last.then_inc(turned, 1)

                def multiply(r, u):
                    pe.wait_ge(rest_ready[u % 2], r * PAIRS + (u // 2 + 3))
                    if u % 2 == 0:
                        pe.wait_ge(biased, r * PAIRS + (u // 2 + 1))
                    for k in range(4):
                        dst = proj_ps[:, u // 2 % 2, 64 * (4 * (u % 2) + k):64 * (4 * (u % 2) + k) + 64]
                        row = slice(k * P, (k + 1) * P)
                        pe.matmul(dst, high[:, u % 8, row], K.Wab_high[:], start=True, stop=False)
                        pe.matmul(dst, high[:, u % 8, row], K.Wab_low[:], start=False, stop=False)
                        last = pe.matmul(dst, low[:, u % 8, row], K.Wab_high[:], start=False, stop=True)
                    last.then_inc(multiplied, 1)

                def turn_b(r, half, n):
                    pe.wait_ge(sig, r * PAIRS + (16 * (half + 1) + 2))
                    pe.wait_ge(b_kept, r * 8 + (4 * half + n + 1))
                    for c in range(4):
                        last = pe.transpose(b_ps[:, n % 2, c * P:(c + 1) * P], ab[:, half, 16 + 4 * n + c, :], K.ident[:])
                    last.then_inc(b_turned, 1)

                with pe.Fori(0, RB * RB // 2) as r:
                    for v in range(UNITS + LAG):
                        if v < UNITS:
                            turn(r, v)
                        if v >= LAG:
                            multiply(r, v - LAG)
                        if 42 <= v < 46:
                            turn_b(r, 0, v - 42)
                    for n in range(4):
                        turn_b(r, 1, n)

            def round_high(engine, copy, r, u):
                engine.wait_ge(normed, r * UNITS + (u + 5))
                engine.wait_ge(multiplied, r * UNITS + (u + 1))
                copy(high[:, u % 8, :], xh[:, u % 4, :]).then_inc(rounded[u % 2], 1)

            def rest(engine, r, u):
                engine.wait_ge(rounded[u % 2], r * PAIRS + (u // 2 + 1))
                engine.tensor_tensor(low[:, u % 8, :], xh[:, u % 4, :], high[:, u % 8, :], ALU.subtract).then_inc(rest_ready[u % 2], 1)

            @block.scalar
            def _(act):
                act.sem_inc(normed, 4)
                act.sem_inc(sig, 2)
                act.sem_inc(b_kept, 2)
                act.sem_inc(b_turned, 8)
                for stored in a_stored + [b_stored]:
                    act.sem_inc(stored, 16)

                def copy(dst, src):
                    return act.activation(dst, src, ACT.Identity)

                def norm(r, u):
                    act.wait_ge(turned, r * UNITS + (u + 9))
                    act.wait_ge(rest_ready[u % 2], r * PAIRS + (u // 2 + 1))
                    act.activation(xh[:, u % 4, :], turned_ps[:, u % 4, :], ACT.Identity, bias=K.gn_shift[:],
                                   scale=K.gn_scale[:]).then_inc(normed, 1)

                def finish_sigmoid(r, q):
                    half, i0 = q // 16, 8 * (q % 16)
                    act.wait_ge(gated, r * PAIRS + (q + 1))
                    if q % 16 == 0:
                        act.wait_ge(a_stored[half], r * 16 + 16)
                        act.wait_ge(b_turned, r * 8 + (4 * half + 1))
                    act.activation(ab[:, half, :, i0:i0 + 8], gate[:, q % 2, :, :].rearrange("p r c -> p c r"),
                                   ACT.Sigmoid).then_inc(sig, 1)

                def keep_b(r, half, n):
                    if n == 0:
                        act.wait_ge(b_stored, r * 32 + 16 * (half + 1))
                    act.wait_ge(b_turned, r * 8 + (4 * half + n + 9))
                    act.activation(b_out[:, 4 * n:4 * n + 4, :], b_ps[:, n % 2, :].rearrange("p (c j) -> p c j", j=P),
                                   ACT.Identity).then_inc(b_kept, 1)

                def store_a(rb, c2, r, half):
                    act.wait_ge(sig, r * PAIRS + (16 * (half + 1) + 2))
                    act.dma_start(a_d[bass.ds(c2 * 2 + half, 1), :, :, bass.ds(rb * P, P)].rearrange("a p c i -> (a p) c i"),
                                  ab[:, half, 0:16, :]).then_inc(a_stored[half], 16)

                def store_b(rb, c2, r, half):
                    act.wait_ge(b_kept, r * 8 + (4 * (half + 1) + 2))
                    act.dma_start(b_d[bass.ds(rb, 1), :, :, bass.ds((c2 * 2 + half) * P, P)].rearrange("a p c i -> (a p) c i"),
                                  b_out[:]).then_inc(b_stored, 16)

                with act.Fori(0, RB) as rb:
                    with act.Fori(0, RB // 2) as c2:
                        r = rb * (RB // 2) + c2
                        for u in range(UNITS):
                            norm(r, u)
                            if u % 2 == 1:
                                round_high(act, copy, r, u - 1)
                            if u % 2 == 1 and u >= LAG + 3:
                                finish_sigmoid(r, (u - LAG - 3) // 2)
                            if u == 39:
                                store_a(rb, c2, r, 0)
                            if 44 <= u < 48:
                                keep_b(r, 0, u - 44)
                            if u == 49:
                                store_b(rb, c2, r, 0)
                        for q in range(PAIRS - LAG // 2 - 1, PAIRS):
                            finish_sigmoid(r, q)
                        store_a(rb, c2, r, 1)
                        for n in range(4):
                            keep_b(r, 1, n)
                        store_b(rb, c2, r, 1)
                for half in range(2):
                    act.wait_ge(a_stored[half], RB * RB * 8 + 16)
                act.wait_ge(b_stored, RB * RB * 16 + 16)

            @block.gpsimd
            def _(pool):
                with pool.Fori(0, RB * RB // 2) as r:
                    for u in range(1, UNITS, 2):
                        rest(pool, r, u)

            @block.vector
            def _(dve):
                for sem in rest_ready:
                    dve.sem_inc(sem, 2)
                dve.sem_inc(biased, 2)

                def multiply_halves(r, q):
                    dve.wait_ge(multiplied, r * UNITS + (2 * q + 10))
                    dve.wait_ge(sig, r * PAIRS + (q + 1))
                    dve.tensor_tensor(pre[:, q % 2, :, :], proj_ps[:, q % 2, :].rearrange("p (r c) -> p r c", c=64),
                                      K.bias_ab[:].rearrange("p (a c) -> p a c", a=1).to_broadcast([P, 8, 64]),
                                      ALU.add).then_inc(biased, 1)
                    dve.wait_ge(biased, r * PAIRS + (q + 3))
                    dve.tensor_tensor(gate[:, q % 2, :, :], pre[:, q % 2, :, 0:32], pre[:, q % 2, :, 32:64],
                                      ALU.mult).then_inc(gated, 1)

                with dve.Fori(0, RB * RB // 2) as r:
                    for u in range(UNITS):
                        if u % 2 == 1:
                            round_high(dve, dve.tensor_copy, r, u)
                            rest(dve, r, u - 1)
                        if u % 2 == 1 and u >= LAG + 1:
                            multiply_halves(r, (u - LAG - 1) // 2)
                    for q in range(PAIRS - LAG // 2, PAIRS):
                        multiply_halves(r, q)


def stage3_triangle(nc, K, a_d, b_d, z_d, N):
    RB, C, SLOTS = N // P, 16, 4
    with ExitStack() as stack:
        s = Scope(nc, stack, "s3")
        at = s.sbuf("at", [P, SLOTS, RB, P])
        bt = s.sbuf("bt", [P, SLOTS, RB, N])
        z = s.sbuf("z", [P, C, N])
        centred = s.sbuf("centred", [P, C, N])
        squares = s.sbuf("squares", [P, C, N])
        mean, var, dev = s.sbuf("mean", [P, N]), s.sbuf("var", [P, N]), s.sbuf("dev", [P, N])
        z_ps = s.psum("z_ps", [P, 8, BANK])
        loaded = s.sems("loaded", SLOTS)
        product, copied, chain, cent, sq, var_ready, dev_ready, z_ready, stored, left = [
            s.sem(n) for n in ("product", "copied", "chain", "cent", "sq", "var_ready", "dev_ready", "z_ready", "stored", "left")]
        CHAIN = 4

        @block_of(nc)
        def _(block):
            @block.sync
            def _(sp):
                with sp.Fori(0, RB) as ib:
                    for c in range(C):
                        sp.wait_ge(product, ib * C + (c + 1))
                        sp.dma_start(at[:, c % SLOTS, :, :], a_d[:, :, c, bass.ds(ib * P, P)].rearrange("k p i -> p k i")).then_inc(loaded[c % SLOTS], 16)
                        sp.dma_start(bt[:, c % SLOTS, :, :], b_d[:, :, c, :].rearrange("k p j -> p k j")).then_inc(loaded[c % SLOTS], 16)

            @block.tensor
            def _(pe):
                pe.sem_inc(product, SLOTS)
                with pe.Fori(0, RB) as ib:
                    for c in range(C):
                        pe.wait_ge(loaded[c % SLOTS], ib * (32 * C // SLOTS) + 32 * (c // SLOTS + 1))
                        pe.wait_ge(copied, ib * C + (c + 1))
                        for kb in range(RB):
                            last = pe.matmul(z_ps[:, c % 8, 0:N], at[:, c % SLOTS, kb, :], bt[:, c % SLOTS, kb, :],
                                             start=kb == 0, stop=kb == RB - 1)
                        last.then_inc(product, 1)

            @block.scalar
            def _(act):
                act.sem_inc(copied, 8)
                with act.Fori(0, RB) as ib:
                    act.wait_ge(cent, ib + 1)
                    for c in range(C):
                        act.wait_ge(product, ib * C + (c + 1 + SLOTS))
                        act.activation(z[:, c, :], z_ps[:, c % 8, 0:N], ACT.Copy).then_inc(copied, 1)
                    act.wait_ge(cent, ib + 2)
                    act.activation(squares[:], centred[:], ACT.Square).then_inc(sq, 1)
                    act.wait_ge(var_ready, ib + 1)
                    act.activation(dev[:], var[:], ACT.Sqrt).then_inc(dev_ready, 1)

            @block.vector
            def _(dve):
                dve.sem_inc(cent, 1)

                def over_channels(tile):
                    return tile[:].rearrange("p c j -> p j c")

                def every_channel(tile):
                    return tile[:].rearrange("p (a j) -> p a j", a=1).to_broadcast([P, C, N])

                with dve.Fori(0, RB) as ib:
                    dve.wait_ge(copied, ib * C + (C + 8))
                    dve.tensor_reduce(mean[:], over_channels(z), AX.X, ALU.add).then_inc(chain, 1)
                    dve.wait_ge(chain, ib * CHAIN + 1)
                    dve.tensor_scalar(mean[:], mean[:], 1.0 / C, None, ALU.mult).then_inc(chain, 1)
                    dve.wait_ge(chain, ib * CHAIN + 2)
                    dve.wait_ge(left, ib + 1)
                    dve.tensor_tensor(centred[:], z[:], every_channel(mean), ALU.subtract).then_inc(cent, 1)
                    dve.wait_ge(sq, ib + 1)
                    dve.tensor_reduce(var[:], over_channels(squares), AX.X, ALU.add).then_inc(chain, 1)
                    dve.wait_ge(chain, ib * CHAIN + 3)
                    dve.tensor_scalar(var[:], var[:], 1.0 / C, LN_EPS, ALU.mult, ALU.add).then_inc(var_ready, 1)
                    dve.wait_ge(dev_ready, ib + 1)
                    dve.reciprocal(dev[:], dev[:]).then_inc(chain, 1)
                    dve.wait_ge(chain, ib * CHAIN + 4)
                    dve.tensor_tensor(centred[:], centred[:], every_channel(dev), ALU.mult).then_inc(z_ready, 1)

            @block.gpsimd
            def _(pool):
                pool.sem_inc(left, 1)
                with pool.Fori(0, RB) as ib:
                    pool.wait_ge(z_ready, ib + 1)
                    pool.dma_start(z_d[:, bass.ds(ib * P, P), :].rearrange("c i j -> i c j"), centred[:]).then_inc(stored, 16)
                    pool.wait_ge(stored, ib * 16 + 16)
                    pool.sem_inc(left, 1)


def stage4_layer0(nc, K, x, z_d, x1_d, N):
    CB, U = N // P, 4
    x_v = x.rearrange("(i q p) c -> p i q c", q=CB, p=P)
    with ExitStack() as stack:
        s = Scope(nc, stack, "s4")
        xt = s.sbuf("xt", [P, 4, 2, CB, P])
        zt = s.sbuf("zt", [16, 2, U, N])
        xT = s.sbuf("xT", [P, U, N])
        g = s.sbuf("g", [P, 2, N])
        gz = s.sbuf("gz", [P, 2, N])
        x1T = s.sbuf("x1T", [P, 4, 2, N])
        stats = s.sbuf("stats", [P, N, 6])
        mv = s.sbuf("mv", [P, 2])
        pair = s.sbuf("pair", [P, 2])
        Wg = s.sbuf("Wg", [P, P])
        bg = s.sbuf("bg", [P, 1])
        x_ps = s.psum("x_ps", [P, 4, BANK])
        g_ps = s.psum("g_ps", [P, 2, BANK])
        z_ps = s.psum("z_ps", [P, 2, BANK])
        loaded, z_loaded, stored = s.sems("loaded", 4), s.sems("z_loaded", 2), s.sems("stored", 4)
        turned, kept, g_prod, z_prod, sig, mixed, added, counted = [
            s.sem(n) for n in ("turned", "kept", "g_prod", "z_prod", "sig", "mixed", "added", "counted")]
        folded, shifted, moments_ready, chain = s.sem("folded"), s.sem("shifted"), s.sem("moments_ready"), s.sem("chain")

        @block_of(nc)
        def _(block):
            moments = g_ps[:, 0, 0:2]
            norm_vector, norm_scalar = norm_from_moments(nc, s, block, K, moments, moments_ready)

            @block.sync
            def _(sp):
                def load(r, n):
                    sp.wait_ge(turned, r * 8 + (2 * n + 2))
                    sp.dma_start(xt[:, n, :, :, :], x_v[:, bass.ds(r * 8 + 2 * n, 2)]).then_inc(loaded[n], 16)
                    if n % 2 == 0:
                        sp.wait_ge(z_prod, r * 8 + (2 * n + 4))
                        sp.dma_start(zt[:, n // 2, :, :], z_d[:, bass.ds(r * 8 + 2 * n, U), :]).then_inc(z_loaded[n // 2], 16)

                def store(r, n):
                    sp.wait_ge(added, r * 8 + (2 * n + 6))
                    sp.dma_start(x1_d[:, bass.ds(r * 8 + 2 * n, 2), :], x1T[:, n, :, :]).then_inc(stored[n], 16)

                for n in range(4):
                    sp.sem_inc(stored[n], 16)
                    load(0, n)
                with sp.Fori(0, N // 8 - 1) as r:
                    for n in range(4):
                        store(r, n)
                        load(r + 1, n)
                for n in range(4):
                    store(N // 8 - 1, n)
                for n in range(4):
                    sp.wait_ge(stored[n], 2 * N + 16)

            @block.tensor
            def _(pe):
                pe.sem_inc(turned, 8)
                pe.sem_inc(z_prod, 8)
                pe.matmul(g_ps[:, 0, 0:1], K.Wg[:], K.gn_shift[:], start=True, stop=True).then_inc(shifted, 1)
                pe.wait_ge(folded, 2)
                with pe.Fori(0, N // 8) as r:
                    for h in range(2):
                        for u in range(U):
                            i = 4 * h + u
                            if u % 2 == 0:
                                pe.wait_ge(loaded[i // 2], r * 16 + 16)
                            pe.wait_ge(kept, r * 8 + (i + 1))
                            for q in range(CB):
                                last = pe.transpose(x_ps[:, u, q * P:(q + 1) * P], xt[:, i // 2, i % 2, q, :], K.ident[:])
                            last.then_inc(turned, 1)
                        pe.wait_ge(z_loaded[h], r * 16 + 16)
                        for u in range(U):
                            i = 4 * h + u
                            pe.wait_ge(mixed, r * 8 + (i + 1))
                            pe.matmul(z_ps[:, u % 2, 0:N], K.Wz[:], zt[:, h, u, :], start=True, stop=True).then_inc(z_prod, 1)
                            pe.wait_ge(kept, r * 8 + (i + 5))
                            pe.matmul(g_ps[:, u % 2, 0:N], Wg[:], xT[:, u, :], start=True, stop=True).then_inc(g_prod, 1)
                pe.wait_ge(chain, 3)
                for m in range(2):
                    pe.matmul(moments[:, m:m + 1], K.group_mean[:], pair[:, m:m + 1], start=True, stop=True).then_inc(moments_ready, 1)

            @block.scalar
            def _(act):
                act.sem_inc(kept, 4)
                with act.Fori(0, N // 8) as r:
                    for h in range(2):
                        for step in range(U + 1):
                            if step < U:
                                i = 4 * h + step
                                act.wait_ge(turned, r * 8 + (i + 9))
                                act.wait_ge(added, r * 8 + (i + 1))
                                act.activation(xT[:, step, :], x_ps[:, step, 0:N], ACT.Copy).then_inc(kept, 1)
                            if step >= 1:
                                i = 4 * h + step - 1
                                act.wait_ge(g_prod, r * 8 + (i + 1))
                                act.activation(g[:, i % 2, :], g_ps[:, i % 2, 0:N], ACT.Sigmoid, bias=bg[:]).then_inc(sig, 1)
                norm_scalar(act)

            @block.vector
            def _(dve):
                dve.sem_inc(mixed, 2)
                dve.tensor_scalar(Wg[:], K.Wg[:], K.gn_scale[:], None, ALU.mult).then_inc(folded, 1)
                dve.wait_ge(shifted, 1)
                dve.tensor_tensor(bg[:], g_ps[:, 0, 0:1], K.bg[:], ALU.add).then_inc(folded, 1)

                def statistics(r, i):
                    dve.wait_ge(added, r * 8 + (i + 5))
                    dve.bn_stats(stats[:, bass.ds(r * 8 + i, 1), :].rearrange("p a s -> p (a s)"),
                                 x1T[:, i // 2, i % 2, :]).then_inc(counted, 1)

                dve.sem_inc(counted, 8)
                with dve.Fori(0, N // 8) as r:
                    for i in range(8):
                        dve.wait_ge(sig, r * 8 + (i + 1))
                        dve.wait_ge(z_prod, r * 8 + (i + 9))
                        dve.wait_ge(added, r * 8 + (i + 3))
                        dve.scalar_tensor_tensor(gz[:, i % 2, :], z_ps[:, i % 2, 0:N], K.z_bias[:], g[:, i % 2, :],
                                                 ALU.add, ALU.mult).then_inc(mixed, 1)
                        if i >= 1:
                            statistics(r, i - 1)
                    statistics(r, 7)
                dve.wait_ge(counted, N + 8)
                dve.bn_aggr(mv[:], stats[:].rearrange("p n s -> p (n s)")).then_inc(chain, 1)
                dve.wait_ge(chain, 1)
                dve.tensor_copy(pair[:, 0:1], mv[:, 0:1])
                dve.tensor_tensor(pair[:, 1:2], mv[:, 0:1], mv[:, 0:1], ALU.mult).then_inc(chain, 1)
                dve.wait_ge(chain, 2)
                dve.tensor_tensor(pair[:, 1:2], pair[:, 1:2], mv[:, 1:2], ALU.add).then_inc(chain, 1)
                norm_vector(dve)

            @block.gpsimd
            def _(pool):
                pool.sem_inc(added, 4)
                with pool.Fori(0, N // 8) as r:
                    for i in range(8):
                        if i % 2 == 0:
                            pool.wait_ge(stored[i // 2], r * 16 + 16)
                        pool.wait_ge(counted, r * 8 + (i + 1))
                        pool.wait_ge(mixed, r * 8 + (i + 3))
                        pool.tensor_tensor(x1T[:, i // 2, i % 2, :], gz[:, i % 2, :], xT[:, i % 4, :], ALU.add).then_inc(added, 1)


def stage5_project(nc, K, x1_d, mask, h_d, N):
    RB, GROUPS = N // P, 8
    last_region = RB * RB
    with ExitStack() as stack:
        s = Scope(nc, stack, "s5")
        xg = s.sbuf("xg", [P, 16, P])
        xh = s.sbuf("xh", [P, 4, 16, P])
        xc = s.sbuf("xc", [P, 2, BANK])
        gate = s.sbuf("gate", [P, 2, BANK])
        h = s.sbuf("h", [P, P, P])
        out1 = s.sbuf("out1", [P, 64, P])
        out2 = s.sbuf("out2", [P, 64, P])
        mask_n = s.sbuf("mask_n", [P, RB, N])
        mask_t = s.sbuf("mask_t", [P, RB, N])
        stats = s.sbuf("stats", [P, 16, 6])
        spread_m, within, var, rstd, rest = [s.sbuf(n, [P, 16]) for n in ("spread_m", "within", "var", "rstd", "rest")]
        parts = s.sbuf("parts", [P, 48], BF16)
        rows = s.sbuf("rows", [48, 2, P], BF16)
        x_ps = s.psum("x_ps", [P, 2, BANK])
        rstd_ps = s.psum("rstd_ps", [P, BANK])
        p_ps = s.psum("p_ps", [P, 2, BANK])
        g_ps = s.psum("g_ps", [P, BANK])
        t_ps = s.psum("t_ps", [P, 2, BANK])
        parts_ps = x_ps[0:48, 0, 0:64].bitcast(BF16)
        loaded = s.sem("loaded")
        mask_loaded, mask_turned, mask_kept = [s.sem(n) for n in ("mask_loaded", "mask_turned", "mask_kept")]
        normed, x_turned, counted, var_ready, rstd_ready, parts_ready, parts_turned, rows_ready, chain = [
            s.sem(n) for n in ("normed", "x_turned", "counted", "var_ready", "rstd_ready", "parts_ready", "parts_turned", "rows_ready", "chain")]
        spread, scaled, p_done, g_done, sig, h_ready, h_turned, h_kept = [
            s.sem(n) for n in ("spread", "scaled", "p_done", "g_done", "sig", "h_ready", "h_turned", "h_kept")]
        stored, met = s.sems("stored", 2), s.sem("met")
        CHAIN = 8

        @block_of(nc)
        def _(block):
            @block.sync
            def _(sp):
                sp.dma_start(mask_n[:], mask.rearrange("(b p) j -> p b j", p=P)).then_inc(mask_loaded, 16)

                def load(g, q):
                    place = g % last_region
                    sp.wait_ge(normed, (g * 8 + q) * 4 + 1)
                    src = x1_d[:, bass.ds(place // RB * P + 16 * q, 16), bass.ds(place % RB * P, P)]
                    sp.dma_start(xg[:], src).then_inc(loaded, 16)

                for m in range(2):
                    sp.sem_inc(stored[m], 16)
                for q in range(3):
                    load(0, q)
                with sp.Fori(0, last_region) as g:
                    for q in range(3, 8):
                        load(g, q)
                    for q in range(3):
                        load(g + 1, q)
                    sp.wait_ge(h_kept, g * 32 + 18)
                    sp.dma_start(h_d[0, bass.ds(g % RB, 1), :, :, bass.ds(g // RB * P, P)].rearrange("a p c i -> (a p) c i"),
                                 out1[:]).then_inc(stored[0], 16)
                    sp.wait_ge(h_kept, g * 32 + 34)
                    sp.dma_start(h_d[1, bass.ds(g // RB, 1), :, :, bass.ds(g % RB * P, P)].rearrange("a p c i -> (a p) c i"),
                                 out2[:]).then_inc(stored[1], 16)
                for m in range(2):
                    sp.wait_ge(stored[m], 16 * last_region + 16)
                sp.wait_ge(loaded, last_region * 128 + 48)

            @block.scalar
            def _(act):
                act.sem_inc(normed, 1)

                def norm(G, n):
                    if n % 4 == 0:
                        act.wait_ge(loaded, G * 16 + 16)
                        act.wait_ge(scaled, G * 4 + 4)
                    slot = n // 4 % 4
                    act.activation(xh[:, slot, 4 * (n % 4):4 * (n % 4) + 4, :], xg[:, 4 * (n % 4):4 * (n % 4) + 4, :],
                                   ACT.Identity, bias=K.gn_shift[:], scale=K.gn_scale[:]).then_inc(normed, 1)

                def keep_rows(G, q):
                    act.wait_ge(parts_turned, G + 1)
                    act.activation(rows[:, q % 2, :], parts_ps, ACT.Copy).then_inc(rows_ready, 1)

                act.sem_inc(sig, 1)
                for n in range(12):
                    norm(n // 4, n)
                keep_rows(0, 0)
                with act.Fori(0, last_region) as g:
                    for q in range(GROUPS):
                        for n in range(4):
                            unit = 4 * q + n
                            if n == 2:
                                keep_rows(g * 8 + (q + 1), q + 1)
                            act.wait_ge(g_done, g * 32 + (unit + 1))
                            act.wait_ge(h_ready, g * 32 + (unit + 1))
                            act.activation(gate[:, unit % 2, :], g_ps[:], ACT.Sigmoid, bias=K.gi_bias[:]).then_inc(sig, 1)
                            norm(g * 8 + (q + 3), unit + 12)

            @block.gpsimd
            def _(pool):
                def power(G):
                    pool.wait_ge(var_ready, G + 1)
                    pool.tensor_tensor(rstd[:], var[:], K.minus_half[:], ALU.pow).then_inc(rstd_ready, 1)

                power(0)
                power(1)
                with pool.Fori(0, last_region) as g:
                    for q in range(GROUPS):
                        power(g * 8 + (q + 2))

            @block.vector
            def _(dve):
                dve.sem_inc(scaled, 16)
                dve.sem_inc(counted, 2)
                dve.sem_inc(h_ready, 2)
                dve.sem_inc(h_kept, 2)
                for b in range(RB):
                    dve.wait_ge(mask_turned, b + 1)
                    dve.tensor_copy(mask_t[:, b, :], t_ps[:, b % 2, 0:N]).then_inc(mask_kept, 1)

                def statistics(g, unit):
                    dve.wait_ge(x_turned, g * 32 + (unit + 1))
                    for r in range(4):
                        last = dve.bn_stats(stats[:, 4 * (unit % 4) + r, :], x_ps[:, unit % 2, r * P:(r + 1) * P])
                    last.then_inc(counted, 1)

                def variance(g, q):
                    base = (g * 8 + q) * CHAIN
                    dve.wait_ge(counted, g * 32 + (4 * q + 6))
                    dve.tensor_tensor(spread_m[:], stats[:, :, 1], stats[:, :, 4], ALU.subtract).then_inc(chain, 1)
                    dve.tensor_tensor(within[:], stats[:, :, 2], stats[:, :, 5], ALU.add).then_inc(chain, 1)
                    dve.wait_ge(chain, base + 2)
                    dve.scalar_tensor_tensor(spread_m[:], spread_m[:], 0.25, spread_m[:], ALU.mult, ALU.mult).then_inc(chain, 1)
                    dve.wait_ge(chain, base + 3)
                    dve.scalar_tensor_tensor(var[:], within[:], 1.0 / P, spread_m[:], ALU.mult, ALU.add).then_inc(chain, 1)
                    dve.wait_ge(chain, base + 4)
                    dve.tensor_scalar(var[:], var[:], LN_EPS, None, ALU.add).then_inc(var_ready, 1)

                def split(g, q):
                    dve.wait_ge(rstd_ready, g * 8 + (q + 1))
                    dve.tensor_copy(parts[:, 0:16], rstd[:]).then_inc(chain, 1)
                    dve.wait_ge(chain, (g * 8 + q) * CHAIN + 5)
                    dve.tensor_tensor(rest[:], rstd[:], parts[:, 0:16], ALU.subtract).then_inc(chain, 1)
                    dve.wait_ge(chain, (g * 8 + q) * CHAIN + 6)
                    dve.tensor_copy(parts[:, 16:32], rest[:]).then_inc(chain, 1)
                    dve.wait_ge(chain, (g * 8 + q) * CHAIN + 7)
                    dve.tensor_tensor(rest[:], rest[:], parts[:, 16:32], ALU.subtract).then_inc(chain, 1)
                    dve.wait_ge(chain, (g * 8 + q) * CHAIN + 8)
                    dve.tensor_copy(parts[:, 32:48], rest[:]).then_inc(parts_ready, 1)

                def scale(g, unit):
                    dve.wait_ge(spread, g * 32 + (unit + 1))
                    x = xh[:, unit // 4 % 4, 4 * (unit % 4):4 * (unit % 4) + 4, :].rearrange("p r j -> p (r j)")
                    dve.tensor_tensor(xc[:, unit % 2, :], x, rstd_ps[:], ALU.mult).then_inc(scaled, 1)

                def gate_h(g, unit):
                    if unit == 0:
                        dve.wait_ge(h_turned, g * 32 + 32)
                    dve.wait_ge(sig, g * 32 + (unit + 2))
                    dve.wait_ge(p_done, g * 32 + (unit + 1))
                    dve.scalar_tensor_tensor(h[:, 4 * unit:4 * unit + 4, :].rearrange("p r j -> p (r j)"), p_ps[:, unit % 2, :],
                                             K.pi_bias[:], gate[:, unit % 2, :], ALU.add, ALU.mult).then_inc(h_ready, 1)

                def keep(g, rb, cb, n):
                    i0 = 8 * (n % 16)
                    dst = (out1 if n < 16 else out2)[:, :, i0:i0 + 8].rearrange("p c i -> p i c")
                    if n % 16 == 0:
                        dve.wait_ge(stored[n // 16], g * 16 + 16)
                    m = (mask_t[:, bass.ds(cb, 1), bass.ds(rb * P + i0, 8)] if n < 16 else
                         mask_n[:, bass.ds(rb, 1), bass.ds(cb * P + i0, 8)])
                    dve.wait_ge(h_turned, g * 32 + (n + 33))
                    dve.tensor_tensor(dst, t_ps[:, n % 2, :].rearrange("p (i c) -> p i c", c=64),
                                      m.rearrange("p a i -> p i a").to_broadcast([P, 8, 64]), ALU.mult).then_inc(h_kept, 1)

                for unit in range(4):
                    statistics(0, unit)
                variance(0, 0)
                split(0, 0)
                for unit in range(4, 8):
                    statistics(0, unit)
                variance(0, 1)
                scale(0, 0)
                with dve.Fori(0, RB) as rb:
                    with dve.Fori(0, RB) as cb:
                        g = rb * RB + cb
                        for q in range(GROUPS):
                            for n in range(4):
                                unit = 4 * q + n
                                if n == 1:
                                    split(g, q + 1)
                                scale(g, unit + 1)
                                gate_h(g, unit)
                                statistics(g, unit + 8)
                                if n == 3:
                                    variance(g, q + 2)
                                if unit % 2 == 0 and unit >= 2:
                                    keep(g, rb, cb, unit // 2 - 1)
                        for n in range(15, 32):
                            keep(g, rb, cb, n)

            @block.tensor
            def _(pe):
                pe.sem_inc(h_turned, 32)
                pe.wait_ge(mask_loaded, 16)
                for cb in range(RB):
                    if cb >= 2:
                        pe.wait_ge(mask_kept, cb - 1)
                    for rb in range(RB):
                        last = pe.transpose(t_ps[:, cb % 2, rb * P:(rb + 1) * P], mask_n[:, rb, cb * P:(cb + 1) * P], K.ident[:])
                    last.then_inc(mask_turned, 1)
                pe.wait_ge(mask_kept, RB)

                def wait_apart(semaphore, value):
                    pe.wait_ge(semaphore, value)
                    pe.sem_inc(met, 1)

                def turn_tokens(g, unit, parts_before=0):
                    pe.wait_ge(normed, g * 32 + (unit + 2))
                    pe.wait_ge(counted, g * 32 + (unit + 1))
                    if parts_before:
                        pe.wait_ge(rows_ready, g * 8 + parts_before)
                    for r in range(4):
                        last = pe.transpose(x_ps[:, unit % 2, r * P:(r + 1) * P], xh[:, unit // 4 % 4, 4 * (unit % 4) + r, :], K.ident[:])
                    last.then_inc(x_turned, 1)

                def turn_parts(g, q, unit):
                    wait_apart(counted, g * 32 + (unit + 3))
                    wait_apart(parts_ready, g * 8 + (q + 1))
                    pe.transpose(parts_ps, parts[:], K.ident_bf[:]).then_inc(parts_turned, 1)

                def spread_scale(g, unit):
                    if unit % 4 == 0:
                        pe.wait_ge(rows_ready, g * 8 + (unit // 4 + 1))
                    pe.wait_ge(scaled, g * 32 + (unit + 16))
                    for r in range(4):
                        t = 4 * (unit % 4) + r
                        last = pe.matmul(rstd_ps[:, r * P:(r + 1) * P], K.select16[:, t, :], rows[:, unit // 4 % 2, :], start=True, stop=True)
                    last.then_inc(spread, 1)

                def project(g, unit):
                    pe.wait_ge(scaled, g * 32 + (unit + 17))
                    pe.wait_ge(sig, g * 32 + (unit + 1))
                    pe.matmul(g_ps[:], K.Wgi[:], xc[:, unit % 2, :], start=True, stop=True).then_inc(g_done, 1)
                    if unit % 4 == 3:
                        spread_scale(g, unit + 1)
                    pe.wait_ge(h_ready, g * 32 + (unit + 2))
                    pe.matmul(p_ps[:, unit % 2, :], K.Wpi[:], xc[:, unit % 2, :], start=True, stop=True).then_inc(p_done, 1)

                def turn_rows(g, unit):
                    n = unit // 2
                    for r in range(4 * unit, 4 * unit + 4):
                        last = pe.transpose(t_ps[:, n % 2, 64 * (r % 8):64 * (r % 8) + 64], h[0:64, r, :], K.ident[0:64, 0:64])
                    if unit % 2 == 1:
                        last.then_inc(h_turned, 1)

                def turn_columns(g, n):
                    wait_apart(h_kept, g * 32 + (n + 17))
                    for j in range(8 * n, 8 * n + 8):
                        last = pe.transpose(t_ps[:, n % 2, 64 * (j % 8):64 * (j % 8) + 64], h[64:128, :, j], K.ident[64:128, 64:128])
                    last.then_inc(h_turned, 1)

                for unit in range(8):
                    turn_tokens(0, unit)
                turn_parts(0, 0, 6)
                spread_scale(0, 0)
                with pe.Fori(0, last_region) as g:
                    for q in range(GROUPS):
                        for n in range(4):
                            unit = 4 * q + n
                            if n < 3:
                                spread_scale(g, unit + 1)
                            if unit % 2 == 1:
                                pe.wait_ge(h_kept, g * 32 + (unit // 2 + 1))
                            project(g, unit)
                            turn_tokens(g, unit + 8, q + 2 if n == 2 else 0)
                            if n == 1:
                                turn_parts(g, q + 1, unit + 7)
                            if unit >= 1:
                                turn_rows(g, unit - 1)
                    wait_apart(h_ready, g * 32 + 34)
                    turn_rows(g, 31)
                    for n in range(16):
                        turn_columns(g, n)


def stage6_triangles(nc, K, h_d, y_d, r_d, N):
    RB, D, SLOTS = N // P, 64, 4
    with ExitStack() as stack:
        s = Scope(nc, stack, "s6")
        at, bt = s.sbuf("at", [P, SLOTS, RB, N]), s.sbuf("bt", [P, SLOTS, RB, N])
        y = s.sbuf("y", [P, 4, RB, N])
        square = s.sbuf("square", [P, 2, RB, N])
        total, total2 = s.sbuf("total", [P, RB, N]), s.sbuf("total2", [P, RB, N])
        parts = s.sbuf("parts", [P, RB, 3, N], BF16)
        y_ps = s.psum("y_ps", [P, 8, BANK])
        loaded, stored, left = s.sems("loaded", SLOTS), s.sem("stored"), s.sem("left")
        zeroed, product, copied, squared, summed, chain, var_ready, dev_ready, parts_ready, parts_stored = [
            s.sem(n) for n in ("zeroed", "product", "copied", "squared", "summed", "chain", "var_ready", "dev_ready", "parts_ready", "parts_stored")]
        GROUP = 4

        @block_of(nc)
        def _(block):
            @block.sync
            def _(sp):
                for t in range(2):
                    with sp.Fori(0, 32 // GROUP) as r:
                        for u in range(GROUP):
                            sp.wait_ge(product, r * (GROUP * RB) + ((32 * t + u + 1) * RB))
                            sp.dma_start(at[:, u, :, :], h_d[t, :, :, bass.ds(r * GROUP + u, 1), :].rearrange("k p a i -> p k (a i)")).then_inc(loaded[u], 16)
                            sp.dma_start(bt[:, u, :, :], h_d[t, :, :, bass.ds(r * GROUP + (32 + u), 1), :].rearrange("k p a i -> p k (a i)")).then_inc(loaded[u], 16)

            @block.tensor
            def _(pe):
                pe.sem_inc(product, SLOTS * RB)
                with pe.Fori(0, D // GROUP) as r:
                    for u in range(GROUP):
                        pe.wait_ge(loaded[u], r * 32 + 32)
                        for ib in range(RB):
                            n = u * RB + ib
                            pe.wait_ge(copied, r * (GROUP * RB) + (n + 1))
                            for kb in range(RB):
                                last = pe.matmul(y_ps[:, n % 8, 0:N], at[:, u, kb, ib * P:(ib + 1) * P], bt[:, u, kb, :],
                                                 start=kb == 0, stop=kb == RB - 1)
                            last.then_inc(product, 1)

            @block.scalar
            def _(act):
                act.sem_inc(copied, 8)
                with act.Fori(0, D // GROUP) as r:
                    for u in range(GROUP):
                        act.wait_ge(left, r * GROUP + (u + 1))
                        act.wait_ge(summed, r * (2 * GROUP) + (2 * u + 2))
                        for ib in range(RB):
                            n = u * RB + ib
                            act.wait_ge(product, r * (GROUP * RB) + (n + 1 + SLOTS * RB))
                            act.activation(y[:, u, ib, :], y_ps[:, n % 8, 0:N], ACT.Copy).then_inc(copied, 1)
                        act.wait_ge(copied, r * (GROUP * RB) + ((u + 1) * RB + 8))
                        act.wait_ge(summed, r * (2 * GROUP) + (2 * u + 6))
                        act.activation(square[:, u % 2, :, :], y[:, u, :, :], ACT.Square).then_inc(squared, 1)
                act.wait_ge(var_ready, 1)
                act.activation(total2[:], total[:], ACT.Sqrt).then_inc(dev_ready, 1)

            @block.gpsimd
            def _(pool):
                pool.sem_inc(left, 4)
                with pool.Fori(0, D // GROUP) as r:
                    for u in range(GROUP):
                        pool.wait_ge(copied, r * (GROUP * RB) + ((u + 1) * RB + 8))
                        pool.dma_start(y_d[bass.ds(r * GROUP + u, 1)].rearrange("a (b p) j -> p (a b) j", p=P),
                                       y[:, u, :, :]).then_inc(stored, 16)
                        pool.wait_ge(stored, r * (GROUP * 16) + (u + 1) * 16)
                        pool.sem_inc(left, 1)
                pool.wait_ge(parts_ready, 1)
                pool.dma_start(r_d.rearrange("(b p) k j -> p b k j", p=P), parts[:]).then_inc(parts_stored, 16)
                pool.wait_ge(parts_stored, 16)

            @block.vector
            def _(dve):
                dve.memset(total[:], 0.0).then_inc(zeroed, 1)
                dve.memset(total2[:], 0.0).then_inc(zeroed, 1)
                dve.wait_ge(zeroed, 2)
                dve.sem_inc(summed, 8)
                with dve.Fori(0, D // GROUP) as r:
                    for u in range(GROUP):
                        dve.wait_ge(summed, r * (2 * GROUP) + (2 * u + 8))
                        dve.wait_ge(squared, r * GROUP + (u + 1))
                        dve.tensor_tensor(total[:], total[:], y[:, u, :, :], ALU.add).then_inc(summed, 1)
                        dve.tensor_tensor(total2[:], total2[:], square[:, u % 2, :, :], ALU.add).then_inc(summed, 1)
                dve.wait_ge(summed, 2 * D + 8)
                n = 0

                def step(ins):
                    nonlocal n
                    ins.then_inc(chain, 1)
                    n += 1
                    dve.wait_ge(chain, n)

                step(dve.tensor_scalar(total[:], total[:], 1.0 / D, None, ALU.mult))
                step(dve.tensor_tensor(total[:], total[:], total[:], ALU.mult))
                step(dve.scalar_tensor_tensor(total[:], total2[:], 1.0 / D, total[:], ALU.mult, ALU.subtract))
                dve.tensor_scalar(total[:], total[:], LN_EPS, None, ALU.add).then_inc(var_ready, 1)
                dve.wait_ge(dev_ready, 1)
                step(dve.reciprocal(total[:], total2[:]))
                for part in range(3):
                    step(dve.tensor_copy(parts[:, :, part, :], total[:]))
                    if part < 2:
                        step(dve.tensor_tensor(total[:], total[:], parts[:, :, part, :], ALU.subtract))
                dve.nop().then_inc(parts_ready, 1)


def stage7_layer1(nc, K, y_d, r_d, x1_d, out, N):
    CB, PAIRS = N // P, 4
    y_v = y_d.rearrange("d (r e) j -> e d r j", e=2)
    r_v = r_d.rearrange("(r e) k j -> (e k) r j", e=2)
    out_v = out.rearrange("(i q p) c -> p i q c", q=CB, p=P)
    with ExitStack() as stack:
        s = Scope(nc, stack, "s7")
        yt = s.sbuf("yt", [P, 2, 2, N])
        rt = s.sbuf("rt", [6, 2, PAIRS // 2, N], BF16)
        x1t = s.sbuf("x1t", [P, 4, 2, N])
        yn = s.sbuf("yn", [P, 2, N])
        gate = s.sbuf("gate", [P, 2, N])
        gated = s.sbuf("gated", [P, 2, N])
        oT = s.sbuf("oT", [P, 4, N])
        ot = s.sbuf("ot", [P, 4, 2, CB, P])
        r_ps = s.psum("r_ps", [P, BANK])
        p_ps = s.psum("p_ps", [P, 2, BANK])
        g_ps = s.psum("g_ps", [P, 2, BANK])
        o_ps = s.psum("o_ps", [P, 2, BANK])
        y_loaded, x_loaded, stored = s.sems("y_loaded", 2), s.sems("x_loaded", 4), s.sems("stored", 4)
        spread, scaled, p_done, g_done, sig, mixed, added, turned, kept = [
            s.sem(n) for n in ("spread", "scaled", "p_done", "g_done", "sig", "mixed", "added", "turned", "kept")]
        ROWS = 2 * PAIRS

        @block_of(nc)
        def _(block):
            @block.sync
            def _(sp):
                with sp.Fori(0, N // ROWS) as r:
                    for n in range(PAIRS):
                        if n % 2 == 0:
                            sp.wait_ge(scaled, r * PAIRS + (n + 2))
                            for e in range(2):
                                sp.dma_start(yt[64 * e:64 * e + 64, n // 2, :, :],
                                             y_v[e, :, bass.ds(r * PAIRS + n, 2), :]).then_inc(y_loaded[n // 2], 16)
                            sp.dma_start(rt[:, n // 2, :, :], r_v[:, bass.ds(r * PAIRS + n, 2), :]).then_inc(y_loaded[n // 2], 16)
                        sp.wait_ge(added, r * ROWS + (2 * n + 2))
                        sp.dma_start(x1t[:, n, :, :], x1_d[:, bass.ds(r * ROWS + 2 * n, 2), :]).then_inc(x_loaded[n], 16)

            @block.tensor
            def _(pe):
                pe.sem_inc(turned, 4)

                def spread_scale(r, n):
                    if n % 2 == 0:
                        pe.wait_ge(y_loaded[n // 2], r * 48 + 48)
                    pe.wait_ge(scaled, r * PAIRS + (n + 4))
                    pe.matmul(r_ps[:, 0:N], K.halves[:], rt[:, n // 2, n % 2, :], start=True, stop=True).then_inc(spread, 1)

                def project(r, row):
                    n, e = row // 2, row % 2
                    if e == 0:
                        pe.wait_ge(scaled, r * PAIRS + (n + 5))
                    pe.wait_ge(mixed, r * ROWS + (row + 1))
                    pe.matmul(g_ps[:, e, 0:N], K.Wgo[:, e, :], yn[:, n % 2, :], start=True, stop=True).then_inc(g_done, 1)
                    pe.matmul(p_ps[:, e, 0:N], K.Wpo[:, e, :], yn[:, n % 2, :], start=True, stop=True).then_inc(p_done, 1)

                def turn(r, row):
                    pe.wait_ge(kept, r * ROWS + (row + 1))
                    pe.wait_ge(added, r * ROWS + (row + 9))
                    for q in range(CB):
                        last = pe.transpose(o_ps[:, row % 2, q * P:(q + 1) * P], oT[:, row % 4, q * P:(q + 1) * P], K.ident[:])
                    last.then_inc(turned, 1)

                with pe.Fori(0, N // ROWS) as r:
                    spread_scale(r, 0)
                    for row in range(ROWS + 2):
                        if row % 2 == 0 and row // 2 + 1 < PAIRS:
                            spread_scale(r, row // 2 + 1)
                        if row < ROWS:
                            project(r, row)
                        if row >= 2:
                            turn(r, row - 2)

            @block.vector
            def _(dve):
                dve.sem_inc(scaled, 4)
                dve.sem_inc(mixed, 2)

                def scale(r, n):
                    dve.wait_ge(spread, r * PAIRS + (n + 1))
                    dve.tensor_tensor(yn[:, n % 2, :], yt[:, n // 2, n % 2, :], r_ps[:, 0:N], ALU.mult).then_inc(scaled, 1)

                with dve.Fori(0, N // ROWS) as r:
                    scale(r, 0)
                    for row in range(ROWS):
                        if row % 2 == 0 and row // 2 + 1 < PAIRS:
                            scale(r, row // 2 + 1)
                        dve.wait_ge(sig, r * ROWS + (row + 1))
                        dve.wait_ge(p_done, r * ROWS + (row + 1))
                        dve.wait_ge(added, r * ROWS + (row + 7))
                        dve.scalar_tensor_tensor(gated[:, row % 2, :], p_ps[:, row % 2, 0:N], K.po_bias[:], gate[:, row % 2, :],
                                                 ALU.add, ALU.mult).then_inc(mixed, 1)

            @block.scalar
            def _(act):
                act.sem_inc(kept, 2)

                def keep(r, row):
                    act.wait_ge(turned, r * ROWS + (row + 5))
                    if row % 2 == 0:
                        act.wait_ge(stored[row // 2], r * 16 + 16)
                    act.activation(ot[:, row // 2, row % 2, :, :], o_ps[:, row % 2, 0:N].rearrange("p (q c) -> p q c", c=P),
                                   ACT.Copy).then_inc(kept, 1)
                    if row % 2 == 1:
                        act.wait_ge(kept, r * ROWS + (row + 3))
                        act.dma_start(out_v[:, bass.ds(r * ROWS + row - 1, 2)], ot[:, row // 2, :, :, :]).then_inc(stored[row // 2], 16)

                for n in range(4):
                    act.sem_inc(stored[n], 16)
                with act.Fori(0, N // ROWS) as r:
                    for row in range(ROWS + 2):
                        if row < ROWS:
                            act.wait_ge(g_done, r * ROWS + (row + 1))
                            act.wait_ge(mixed, r * ROWS + (row + 1))
                            act.activation(gate[:, row % 2, :], g_ps[:, row % 2, 0:N], ACT.Sigmoid, bias=K.go_bias[:]).then_inc(sig, 1)
                        if row >= 2:
                            keep(r, row - 2)
                for n in range(4):
                    act.wait_ge(stored[n], N // ROWS * 16 + 16)

            @block.gpsimd
            def _(pool):
                pool.sem_inc(added, 8)
                with pool.Fori(0, N // ROWS) as r:
                    for row in range(ROWS):
                        if row % 2 == 0:
                            pool.wait_ge(x_loaded[row // 2], r * 16 + 16)
                        pool.wait_ge(mixed, r * ROWS + (row + 3))
                        pool.wait_ge(turned, r * ROWS + (row + 1))
                        pool.tensor_tensor(oT[:, row % 4, :], gated[:, row % 2, :], x1t[:, row // 2, row % 2, :], ALU.add).then_inc(added, 1)


class Constants:
    pass


def pair_layers(nc, x, W, out):
    N = x.shape[0]
    x_flat = x.rearrange("i j c -> (i j) c")
    out_flat = out.rearrange("i j c -> (i j) c")
    RB = N // P
    a_d = nc.dram_tensor("a_d", [RB, P, 16, N], FP32, kind="Internal").ap()
    b_d = nc.dram_tensor("b_d", [RB, P, 16, N], FP32, kind="Internal").ap()
    z_d = nc.dram_tensor("z_d", [16, N, N], FP32, kind="Internal").ap()
    x1_d = nc.dram_tensor("x1_d", [P, N, N], FP32, kind="Internal").ap()
    h_d = nc.dram_tensor("h_d", [2, RB, P, 64, N], FP32, kind="Internal").ap()
    y_d = nc.dram_tensor("y_d", [64, N, N], FP32, kind="Internal").ap()
    r_d = nc.dram_tensor("r_d", [N, 3, N], BF16, kind="Internal").ap()
    with ExitStack() as stack:
        s = Scope(nc, stack, "k")
        K = Constants()
        K.ident, K.ident_bf = s.sbuf("ident", [P, P]), s.sbuf("ident_bf", [P, P], BF16)
        K.group_mean = s.sbuf("group_mean", [P, P])
        K.select16, K.halves = s.sbuf("select16", [48, 16, P], BF16), s.sbuf("halves", [6, P], BF16)
        K.mean_col, K.mean_square = s.sbuf("mean_col", [P, 1]), s.sbuf("mean_square", [P, 1])
        K.minus_half = s.sbuf("minus_half", [P, 16])
        K.Wab_high, K.Wab_low = s.sbuf("Wab_high", [P, 64], FP16), s.sbuf("Wab_low", [P, 64], FP16)
        K.bias_ab = s.sbuf("bias_ab", [P, 64])
        K.Wg, K.bg = s.sbuf("Wg", [P, P]), s.sbuf("bg", [P, 1])
        K.Wz_raw, K.Wz, K.z_bias = s.sbuf("Wz_raw", [16, P]), s.sbuf("Wz", [16, P]), s.sbuf("z_bias", [P, 1])
        K.Wpi, K.Wgi, K.pi_bias, K.gi_bias = s.sbuf("Wpi", [P, P]), s.sbuf("Wgi", [P, P]), s.sbuf("pi_bias", [P, 1]), s.sbuf("gi_bias", [P, 1])
        K.Wpo, K.Wgo, K.po_bias, K.go_bias = s.sbuf("Wpo", [P, 2, P]), s.sbuf("Wgo", [P, 2, P]), s.sbuf("po_bias", [P, 1]), s.sbuf("go_bias", [P, 1])
        K.gn_mean, K.gn_scale, K.gn_shift = s.sbuf("gn_mean", [P, 1]), s.sbuf("gn_scale", [P, 1]), s.sbuf("gn_shift", [P, 1])
        prepare(nc, K, W)
        stage1_statistics(nc, K, x_flat, N)
        stage2_gates(nc, K, x_flat, a_d, b_d, N)
        stage3_triangle(nc, K, a_d, b_d, z_d, N)
        stage4_layer0(nc, K, x_flat, z_d, x1_d, N)
        stage5_project(nc, K, x1_d, W["mask"], h_d, N)
        stage6_triangles(nc, K, h_d, y_d, r_d, N)
        stage7_layer1(nc, K, y_d, r_d, x1_d, out_flat, N)


_WEIGHTS = {
    "Wa1": "L0_conv_Wa1", "ba1": "L0_conv_ba1", "Wa2": "L0_conv_Wa2", "ba2": "L0_conv_ba2",
    "Wb1": "L0_conv_Wb1", "bb1": "L0_conv_bb1", "Wb2": "L0_conv_Wb2", "bb2": "L0_conv_bb2",
    "ln2_g0": "L0_conv_ln2_g", "ln2_b0": "L0_conv_ln2_b", "Wg": "L0_conv_Wg", "bg": "L0_conv_bg",
    "Wz": "L0_conv_Wz", "bz": "L0_conv_bz", "mask": "L1_conv_mask", "ln1_w": "L1_conv_ln1_w",
    "ln1_b": "L1_conv_ln1_b", "pi_w": "L1_conv_pi_w", "pi_b": "L1_conv_pi_b", "gi_w": "L1_conv_gi_w",
    "gi_b": "L1_conv_gi_b", "ln2_w": "L1_conv_ln2_w", "ln2_b": "L1_conv_ln2_b", "po_w": "L1_conv_po_w",
    "po_b": "L1_conv_po_b", "go_w": "L1_conv_go_w", "go_b": "L1_conv_go_b",
}


def kernel(**inputs):
    import numpy as np
    import concourse.bacc as bacc
    from concourse.bass_utils import run_bass_kernel_spmd

    nc = bacc.Bacc("TRN2", target_bir_lowering=False, num_devices=1)
    arrays, weights = {}, {}

    def give(name, array):
        array = np.ascontiguousarray(array)
        arrays[f"in_{name}"] = array
        return nc.dram_tensor(f"in_{name}", array.shape, FP32, kind="ExternalInput").ap()

    x = give("x", inputs["x"][0])
    for short, name in _WEIGHTS.items():
        weights[short] = give(short, inputs[name][0] if short == "mask" else inputs[name])
    out = nc.dram_tensor("out", arrays["in_x"].shape, FP32, kind="ExternalOutput").ap()
    pair_layers(nc, x, weights, out)
    result = run_bass_kernel_spmd(nc, [arrays], core_ids=[0]).results[0]["out"]
    return result[None]
```

```python
import concourse.bass as bass
from concourse import mybir
from contextlib import ExitStack

FP32 = mybir.dt.float32
BF16 = mybir.dt.bfloat16
FP16 = mybir.dt.float16
ALU = mybir.AluOpType
ACT = mybir.ActivationFunctionType
AX = mybir.AxisListType

P = 128
BANK = 512
GN_EPS = 1e-5
LN_EPS = 1e-5


class Scope:

    def __init__(self, nc, stack, tag):
        self.nc, self.stack, self.tag = nc, stack, tag

    def sbuf(self, name, shape, dtype=FP32):
        return self.stack.enter_context(self.nc.sbuf_tensor(f"{self.tag}_{name}", shape, dtype))

    def psum(self, name, shape, dtype=FP32):
        return self.stack.enter_context(self.nc.psum_tensor(f"{self.tag}_{name}", shape, dtype))

    def sem(self, name):
        return self.stack.enter_context(self.nc.semaphore(f"{self.tag}_{name}"))

    def sems(self, name, n):
        return [self.sem(f"{name}{i}") for i in range(n)]


def column(vector):
    return vector.rearrange("(p a) -> p a", a=1)


def prepare(nc, K, W):
    with ExitStack() as stack:
        s = Scope(nc, stack, "w")
        pi, gi = s.sbuf("pi", [P, P]), s.sbuf("gi", [P, P])
        po, go = s.sbuf("po", [P, 64]), s.sbuf("go", [P, 64])
        cols = s.sbuf("cols", [P, 12])
        transposed = s.sbuf("transposed", [P, 4, P])
        Wab = s.sbuf("Wab", [P, 64])
        wide = s.sbuf("wide", [P, P])
        Wz = s.sbuf("Wz", [64, P])
        center = s.sbuf("center", [P, P])
        center64 = s.sbuf("center64", [64, P])
        ps_t = s.psum("ps_t", [P, 4, P])
        ps_b = s.psum("ps_b", [P, BANK])
        ps_c = s.psum("ps_c", [P, 4, P])
        loaded, built, turned, kept = s.sem("loaded"), s.sem("built"), s.sem("turned"), s.sem("kept")
        biased, centred, done = s.sem("biased"), s.sem("centred"), s.sem("done")
        rounded = s.sem("rounded")
        loads = [
            (Wab[:, 0:16], W["Wa1"]), (Wab[:, 16:32], W["Wb1"]), (Wab[:, 32:48], W["Wa2"]), (Wab[:, 48:64], W["Wb2"]),
            (K.bias_ab[:, 0:16], W["ba1"].partition_broadcast(P)), (K.bias_ab[:, 16:32], W["bb1"].partition_broadcast(P)),
            (K.bias_ab[:, 32:48], W["ba2"].partition_broadcast(P)), (K.bias_ab[:, 48:64], W["bb2"].partition_broadcast(P)),
            (K.Wg[:], W["Wg"]), (K.bg[:], column(W["bg"])),
            (pi[:], W["pi_w"]), (gi[:], W["gi_w"]), (po[:], W["po_w"]), (go[:], W["go_w"]),
            (cols[:, 0:1], column(W["bz"])), (cols[:, 1:2], column(W["pi_b"])), (cols[:, 2:3], column(W["gi_b"])),
            (cols[:, 3:4], column(W["po_b"])), (cols[:, 4:5], column(W["go_b"])),
            (cols[:, 5:6], column(W["ln1_w"])), (cols[:, 6:7], column(W["ln1_b"])),
            (cols[0:64, 7:8], column(W["ln2_w"])), (cols[64:128, 7:8], column(W["ln2_w"])),
            (cols[0:64, 8:9], column(W["ln2_b"])),
            (cols[0:16, 10:11], column(W["ln2_b0"])),
        ] + [(Wz[16 * k:16 * k + 16, :], W["Wz"]) for k in range(4)] + [
            (cols[16 * k:16 * k + 16, 9:10], column(W["ln2_g0"])) for k in range(4)]
        with nc.Block() as block:
            @block.sync
            def _(sp):
                for dst, src in loads:
                    sp.dma_start(dst, src).then_inc(loaded, 16)
                sp.wait_ge(loaded, 16 * len(loads))

            @block.gpsimd
            def _(pool):
                n = 0

                def step(ins):
                    nonlocal n
                    ins.then_inc(built, 1)
                    n += 1
                    pool.wait_ge(built, n)

                def diagonal(tile, pattern, base=0):
                    step(pool.affine_select(out=tile, in_=tile, compare_op=ALU.not_equal, fill=1.0, base=base,
                                            pattern=pattern, channel_multiplier=1))

                step(pool.memset(K.ident[:], 0.0))
                diagonal(K.ident[:], [[-1, P]])
                step(pool.memset(K.ident_bf[:], 0.0))
                diagonal(K.ident_bf[:], [[-1, P]])
                step(pool.memset(K.group_mean[:], 0.25))
                view = K.group_mean[:].rearrange("p (g c) -> p g c", c=4)
                step(pool.affine_select(out=view, in_=view, compare_op=ALU.is_ge, fill=0.0, base=0,
                                        pattern=[[-4, 32], [0, 4]], channel_multiplier=1))
                step(pool.affine_select(out=view, in_=view, compare_op=ALU.is_ge, fill=0.0, base=3,
                                        pattern=[[4, 32], [0, 4]], channel_multiplier=-1))
                step(pool.memset(K.select16[:], 0.0))
                for part in range(3):
                    diagonal(K.select16[:], [[-1, 16], [0, P]], base=-16 * part)
                step(pool.memset(K.halves[:], 1.0 / 16))
                step(pool.affine_select(out=K.halves[:, 0:64], in_=K.halves[:, 0:64], compare_op=ALU.is_ge, fill=0.0,
                                        base=2, pattern=[[0, 64]], channel_multiplier=-1))
                step(pool.affine_select(out=K.halves[:, 64:128], in_=K.halves[:, 64:128], compare_op=ALU.is_ge,
                                        fill=0.0, base=-3, pattern=[[0, 64]], channel_multiplier=1))
                step(pool.memset(K.mean_col[:], 1.0 / P))
                pool.memset(K.minus_half[:], -0.5).then_inc(built, 1)

            BUILT = 16

            @block.tensor
            def _(pe):
                pe.wait_ge(built, BUILT)
                pe.wait_ge(loaded, 16 * len(loads))
                pe.transpose(ps_t[:, 0, :], pi[:], K.ident[:]).then_inc(turned, 1)
                pe.transpose(ps_t[:, 1, :], gi[:], K.ident[:]).then_inc(turned, 1)
                pe.transpose(ps_t[0:64, 2, :], po[:], K.ident[:]).then_inc(turned, 1)
                pe.transpose(ps_t[0:64, 3, :], go[:], K.ident[:]).then_inc(turned, 1)
                pe.wait_ge(kept, 1)
                for n, (w, rows, b) in enumerate([(transposed[:, 0, :], P, 6), (transposed[:, 1, :], P, 6),
                                                  (transposed[0:64, 2, :], 64, 8), (transposed[0:64, 3, :], 64, 8),
                                                  (Wz[0:16, :], 16, 10)]):
                    pe.matmul(ps_b[:, n:n + 1], w, cols[0:rows, b:b + 1], start=True, stop=True).then_inc(biased, 1)
                pe.wait_ge(kept, 2)
                pe.matmul(ps_c[:, 0, :], center[:], transposed[:, 0, :], start=True, stop=True).then_inc(centred, 1)
                pe.matmul(ps_c[:, 1, :], center[:], transposed[:, 1, :], start=True, stop=True).then_inc(centred, 1)
                pe.matmul(ps_c[:, 2, :], center64[:], transposed[0:64, 2, :], start=True, stop=True).then_inc(centred, 1)
                pe.matmul(ps_c[:, 3, :], center64[:], transposed[0:64, 3, :], start=True, stop=True).then_inc(centred, 1)

            @block.vector
            def _(dve):
                dve.wait_ge(loaded, 16 * len(loads))
                dve.tensor_copy(K.Wab_high[:], Wab[:]).then_inc(rounded, 1)
                dve.wait_ge(rounded, 1)
                dve.tensor_tensor(K.Wab_low[:], Wab[:], K.Wab_high[:], ALU.subtract)
                dve.wait_ge(turned, 4)
                for n in range(4):
                    rows = P if n < 2 else 64
                    last = dve.tensor_copy(transposed[0:rows, n, :], ps_t[0:rows, n, :])
                last.then_inc(kept, 1)
                dve.wait_ge(built, BUILT)
                dve.tensor_scalar(center[:], K.ident[:], -1.0 / P, None, ALU.add)
                dve.tensor_scalar(center64[:, 0:64], K.ident[0:64, 0:64], -1.0 / 64, None, ALU.add)
                dve.tensor_scalar(center64[:, 64:128], K.ident[0:64, 0:64], -1.0 / 64, None, ALU.add)
                dve.wait_ge(biased, 5)
                for n, col in ((0, 5), (1, 5), (2, 7), (3, 7)):
                    rows = P if n < 2 else 64
                    last = dve.tensor_scalar(transposed[0:rows, n, :], transposed[0:rows, n, :],
                                             cols[0:rows, col:col + 1], None, ALU.mult)
                last.then_inc(kept, 1)
                dve.tensor_tensor(K.pi_bias[:], ps_b[:, 0:1], cols[:, 1:2], ALU.add)
                dve.tensor_tensor(K.gi_bias[:], ps_b[:, 1:2], cols[:, 2:3], ALU.add)
                dve.tensor_tensor(K.po_bias[:], ps_b[:, 2:3], cols[:, 3:4], ALU.add)
                dve.tensor_tensor(K.go_bias[:], ps_b[:, 3:4], cols[:, 4:5], ALU.add)
                dve.tensor_tensor(K.z_bias[:], ps_b[:, 4:5], cols[:, 0:1], ALU.add)
                dve.tensor_scalar(Wz[:], Wz[:], cols[0:64, 9:10], None, ALU.mult).then_inc(rounded, 1)
                dve.wait_ge(rounded, 2)
                dve.tensor_copy(K.Wz[:], Wz[:]).then_inc(rounded, 1)
                dve.wait_ge(rounded, 3)
                dve.tensor_tensor(K.Wz[32:64, :], Wz[32:64, :], K.Wz[32:64, :], ALU.subtract)
                dve.wait_ge(centred, 4)
                dve.tensor_copy(K.Wpi[:], ps_c[:, 0, :])
                dve.tensor_copy(K.Wgi[:], ps_c[:, 1, :])
                count = 3
                for n, w in ((2, K.Wpo), (3, K.Wgo)):
                    for e in range(2):
                        own, other = slice(64 * e, 64 * e + 64), slice(64 - 64 * e, 128 - 64 * e)
                        dve.memset(w[other, :, e, :], 0.0)
                        dve.tensor_scalar(wide[own, :], ps_c[own, n, :], 16.0, None, ALU.mult).then_inc(rounded, 1)
                        count += 1
                        dve.wait_ge(rounded, count)
                        dve.tensor_copy(w[own, 0, e, :], wide[own, :]).then_inc(rounded, 1)
                        count += 1
                        dve.wait_ge(rounded, count)
                        last = dve.tensor_tensor(w[own, 1, e, :], wide[own, :], w[own, 0, e, :], ALU.subtract)
                last.then_inc(done, 1)


def norm_from_moments(nc, s, block, K, moments, moments_ready):
    var, deviation = s.sbuf("gn_var", [P, 1]), s.sbuf("gn_dev", [P, 1])
    chain, var_ready, dev_ready = s.sem("gn_chain"), s.sem("gn_var_ready"), s.sem("gn_dev_ready")

    def vector_part(dve):
        dve.wait_ge(moments_ready, 2)
        dve.tensor_copy(K.gn_mean[:], moments[:, 0:1]).then_inc(chain, 1)
        dve.wait_ge(chain, 1)
        dve.tensor_tensor(var[:], K.gn_mean[:], K.gn_mean[:], ALU.mult).then_inc(chain, 1)
        dve.wait_ge(chain, 2)
        dve.tensor_tensor(var[:], moments[:, 1:2], var[:], ALU.subtract).then_inc(chain, 1)
        dve.wait_ge(chain, 3)
        dve.tensor_scalar(var[:], var[:], GN_EPS, None, ALU.add).then_inc(var_ready, 1)
        dve.wait_ge(dev_ready, 1)
        dve.reciprocal(K.gn_scale[:], deviation[:]).then_inc(chain, 1)
        dve.wait_ge(chain, 4)
        dve.scalar_tensor_tensor(K.gn_shift[:], K.gn_mean[:], -1.0, K.gn_scale[:], ALU.mult, ALU.mult).then_inc(chain, 1)
        dve.wait_ge(chain, 5)

    def scalar_part(act):
        act.wait_ge(var_ready, 1)
        act.activation(deviation[:], var[:], ACT.Sqrt).then_inc(dev_ready, 1)

    return vector_part, scalar_part


def stage1_statistics(nc, K, x, N):
    T = 128
    chunks = N * N // P // T
    x_v = x.rearrange("(p n t) c -> n p t c", p=P, t=T)
    with ExitStack() as stack:
        s = Scope(nc, stack, "s1")
        xt = s.sbuf("xt", [P, 2, T, P])
        stats = s.sbuf("stats", [P, 32, chunks, 6])
        mv = s.sbuf("mv", [P, 32, 2])
        square = s.sbuf("square", [P, 32])
        wide = s.sbuf("wide", [P, 2, 32, 4])
        moments = s.psum("moments", [P, 2])
        loaded = s.sems("loaded", 2)
        used, aggregated, wide_ready, moments_ready = s.sem("used"), s.sem("aggregated"), s.sem("wide_ready"), s.sem("moments_ready")
        with nc.Block() as block:
            norm_vector, norm_scalar = norm_from_moments(nc, s, block, K, moments, moments_ready)

            @block.sync
            def _(sp):
                with sp.Fori(0, chunks // 2) as r:
                    for u in range(2):
                        sp.wait_ge(used, r * 2 + (u + 1))
                        sp.dma_start(xt[:, u, :, :], x_v[bass.ds(r * 2 + u, 1)].rearrange("a p t c -> p (a t) c")).then_inc(loaded[u], 16)

            @block.vector
            def _(dve):
                dve.sem_inc(used, 2)
                with dve.Fori(0, chunks // 2) as r:
                    for u in range(2):
                        dve.wait_ge(loaded[u], r * 16 + 16)
                        for g in range(32):
                            last = dve.bn_stats(stats[:, g, bass.ds(r * 2 + u, 1), :].rearrange("p a s -> p (a s)"),
                                                xt[:, u, :, 4 * g:4 * g + 4])
                        last.then_inc(used, 1)
                dve.wait_ge(used, chunks + 2)
                for g in range(32):
                    dve.bn_aggr(mv[:, g, :], stats[:, g, :, :].rearrange("p n s -> p (n s)")).then_inc(aggregated, 1)
                dve.wait_ge(aggregated, 32)
                dve.tensor_tensor(square[:], mv[:, :, 0], mv[:, :, 0], ALU.mult).then_inc(aggregated, 1)
                dve.tensor_copy(wide[:, 0, :, :], mv[:, :, 0:1].to_broadcast([P, 32, 4]))
                dve.wait_ge(aggregated, 33)
                dve.tensor_tensor(square[:], square[:], mv[:, :, 1], ALU.add).then_inc(aggregated, 1)
                dve.wait_ge(aggregated, 34)
                dve.tensor_copy(wide[:, 1, :, :], square[:].rearrange("p (g a) -> p g a", a=1).to_broadcast([P, 32, 4])).then_inc(wide_ready, 1)
                norm_vector(dve)

            @block.tensor
            def _(pe):
                pe.wait_ge(wide_ready, 1)
                for m in range(2):
                    pe.matmul(moments[:, m:m + 1], wide[:, m, :, :].rearrange("p g c -> p (g c)"), K.mean_col[:],
                              start=True, stop=True).then_inc(moments_ready, 1)

            @block.scalar
            def _(act):
                norm_scalar(act)


def block_of(nc):
    def run(build):
        with nc.Block() as block:
            build(block)
    return run


def stage2_gates(nc, K, x, a_d, b_d, N):
    RB = N // P
    ROWS, UNITS = 8, 64
    PAIRS = UNITS // 2
    LAG = 4
    x_v = x.rearrange("(rb n r j) c -> rb n j r c", rb=RB, r=ROWS, j=N)
    with ExitStack() as stack:
        s = Scope(nc, stack, "s2")
        xt = s.sbuf("xt", [P, 4, ROWS, P])
        xh = s.sbuf("xh", [P, 4, BANK])
        high, low = s.sbuf("high", [P, 8, BANK], FP16), s.sbuf("low", [P, 8, BANK], FP16)
        pre = s.sbuf("pre", [P, 2, 8, 64])
        gate = s.sbuf("gate", [P, 2, 8, 32])
        ab = s.sbuf("ab", [P, 2, 32, P])
        b_out = s.sbuf("b_out", [P, 16, P])
        turned_ps = s.psum("turned_ps", [P, 4, BANK])
        proj_ps = s.psum("proj_ps", [P, 2, BANK])
        b_ps = s.psum("b_ps", [P, 2, BANK])
        loaded = s.sems("loaded", 4)
        turned, normed, multiplied = s.sem("turned"), s.sem("normed"), s.sem("multiplied")
        rounded, rest_ready = s.sems("rounded", 2), s.sems("rest_ready", 2)
        biased, gated, sig = s.sem("biased"), s.sem("gated"), s.sem("sig")
        b_turned, b_kept = s.sem("b_turned"), s.sem("b_kept")
        a_stored, b_stored = s.sems("a_stored", 2), s.sem("b_stored")

        @block_of(nc)
        def _(block):
            @block.sync
            def _(sp):
                with sp.Fori(0, RB) as rb:
                    with sp.Fori(0, RB // 2) as c2:
                        r = rb * (RB // 2) + c2
                        for n in range(32):
                            sp.wait_ge(turned, r * UNITS + (2 * n + 2))
                            src = x_v[bass.ds(rb, 1), n % 16, bass.ds((c2 * 2 + n // 16) * P, P)].rearrange("a j r c -> (a j) r c")
                            sp.dma_start(xt[:, n % 4, :, :], src).then_inc(loaded[n % 4], 16)

            @block.tensor
            def _(pe):
                pe.sem_inc(turned, 8)
                pe.sem_inc(multiplied, 8)

                def turn(r, u):
                    if u % 2 == 0:
                        pe.wait_ge(loaded[u // 2 % 4], r * 128 + 16 * (u // 8 + 1))
                    pe.wait_ge(normed, r * UNITS + (u + 1))
                    for k in range(4):
                        last = pe.transpose(turned_ps[:, u % 4, k * P:(k + 1) * P],
                                            xt[:, u // 2 % 4, 4 * (u % 2) + k, :], K.ident[:])
                    last.then_inc(turned, 1)

                def multiply(r, u):
                    pe.wait_ge(rest_ready[u % 2], r * PAIRS + (u // 2 + 3))
                    if u % 2 == 0:
                        pe.wait_ge(biased, r * PAIRS + (u // 2 + 1))
                    for k in range(4):
                        dst = proj_ps[:, u // 2 % 2, 64 * (4 * (u % 2) + k):64 * (4 * (u % 2) + k) + 64]
                        row = slice(k * P, (k + 1) * P)
                        pe.matmul(dst, high[:, u % 8, row], K.Wab_high[:], start=True, stop=False)
                        pe.matmul(dst, high[:, u % 8, row], K.Wab_low[:], start=False, stop=False)
                        last = pe.matmul(dst, low[:, u % 8, row], K.Wab_high[:], start=False, stop=True)
                    last.then_inc(multiplied, 1)

                def turn_b(r, half, n):
                    pe.wait_ge(sig, r * PAIRS + (16 * (half + 1) + 2))
                    pe.wait_ge(b_kept, r * 8 + (4 * half + n + 1))
                    for c in range(4):
                        last = pe.transpose(b_ps[:, n % 2, c * P:(c + 1) * P], ab[:, half, 16 + 4 * n + c, :], K.ident[:])
                    last.then_inc(b_turned, 1)

                with pe.Fori(0, RB * RB // 2) as r:
                    for v in range(UNITS + LAG):
                        if v < UNITS:
                            turn(r, v)
                        if v >= LAG:
                            multiply(r, v - LAG)
                        if 42 <= v < 46:
                            turn_b(r, 0, v - 42)
                    for n in range(4):
                        turn_b(r, 1, n)

            def round_high(engine, copy, r, u):
                engine.wait_ge(normed, r * UNITS + (u + 5))
                engine.wait_ge(multiplied, r * UNITS + (u + 1))
                copy(high[:, u % 8, :], xh[:, u % 4, :]).then_inc(rounded[u % 2], 1)

            def rest(engine, r, u):
                engine.wait_ge(rounded[u % 2], r * PAIRS + (u // 2 + 1))
                engine.tensor_tensor(low[:, u % 8, :], xh[:, u % 4, :], high[:, u % 8, :], ALU.subtract).then_inc(rest_ready[u % 2], 1)

            @block.scalar
            def _(act):
                act.sem_inc(normed, 4)
                act.sem_inc(sig, 2)
                act.sem_inc(b_kept, 2)
                act.sem_inc(b_turned, 8)
                for stored in a_stored + [b_stored]:
                    act.sem_inc(stored, 16)

                def copy(dst, src):
                    return act.activation(dst, src, ACT.Identity)

                def norm(r, u):
                    act.wait_ge(turned, r * UNITS + (u + 9))
                    act.wait_ge(rest_ready[u % 2], r * PAIRS + (u // 2 + 1))
                    act.activation(xh[:, u % 4, :], turned_ps[:, u % 4, :], ACT.Identity, bias=K.gn_shift[:],
                                   scale=K.gn_scale[:]).then_inc(normed, 1)

                def finish_sigmoid(r, q):
                    half, i0 = q // 16, 8 * (q % 16)
                    act.wait_ge(gated, r * PAIRS + (q + 1))
                    if q % 16 == 0:
                        act.wait_ge(a_stored[half], r * 16 + 16)
                        act.wait_ge(b_turned, r * 8 + (4 * half + 1))
                    act.activation(ab[:, half, :, i0:i0 + 8], gate[:, q % 2, :, :].rearrange("p r c -> p c r"),
                                   ACT.Sigmoid).then_inc(sig, 1)

                def keep_b(r, half, n):
                    if n == 0:
                        act.wait_ge(b_stored, r * 32 + 16 * (half + 1))
                    act.wait_ge(b_turned, r * 8 + (4 * half + n + 9))
                    act.activation(b_out[:, 4 * n:4 * n + 4, :], b_ps[:, n % 2, :].rearrange("p (c j) -> p c j", j=P),
                                   ACT.Identity).then_inc(b_kept, 1)

                def store_a(rb, c2, r, half):
                    act.wait_ge(sig, r * PAIRS + (16 * (half + 1) + 2))
                    act.dma_start(a_d[bass.ds(c2 * 2 + half, 1), :, :, bass.ds(rb * P, P)].rearrange("a p c i -> (a p) c i"),
                                  ab[:, half, 0:16, :]).then_inc(a_stored[half], 16)

                def store_b(rb, c2, r, half):
                    act.wait_ge(b_kept, r * 8 + (4 * (half + 1) + 2))
                    act.dma_start(b_d[bass.ds(rb, 1), :, :, bass.ds((c2 * 2 + half) * P, P)].rearrange("a p c i -> (a p) c i"),
                                  b_out[:]).then_inc(b_stored, 16)

                with act.Fori(0, RB) as rb:
                    with act.Fori(0, RB // 2) as c2:
                        r = rb * (RB // 2) + c2
                        for u in range(UNITS):
                            norm(r, u)
                            if u % 2 == 1:
                                round_high(act, copy, r, u - 1)
                            if u % 2 == 1 and u >= LAG + 3:
                                finish_sigmoid(r, (u - LAG - 3) // 2)
                            if u == 39:
                                store_a(rb, c2, r, 0)
                            if 44 <= u < 48:
                                keep_b(r, 0, u - 44)
                            if u == 49:
                                store_b(rb, c2, r, 0)
                        for q in range(PAIRS - LAG // 2 - 1, PAIRS):
                            finish_sigmoid(r, q)
                        store_a(rb, c2, r, 1)
                        for n in range(4):
                            keep_b(r, 1, n)
                        store_b(rb, c2, r, 1)
                for half in range(2):
                    act.wait_ge(a_stored[half], RB * RB * 8 + 16)
                act.wait_ge(b_stored, RB * RB * 16 + 16)

            @block.gpsimd
            def _(pool):
                with pool.Fori(0, RB * RB // 2) as r:
                    for u in range(1, UNITS, 2):
                        rest(pool, r, u)

            @block.vector
            def _(dve):
                for sem in rest_ready:
                    dve.sem_inc(sem, 2)
                dve.sem_inc(biased, 2)

                def multiply_halves(r, q):
                    dve.wait_ge(multiplied, r * UNITS + (2 * q + 10))
                    dve.wait_ge(sig, r * PAIRS + (q + 1))
                    dve.tensor_tensor(pre[:, q % 2, :, :], proj_ps[:, q % 2, :].rearrange("p (r c) -> p r c", c=64),
                                      K.bias_ab[:].rearrange("p (a c) -> p a c", a=1).to_broadcast([P, 8, 64]),
                                      ALU.add).then_inc(biased, 1)
                    dve.wait_ge(biased, r * PAIRS + (q + 3))
                    dve.tensor_tensor(gate[:, q % 2, :, :], pre[:, q % 2, :, 0:32], pre[:, q % 2, :, 32:64],
                                      ALU.mult).then_inc(gated, 1)

                with dve.Fori(0, RB * RB // 2) as r:
                    for u in range(UNITS):
                        if u % 2 == 1:
                            round_high(dve, dve.tensor_copy, r, u)
                            rest(dve, r, u - 1)
                        if u % 2 == 1 and u >= LAG + 1:
                            multiply_halves(r, (u - LAG - 1) // 2)
                    for q in range(PAIRS - LAG // 2, PAIRS):
                        multiply_halves(r, q)


def stage3_triangle(nc, K, a_d, b_d, z_d, N):
    RB, C, SLOTS = N // P, 16, 4
    with ExitStack() as stack:
        s = Scope(nc, stack, "s3")
        at = s.sbuf("at", [P, SLOTS, RB, P])
        bt = s.sbuf("bt", [P, SLOTS, RB, N])
        z = s.sbuf("z", [P, C, N])
        centred = s.sbuf("centred", [P, C, N])
        squares = s.sbuf("squares", [P, C, N])
        parts = s.sbuf("parts", [P, 2, C, N], FP16)
        mean, var, dev = s.sbuf("mean", [P, N]), s.sbuf("var", [P, N]), s.sbuf("dev", [P, N])
        z_ps = s.psum("z_ps", [P, 8, BANK])
        loaded = s.sems("loaded", SLOTS)
        product, copied, chain, cent, sq, var_ready, dev_ready, z_ready, stored, left = [
            s.sem(n) for n in ("product", "copied", "chain", "cent", "sq", "var_ready", "dev_ready", "z_ready", "stored", "left")]
        z_rounded, z_split = s.sem("z_rounded"), s.sem("z_split")
        CHAIN = 4

        @block_of(nc)
        def _(block):
            @block.sync
            def _(sp):
                with sp.Fori(0, RB) as ib:
                    for c in range(C):
                        sp.wait_ge(product, ib * C + (c + 1))
                        sp.dma_start(at[:, c % SLOTS, :, :], a_d[:, :, c, bass.ds(ib * P, P)].rearrange("k p i -> p k i")).then_inc(loaded[c % SLOTS], 16)
                        sp.dma_start(bt[:, c % SLOTS, :, :], b_d[:, :, c, :].rearrange("k p j -> p k j")).then_inc(loaded[c % SLOTS], 16)

            @block.tensor
            def _(pe):
                pe.sem_inc(product, SLOTS)
                with pe.Fori(0, RB) as ib:
                    for c in range(C):
                        pe.wait_ge(loaded[c % SLOTS], ib * (32 * C // SLOTS) + 32 * (c // SLOTS + 1))
                        pe.wait_ge(copied, ib * C + (c + 1))
                        for kb in range(RB):
                            last = pe.matmul(z_ps[:, c % 8, 0:N], at[:, c % SLOTS, kb, :], bt[:, c % SLOTS, kb, :],
                                             start=kb == 0, stop=kb == RB - 1)
                        last.then_inc(product, 1)

            @block.scalar
            def _(act):
                act.sem_inc(copied, 8)
                with act.Fori(0, RB) as ib:
                    act.wait_ge(cent, ib + 1)
                    for c in range(C):
                        act.wait_ge(product, ib * C + (c + 1 + SLOTS))
                        act.activation(z[:, c, :], z_ps[:, c % 8, 0:N], ACT.Copy).then_inc(copied, 1)
                    act.wait_ge(cent, ib + 2)
                    act.activation(squares[:], centred[:], ACT.Square).then_inc(sq, 1)
                    act.wait_ge(var_ready, ib + 1)
                    act.activation(dev[:], var[:], ACT.Sqrt).then_inc(dev_ready, 1)
                    act.wait_ge(left, ib + 1)
                    for half in range(2):
                        channels = slice(half * C // 2, (half + 1) * C // 2)
                        act.wait_ge(z_ready, ib * 2 + (half + 1))
                        act.activation(parts[:, 0, channels, :], centred[:, channels, :], ACT.Copy).then_inc(z_rounded, 1)

            @block.vector
            def _(dve):
                dve.sem_inc(cent, 1)

                def over_channels(tile):
                    return tile[:].rearrange("p c j -> p j c")

                def every_channel(tile, channels=C):
                    return tile[:].rearrange("p (a j) -> p a j", a=1).to_broadcast([P, channels, N])

                with dve.Fori(0, RB) as ib:
                    dve.wait_ge(copied, ib * C + (C + 8))
                    dve.tensor_reduce(mean[:], over_channels(z), AX.X, ALU.add).then_inc(chain, 1)
                    dve.wait_ge(chain, ib * CHAIN + 1)
                    dve.tensor_scalar(mean[:], mean[:], 1.0 / C, None, ALU.mult).then_inc(chain, 1)
                    dve.wait_ge(chain, ib * CHAIN + 2)
                    dve.tensor_tensor(centred[:], z[:], every_channel(mean), ALU.subtract).then_inc(cent, 1)
                    dve.wait_ge(sq, ib + 1)
                    dve.tensor_reduce(var[:], over_channels(squares), AX.X, ALU.add).then_inc(chain, 1)
                    dve.wait_ge(chain, ib * CHAIN + 3)
                    dve.tensor_scalar(var[:], var[:], 1.0 / C, LN_EPS, ALU.mult, ALU.add).then_inc(var_ready, 1)
                    dve.wait_ge(dev_ready, ib + 1)
                    dve.reciprocal(dev[:], dev[:]).then_inc(chain, 1)
                    dve.wait_ge(chain, ib * CHAIN + 4)
                    halves = [slice(half * C // 2, (half + 1) * C // 2) for half in range(2)]
                    for channels in halves:
                        dve.tensor_tensor(centred[:, channels, :], centred[:, channels, :], every_channel(dev, C // 2),
                                          ALU.mult).then_inc(z_ready, 1)
                    for half, channels in enumerate(halves):
                        dve.wait_ge(z_rounded, ib * 2 + (half + 1))
                        dve.tensor_tensor(parts[:, 1, channels, :], centred[:, channels, :], parts[:, 0, channels, :],
                                          ALU.subtract).then_inc(z_split, 1)

            @block.gpsimd
            def _(pool):
                pool.sem_inc(left, 1)
                with pool.Fori(0, RB) as ib:
                    pool.wait_ge(z_split, ib * 2 + 2)
                    pool.dma_start(z_d[:, bass.ds(ib * P, P), :].rearrange("c i j -> i c j"),
                                   parts[:].rearrange("p h c j -> p (h c) j")).then_inc(stored, 16)
                    pool.wait_ge(stored, ib * 16 + 16)
                    pool.sem_inc(left, 1)


def stage4_layer0(nc, K, x, z_d, x1_d, N):
    CB, U = N // P, 4
    x_v = x.rearrange("(i q p) c -> p i q c", q=CB, p=P)
    with ExitStack() as stack:
        s = Scope(nc, stack, "s4")
        xt = s.sbuf("xt", [P, 4, 2, CB, P])
        zt = s.sbuf("zt", [64, 2, U, N], FP16)
        xT = s.sbuf("xT", [P, 8, N])
        g = s.sbuf("g", [P, 2, N])
        gz = s.sbuf("gz", [P, 4, N])
        x1T = s.sbuf("x1T", [P, 4, 2, N])
        stats = s.sbuf("stats", [P, N, 6])
        mv = s.sbuf("mv", [P, 2])
        pair = s.sbuf("pair", [P, 2])
        Wg = s.sbuf("Wg", [P, P])
        bg = s.sbuf("bg", [P, 1])
        x_ps = s.psum("x_ps", [P, 4, BANK])
        g_ps = s.psum("g_ps", [P, 2, BANK])
        z_ps = s.psum("z_ps", [P, 2, BANK])
        loaded, z_loaded, stored = s.sems("loaded", 4), s.sems("z_loaded", 2), s.sems("stored", 4)
        turned, kept, g_prod, z_prod, sig, mixed, added, counted = [
            s.sem(n) for n in ("turned", "kept", "g_prod", "z_prod", "sig", "mixed", "added", "counted")]
        folded, shifted, moments_ready, chain = s.sem("folded"), s.sem("shifted"), s.sem("moments_ready"), s.sem("chain")

        @block_of(nc)
        def _(block):
            moments = g_ps[:, 0, 0:2]
            norm_vector, norm_scalar = norm_from_moments(nc, s, block, K, moments, moments_ready)

            @block.sync
            def _(sp):
                def load_x(r, n):
                    r, n = r + n // 4, n % 4
                    sp.wait_ge(turned, r * 8 + (2 * n + 2))
                    sp.dma_start(xt[:, n, :, :, :], x_v[:, bass.ds(r * 8 + 2 * n, 2)]).then_inc(loaded[n], 16)

                def load_z(r, h):
                    sp.wait_ge(z_prod, r * 8 + (4 * h + 4))
                    for k in range(2):
                        sp.dma_start(zt[32 * k:32 * k + 32, h, :, :], z_d[:, bass.ds(r * 8 + 4 * h, U), :]).then_inc(z_loaded[h], 16)

                def step(r, n, loads=0):
                    sp.wait_ge(added, r * 8 + (2 * n + 10))
                    sp.dma_start(x1_d[:, bass.ds(r * 8 + 2 * n, 2), :], x1T[:, n, :, :]).then_inc(stored[n], 16)
                    if n % 2 == 1 and loads >= 1:
                        load_z(r + 1, n // 2)
                    if loads == 2 or loads == 1 and n < 2:
                        load_x(r + 1, n + 2)

                for n in range(4):
                    sp.sem_inc(stored[n], 16)
                    load_x(0, n)
                    if n < 2:
                        load_z(0, n)
                load_x(1, 0)
                load_x(1, 1)
                with sp.Fori(0, N // 8 - 2) as r:
                    for n in range(4):
                        step(r, n, loads=2)
                for r in (N // 8 - 2, N // 8 - 1):
                    for n in range(4):
                        step(r, n, loads=N // 8 - 1 - r)
                for n in range(4):
                    sp.wait_ge(stored[n], 2 * N + 16)

            @block.tensor
            def _(pe):
                pe.sem_inc(turned, 8)
                pe.sem_inc(z_prod, 8)
                pe.matmul(g_ps[:, 0, 0:1], K.Wg[:], K.gn_shift[:], start=True, stop=True).then_inc(shifted, 1)
                pe.wait_ge(folded, 2)
                def turn(r, i):
                    r, i = r + i // 8, i % 8
                    if i % 2 == 0:
                        pe.wait_ge(loaded[i // 2], r * 16 + 16)
                    pe.wait_ge(kept, r * 8 + (i + 1))
                    for q in range(CB):
                        last = pe.transpose(x_ps[:, i % 4, q * P:(q + 1) * P], xt[:, i // 2, i % 2, q, :], K.ident[:])
                    last.then_inc(turned, 1)

                def step(r, i, last=False):
                    if i % 4 == 0:
                        pe.wait_ge(z_loaded[i // 4], r * 32 + 32)
                    pe.wait_ge(mixed, r * 8 + (i + 1))
                    pe.matmul(z_ps[:, i % 2, 0:N], K.Wz[:], zt[:, i // 4, i % 4, :], start=True, stop=True).then_inc(z_prod, 1)
                    pe.wait_ge(kept, r * 8 + (i + 5))
                    pe.matmul(g_ps[:, i % 2, 0:N], Wg[:], xT[:, i, :], start=True, stop=True).then_inc(g_prod, 1)
                    if not (last and i + 4 >= 8):
                        turn(r, i + 4)

                for i in range(4):
                    turn(0, i)
                with pe.Fori(0, N // 8 - 1) as r:
                    for i in range(8):
                        step(r, i)
                for i in range(8):
                    step(N // 8 - 1, i, last=True)
                pe.wait_ge(chain, 3)
                for m in range(2):
                    pe.matmul(moments[:, m:m + 1], K.group_mean[:], pair[:, m:m + 1], start=True, stop=True).then_inc(moments_ready, 1)

            @block.scalar
            def _(act):
                act.sem_inc(kept, 4)
                def keep(r, i):
                    act.wait_ge(turned, r * 8 + (i + 9))
                    act.wait_ge(added, r * 8 + (i + 1))
                    act.activation(xT[:, i % 8, :], x_ps[:, i % 4, 0:N], ACT.Identity).then_inc(kept, 1)

                def step(r, i, last=False):
                    act.wait_ge(g_prod, r * 8 + (i + 1))
                    act.activation(g[:, i % 2, :], g_ps[:, i % 2, 0:N], ACT.Sigmoid, bias=bg[:]).then_inc(sig, 1)
                    if not (last and i + 4 >= 8):
                        keep(r, i + 4)

                act.activation(g[:, 0, 0:1], K.bg[:], ACT.Sigmoid)
                for i in range(4):
                    keep(0, i)
                with act.Fori(0, N // 8 - 1) as r:
                    for i in range(8):
                        step(r, i)
                for i in range(8):
                    step(N // 8 - 1, i, last=True)
                norm_scalar(act)

            @block.vector
            def _(dve):
                dve.sem_inc(mixed, 2)
                dve.tensor_scalar(Wg[:], K.Wg[:], K.gn_scale[:], None, ALU.mult).then_inc(folded, 1)
                dve.wait_ge(shifted, 1)
                dve.tensor_tensor(bg[:], g_ps[:, 0, 0:1], K.bg[:], ALU.add).then_inc(folded, 1)

                def statistics(r, i):
                    dve.wait_ge(added, r * 8 + (i + 9))
                    dve.bn_stats(stats[:, bass.ds(r * 8 + i, 1), :].rearrange("p a s -> p (a s)"),
                                 x1T[:, i // 2, i % 2, :]).then_inc(counted, 1)

                dve.sem_inc(counted, 8)

                def mix(r, i):
                    dve.wait_ge(sig, r * 8 + (i + 1))
                    dve.wait_ge(z_prod, r * 8 + (i + 9))
                    dve.wait_ge(added, r * 8 + (i + 5))
                    dve.scalar_tensor_tensor(gz[:, i % 4, :], z_ps[:, i % 2, 0:N], K.z_bias[:], g[:, i % 2, :],
                                             ALU.add, ALU.mult).then_inc(mixed, 1)

                def step(r, i, last=False):
                    if not (last and i + 2 >= 8):
                        mix(r, i + 2)
                    statistics(r, i)

                mix(0, 0)
                mix(0, 1)
                with dve.Fori(0, N // 8 - 1) as r:
                    for i in range(8):
                        step(r, i)
                for i in range(8):
                    step(N // 8 - 1, i, last=True)
                dve.wait_ge(counted, N + 8)
                dve.bn_aggr(mv[:], stats[:].rearrange("p n s -> p (n s)")).then_inc(chain, 1)
                dve.wait_ge(chain, 1)
                dve.tensor_copy(pair[:, 0:1], mv[:, 0:1])
                dve.tensor_tensor(pair[:, 1:2], mv[:, 0:1], mv[:, 0:1], ALU.mult).then_inc(chain, 1)
                dve.wait_ge(chain, 2)
                dve.tensor_tensor(pair[:, 1:2], pair[:, 1:2], mv[:, 1:2], ALU.add).then_inc(chain, 1)
                norm_vector(dve)

            @block.gpsimd
            def _(pool):
                pool.sem_inc(added, 8)
                with pool.Fori(0, N // 8) as r:
                    for i in range(8):
                        if i % 2 == 0:
                            pool.wait_ge(stored[i // 2], r * 16 + 16)
                        pool.wait_ge(counted, r * 8 + (i + 1))
                        pool.wait_ge(mixed, r * 8 + (i + 3))
                        pool.tensor_tensor(x1T[:, i // 2, i % 2, :], gz[:, i % 4, :], xT[:, i, :], ALU.add).then_inc(added, 1)


def stage5_project(nc, K, x1_d, mask, h_d, N):
    RB, GROUPS = N // P, 8
    last_region = RB * RB
    with ExitStack() as stack:
        s = Scope(nc, stack, "s5")
        xg = s.sbuf("xg", [P, 2, 8, P])
        xh = s.sbuf("xh", [P, 4, 16, P])
        xc = s.sbuf("xc", [P, 2, BANK])
        gate = s.sbuf("gate", [P, 2, BANK])
        h = s.sbuf("h", [P, P, P])
        rows_out = s.sbuf("rows_out", [P, 2, BANK])
        out1 = s.sbuf("out1", [P, 64, P])
        out2 = s.sbuf("out2", [P, 64, P])
        mask_n = s.sbuf("mask_n", [P, RB, N])
        mask_t = s.sbuf("mask_t", [P, RB, N])
        stats = s.sbuf("stats", [P, 16, 6])
        spread_m, within, var, rstd, rest = [s.sbuf(n, [P, 16]) for n in ("spread_m", "within", "var", "rstd", "rest")]
        parts = s.sbuf("parts", [P, 48], BF16)
        rows = s.sbuf("rows", [48, 2, P], BF16)
        x_ps = s.psum("x_ps", [P, 2, BANK])
        rstd_ps = s.psum("rstd_ps", [P, BANK])
        p_ps = s.psum("p_ps", [P, 2, BANK])
        g_ps = s.psum("g_ps", [P, BANK])
        t_ps = s.psum("t_ps", [P, 2, BANK])
        parts_ps = x_ps[0:48, 0, 0:64].bitcast(BF16)

        def column_bank(n):
            return (t_ps if n % 4 < 2 else p_ps)[:, n % 2, :]

        loaded = s.sems("loaded", 2)
        mask_loaded, mask_turned, mask_kept = [s.sem(n) for n in ("mask_loaded", "mask_turned", "mask_kept")]
        normed, x_turned, counted, var_ready, rstd_ready, parts_ready, parts_turned, rows_ready, chain = [
            s.sem(n) for n in ("normed", "x_turned", "counted", "var_ready", "rstd_ready", "parts_ready", "parts_turned", "rows_ready", "chain")]
        rows_copied = s.sem("rows_copied")
        spread, scaled, p_done, g_done, sig, h_ready, h_turned, rows_kept, cols_kept = [
            s.sem(n) for n in ("spread", "scaled", "p_done", "g_done", "sig", "h_ready", "h_turned", "rows_kept", "cols_kept")]
        stored, met = s.sems("stored", 2), s.sem("met")
        CHAIN = 8
        PARTS = 4

        @block_of(nc)
        def _(block):
            @block.sync
            def _(sp):
                sp.dma_start(mask_n[:], mask.rearrange("(b p) j -> p b j", p=P)).then_inc(mask_loaded, 16)

                def load(g, n):
                    place = g % last_region
                    sp.wait_ge(normed, g * 32 + (2 * n + 1))
                    src = x1_d[:, bass.ds(place // RB * P + 8 * n, 8), bass.ds(place % RB * P, P)]
                    sp.dma_start(xg[:, n % 2, :, :], src).then_inc(loaded[n % 2], 16)

                def store(g, t, out, part):
                    block = bass.ds(g % RB, 1) if t == 0 else bass.ds(g // RB, 1)
                    tokens = bass.ds(g // RB * P, P) if t == 0 else bass.ds(g % RB * P, P)
                    channels = slice(part * 64 // PARTS, (part + 1) * 64 // PARTS)
                    sp.dma_start(h_d[t, block, :, channels, tokens].rearrange("a p c i -> (a p) c i"),
                                 out[:, channels, :]).then_inc(stored[t], 16)

                def region(g, last=False):
                    for n in range(10, 16):
                        load(g, n)
                    for n in range(8):
                        load(g + 1, n)
                    sp.wait_ge(rows_kept, g * 16 + 18)
                    for part in range(PARTS):
                        store(g, 0, out1, part)
                    sp.wait_ge(cols_kept, g * 16 + 18)
                    for part in range(PARTS):
                        store(g, 1, out2, part)
                        if part < 2 and not last:
                            load(g + 1, 8 + part)

                for m in range(2):
                    sp.sem_inc(stored[m], 16 * PARTS)
                for n in range(10):
                    load(0, n)
                with sp.Fori(0, last_region - 1) as g:
                    region(g)
                region(last_region - 1, last=True)
                for m in range(2):
                    sp.wait_ge(stored[m], 16 * PARTS * (last_region + 1))
                    sp.wait_ge(loaded[m], last_region * 128 + 64)

            @block.scalar
            def _(act):
                act.sem_inc(normed, 3)

                def norm(g, unit):
                    if unit % 2 == 0:
                        act.wait_ge(loaded[unit // 2 % 2], g * 128 + 16 * (unit // 4 + 1))
                    if unit % 4 == 0:
                        act.wait_ge(scaled, g * 32 + (unit + 4))
                    src = xg[:, unit // 2 % 2, 4 * (unit % 2):4 * (unit % 2) + 4, :]
                    act.activation(xh[:, unit // 4 % 4, 4 * (unit % 4):4 * (unit % 4) + 4, :], src,
                                   ACT.Identity, bias=K.gn_shift[:], scale=K.gn_scale[:]).then_inc(normed, 1)

                def keep_rows(G, q):
                    act.wait_ge(parts_turned, G + 1)
                    act.activation(rows[:, q % 2, :], parts_ps, ACT.Identity).then_inc(rows_ready, 1)

                def copy_rows(g, n):
                    act.wait_ge(h_turned, g * 32 + (n + 33))
                    act.wait_ge(rows_kept, g * 16 + (n + 1))
                    act.activation(rows_out[:, n % 2, :], t_ps[:, n % 2, :], ACT.Identity).then_inc(rows_copied, 1)

                act.sem_inc(sig, 1)
                for unit in range(12):
                    norm(0, unit)
                keep_rows(0, 0)
                with act.Fori(0, last_region) as g:
                    for q in range(GROUPS):
                        for n in range(4):
                            unit = 4 * q + n
                            act.wait_ge(g_done, g * 32 + (unit + 1))
                            act.wait_ge(h_ready, g * 32 + (unit + 1))
                            act.activation(gate[:, unit % 2, :], g_ps[:], ACT.Sigmoid, bias=K.gi_bias[:]).then_inc(sig, 1)
                            if n == 2:
                                keep_rows(g * 8 + (q + 1), q + 1)
                            norm(g, unit + 12)
                            if unit % 2 == 0 and unit >= 2:
                                copy_rows(g, unit // 2 - 1)
                    copy_rows(g, 15)

            @block.gpsimd
            def _(pool):
                def power(G):
                    pool.wait_ge(var_ready, G + 1)
                    pool.tensor_tensor(rstd[:], var[:], K.minus_half[:], ALU.pow).then_inc(rstd_ready, 1)

                def keep_rows(g, rb, cb, n):
                    if n == 0:
                        pool.wait_ge(stored[0], (g * 16 + 16) * PARTS)
                    mask = mask_t[:, bass.ds(cb, 1), bass.ds(rb * P + 8 * n, 8)]
                    pool.wait_ge(rows_copied, g * 16 + (n + 1))
                    pool.tensor_tensor(out1[:, :, 8 * n:8 * n + 8].rearrange("p c i -> p i c"),
                                       rows_out[:, n % 2, :].rearrange("p (i c) -> p i c", c=64),
                                       mask.rearrange("p a i -> p i a").to_broadcast([P, 8, 64]), ALU.mult).then_inc(rows_kept, 1)

                pool.sem_inc(rows_kept, 2)
                power(0)
                power(1)
                pool.wait_ge(mask_kept, RB)
                with pool.Fori(0, RB) as rb:
                    with pool.Fori(0, RB) as cb:
                        g = rb * RB + cb
                        for q in range(GROUPS):
                            if q >= 1:
                                keep_rows(g, rb, cb, 2 * q - 1)
                            power(g * 8 + (q + 2))
                            keep_rows(g, rb, cb, 2 * q)
                        keep_rows(g, rb, cb, 15)

            @block.vector
            def _(dve):
                dve.sem_inc(scaled, 16)
                dve.sem_inc(counted, 2)
                dve.sem_inc(h_ready, 2)
                dve.sem_inc(cols_kept, 2)
                for b in range(RB):
                    dve.wait_ge(mask_turned, b + 1)
                    dve.tensor_copy(mask_t[:, b, :], t_ps[:, b % 2, 0:N]).then_inc(mask_kept, 1)

                def statistics(g, unit, between=None):
                    dve.wait_ge(x_turned, g * 32 + (unit + 1))
                    for r in range(4):
                        if r == 2 and between:
                            split(*between)
                        last = dve.bn_stats(stats[:, 4 * (unit % 4) + r, :], x_ps[:, unit % 2, r * P:(r + 1) * P])
                    last.then_inc(counted, 1)

                def variance(g, q):
                    base = (g * 8 + q) * CHAIN
                    dve.wait_ge(counted, g * 32 + (4 * q + 6))
                    dve.tensor_tensor(spread_m[:], stats[:, :, 1], stats[:, :, 4], ALU.subtract).then_inc(chain, 1)
                    dve.tensor_tensor(within[:], stats[:, :, 2], stats[:, :, 5], ALU.add).then_inc(chain, 1)
                    dve.wait_ge(chain, base + 2)
                    dve.scalar_tensor_tensor(spread_m[:], spread_m[:], 0.25, spread_m[:], ALU.mult, ALU.mult).then_inc(chain, 1)
                    dve.wait_ge(chain, base + 3)
                    dve.scalar_tensor_tensor(var[:], within[:], 1.0 / P, spread_m[:], ALU.mult, ALU.add).then_inc(chain, 1)
                    dve.wait_ge(chain, base + 4)
                    dve.tensor_scalar(var[:], var[:], LN_EPS, None, ALU.add).then_inc(var_ready, 1)

                def split(g, q, step):
                    base = (g * 8 + q) * CHAIN
                    if step == 0:
                        dve.wait_ge(rstd_ready, g * 8 + (q + 1))
                        dve.tensor_copy(parts[:, 0:16], rstd[:]).then_inc(chain, 1)
                        return
                    dve.wait_ge(chain, base + (4 + step))
                    if step == 1:
                        dve.tensor_tensor(rest[:], rstd[:], parts[:, 0:16], ALU.subtract).then_inc(chain, 1)
                    elif step == 2:
                        dve.tensor_copy(parts[:, 16:32], rest[:]).then_inc(chain, 1)
                    elif step == 3:
                        dve.tensor_tensor(rest[:], rest[:], parts[:, 16:32], ALU.subtract).then_inc(chain, 1)
                    else:
                        dve.tensor_copy(parts[:, 32:48], rest[:]).then_inc(parts_ready, 1)

                def scale(g, unit):
                    dve.wait_ge(spread, g * 32 + (unit + 1))
                    x = xh[:, unit // 4 % 4, 4 * (unit % 4):4 * (unit % 4) + 4, :].rearrange("p r j -> p (r j)")
                    dve.tensor_tensor(xc[:, unit % 2, :], x, rstd_ps[:], ALU.mult).then_inc(scaled, 1)

                def gate_h(g, unit):
                    if unit == 0:
                        dve.wait_ge(h_turned, g * 32 + 32)
                    dve.wait_ge(sig, g * 32 + (unit + 2))
                    dve.wait_ge(p_done, g * 32 + (unit + 1))
                    dve.scalar_tensor_tensor(h[:, 4 * unit:4 * unit + 4, :].rearrange("p r j -> p (r j)"), p_ps[:, unit % 2, :],
                                             K.pi_bias[:], gate[:, unit % 2, :], ALU.add, ALU.mult).then_inc(h_ready, 1)

                def keep_columns(g, rb, cb, n):
                    if n == 0:
                        dve.wait_ge(stored[1], (g * 16 + 16) * PARTS)
                    mask = mask_n[:, bass.ds(rb, 1), bass.ds(cb * P + 8 * n, 8)]
                    dve.wait_ge(h_turned, g * 32 + (n + 49))
                    dve.tensor_tensor(out2[:, :, 8 * n:8 * n + 8].rearrange("p c i -> p i c"),
                                      column_bank(n).rearrange("p (i c) -> p i c", c=64),
                                      mask.rearrange("p a i -> p i a").to_broadcast([P, 8, 64]), ALU.mult).then_inc(cols_kept, 1)

                for unit in range(4):
                    statistics(0, unit)
                variance(0, 0)
                for step in range(5):
                    split(0, 0, step)
                for unit in range(4, 8):
                    statistics(0, unit)
                variance(0, 1)
                scale(0, 0)
                with dve.Fori(0, RB) as rb:
                    with dve.Fori(0, RB) as cb:
                        g = rb * RB + cb
                        scale(g, 1)
                        for q in range(GROUPS):
                            for n in range(4):
                                unit = 4 * q + n
                                gate_h(g, unit)
                                if n == 1:
                                    split(g, q + 1, 0)
                                if unit < 31:
                                    scale(g, unit + 2)
                                if n == 1:
                                    split(g, q + 1, 1)
                                statistics(g, unit + 8, (g, q + 1, 2) if n == 1 else None)
                                if n == 1:
                                    split(g, q + 1, 3)
                                    split(g, q + 1, 4)
                                if n == 3:
                                    variance(g, q + 2)
                        for n in range(16):
                            keep_columns(g, rb, cb, n)

            @block.tensor
            def _(pe):
                pe.sem_inc(h_turned, 32)
                pe.wait_ge(mask_loaded, 16)
                for cb in range(RB):
                    if cb >= 2:
                        pe.wait_ge(mask_kept, cb - 1)
                    for rb in range(RB):
                        last = pe.transpose(t_ps[:, cb % 2, rb * P:(rb + 1) * P], mask_n[:, rb, cb * P:(cb + 1) * P], K.ident[:])
                    last.then_inc(mask_turned, 1)
                pe.wait_ge(mask_kept, RB)

                def wait_apart(semaphore, value):
                    pe.wait_ge(semaphore, value)
                    pe.sem_inc(met, 1)

                def turn_tokens(g, unit, parts_before=0):
                    pe.wait_ge(normed, g * 32 + (unit + 4))
                    pe.wait_ge(counted, g * 32 + (unit + 1))
                    if parts_before:
                        pe.wait_ge(rows_ready, g * 8 + parts_before)
                    for r in range(4):
                        last = pe.transpose(x_ps[:, unit % 2, r * P:(r + 1) * P], xh[:, unit // 4 % 4, 4 * (unit % 4) + r, :], K.ident[:])
                    last.then_inc(x_turned, 1)

                def turn_parts(g, q, unit):
                    wait_apart(counted, g * 32 + (unit + 3))
                    wait_apart(parts_ready, g * 8 + (q + 1))
                    pe.transpose(parts_ps, parts[:], K.ident_bf[:]).then_inc(parts_turned, 1)

                def spread_scale(g, unit):
                    if unit % 4 == 0:
                        pe.wait_ge(rows_ready, g * 8 + (unit // 4 + 1))
                    pe.wait_ge(scaled, g * 32 + (unit + 16))
                    for r in range(4):
                        t = 4 * (unit % 4) + r
                        last = pe.matmul(rstd_ps[:, r * P:(r + 1) * P], K.select16[:, t, :], rows[:, unit // 4 % 2, :], start=True, stop=True)
                    last.then_inc(spread, 1)

                def project(g, unit):
                    pe.wait_ge(scaled, g * 32 + (unit + 17))
                    pe.wait_ge(sig, g * 32 + (unit + 1))
                    pe.matmul(g_ps[:], K.Wgi[:], xc[:, unit % 2, :], start=True, stop=True).then_inc(g_done, 1)
                    pe.wait_ge(h_ready, g * 32 + (unit + 2))
                    pe.matmul(p_ps[:, unit % 2, :], K.Wpi[:], xc[:, unit % 2, :], start=True, stop=True).then_inc(p_done, 1)

                def turn_rows(g, unit):
                    n = unit // 2
                    for r in range(4 * unit, 4 * unit + 4):
                        last = pe.transpose(t_ps[:, n % 2, 64 * (r % 8):64 * (r % 8) + 64], h[0:64, r, :], K.ident[0:64, 0:64])
                    if unit % 2 == 1:
                        last.then_inc(h_turned, 1)

                def turn_columns(g, n):
                    if n < 2:
                        wait_apart(rows_copied, g * 16 + (n + 15))
                    elif n >= 4:
                        wait_apart(cols_kept, g * 16 + (n - 1))
                    for j in range(8 * n, 8 * n + 8):
                        last = pe.transpose(column_bank(n)[:, 64 * (j % 8):64 * (j % 8) + 64], h[64:128, :, j], K.ident[64:128, 64:128])
                    last.then_inc(h_turned, 1)

                for unit in range(8):
                    turn_tokens(0, unit)
                turn_parts(0, 0, 6)
                spread_scale(0, 0)
                with pe.Fori(0, last_region) as g:
                    pe.wait_ge(cols_kept, g * 16 + 2)
                    for q in range(GROUPS):
                        for n in range(4):
                            unit = 4 * q + n
                            spread_scale(g, unit + 1)
                            if unit % 2 == 1:
                                if unit // 2 >= 2:
                                    pe.wait_ge(rows_copied, g * 16 + (unit // 2 - 1))
                            project(g, unit)
                            if n == 2:
                                turn_parts(g, q + 1, unit + 6)
                            if unit >= 1:
                                turn_rows(g, unit - 1)
                            turn_tokens(g, unit + 8, q + 2 if n == 2 else 0)
                    wait_apart(h_ready, g * 32 + 34)
                    turn_rows(g, 31)
                    for n in range(16):
                        turn_columns(g, n)


def stage6_triangles(nc, K, h_d, y_d, r_d, N):
    RB, D, SLOTS = N // P, 64, 4
    with ExitStack() as stack:
        s = Scope(nc, stack, "s6")
        at, bt = s.sbuf("at", [P, SLOTS, RB, N]), s.sbuf("bt", [P, SLOTS, RB, N])
        ab = s.sbuf("ab", [P, 2, 2, 2, RB, N], FP16)
        y = s.sbuf("y", [P, 4, RB, N])
        square = s.sbuf("square", [P, 2, RB, N])
        total, total2 = s.sbuf("total", [P, RB, N]), s.sbuf("total2", [P, RB, N])
        parts = s.sbuf("parts", [P, RB, 3, N], BF16)
        y_ps = s.psum("y_ps", [P, 8, BANK])
        rounded, rest_ready = s.sem("rounded"), s.sem("rest_ready")
        loaded, stored, left = s.sems("loaded", SLOTS), s.sem("stored"), s.sem("left")
        zeroed, product, copied, squared, summed, chain, var_ready, dev_ready, parts_ready, parts_stored = [
            s.sem(n) for n in ("zeroed", "product", "copied", "squared", "summed", "chain", "var_ready", "dev_ready", "parts_ready", "parts_stored")]
        GROUP = 4

        @block_of(nc)
        def _(block):
            @block.sync
            def _(sp):
                for t in range(2):
                    with sp.Fori(0, 32 // GROUP) as r:
                        for u in range(GROUP):
                            sp.wait_ge(rest_ready, r * GROUP + (32 * t + u + 1))
                            sp.dma_start(at[:, u, :, :], h_d[t, :, :, bass.ds(r * GROUP + u, 1), :].rearrange("k p a i -> p k (a i)")).then_inc(loaded[u], 16)
                            sp.dma_start(bt[:, u, :, :], h_d[t, :, :, bass.ds(r * GROUP + (32 + u), 1), :].rearrange("k p a i -> p k (a i)")).then_inc(loaded[u], 16)

            @block.tensor
            def _(pe):
                with pe.Fori(0, D // GROUP) as r:
                    for u in range(GROUP):
                        pe.wait_ge(rest_ready, r * GROUP + (u + 5))
                        for ib in range(RB):
                            n = u * RB + ib
                            pe.wait_ge(copied, r * (GROUP * RB) + (n + 1))
                            terms = [(kb, a, b) for kb in range(RB) for a, b in ((0, 0), (0, 1), (1, 0))]
                            for m, (kb, a, b) in enumerate(terms):
                                last = pe.matmul(y_ps[:, n % 8, 0:N], ab[:, u % 2, 0, a, kb, ib * P:(ib + 1) * P],
                                                 ab[:, u % 2, 1, b, kb, :], start=m == 0, stop=m == len(terms) - 1)
                            last.then_inc(product, 1)

            @block.scalar
            def _(act):
                act.sem_inc(copied, 8)

                def round_high(r, u):
                    r, u = r + u // GROUP, u % GROUP
                    act.wait_ge(loaded[u], r * 32 + 32)
                    act.activation(ab[:, u % 2, 0, 0, :, :], at[:, u, :, :], ACT.Copy)
                    act.activation(ab[:, u % 2, 1, 0, :, :], bt[:, u, :, :], ACT.Copy).then_inc(rounded, 1)

                def channel(r, u, last=False):
                    act.wait_ge(left, r * GROUP + (u + 1))
                    act.wait_ge(summed, r * (2 * GROUP) + (2 * u + 2))
                    for ib in range(RB):
                        n = u * RB + ib
                        act.wait_ge(product, r * (GROUP * RB) + (n + 1))
                        act.activation(y[:, u, ib, :], y_ps[:, n % 8, 0:N], ACT.Copy).then_inc(copied, 1)
                    if not (last and u + 2 >= GROUP):
                        round_high(r, u + 2)
                    act.wait_ge(copied, r * (GROUP * RB) + ((u + 1) * RB + 8))
                    act.wait_ge(summed, r * (2 * GROUP) + (2 * u + 6))
                    act.activation(square[:, u % 2, :, :], y[:, u, :, :], ACT.Square).then_inc(squared, 1)

                for u in range(2):
                    round_high(0, u)
                with act.Fori(0, D // GROUP - 1) as r:
                    for u in range(GROUP):
                        channel(r, u)
                for u in range(GROUP):
                    channel(D // GROUP - 1, u, last=True)
                act.wait_ge(var_ready, 1)
                act.activation(total2[:], total[:], ACT.Sqrt).then_inc(dev_ready, 1)

            @block.gpsimd
            def _(pool):
                pool.sem_inc(left, 4)
                with pool.Fori(0, D // GROUP) as r:
                    for u in range(GROUP):
                        pool.wait_ge(copied, r * (GROUP * RB) + ((u + 1) * RB + 8))
                        pool.dma_start(y_d[bass.ds(r * GROUP + u, 1)].rearrange("a (b p) j -> p (a b) j", p=P),
                                       y[:, u, :, :]).then_inc(stored, 16)
                        pool.wait_ge(stored, r * (GROUP * 16) + (u + 1) * 16)
                        pool.sem_inc(left, 1)
                pool.wait_ge(parts_ready, 1)
                pool.dma_start(r_d.rearrange("(b p) k j -> p b k j", p=P), parts[:]).then_inc(parts_stored, 16)
                pool.wait_ge(parts_stored, 16)

            @block.vector
            def _(dve):
                dve.memset(total[:], 0.0).then_inc(zeroed, 1)
                dve.memset(total2[:], 0.0).then_inc(zeroed, 1)
                dve.wait_ge(zeroed, 2)
                dve.sem_inc(summed, 8)
                dve.sem_inc(rest_ready, SLOTS)

                def rest(r, u):
                    dve.wait_ge(rounded, r * GROUP + (u + 1))
                    for m, operand in enumerate((at, bt)):
                        last = dve.tensor_tensor(ab[:, u % 2, m, 1, :, :], operand[:, u % GROUP, :, :], ab[:, u % 2, m, 0, :, :],
                                                 ALU.subtract)
                    last.then_inc(rest_ready, 1)

                def channel(r, u, last=False):
                    if not (last and u + 2 >= GROUP):
                        rest(r, u + 2)
                    dve.wait_ge(summed, r * (2 * GROUP) + (2 * u + 8))
                    dve.wait_ge(squared, r * GROUP + (u + 1))
                    dve.tensor_tensor(total[:], total[:], y[:, u, :, :], ALU.add).then_inc(summed, 1)
                    dve.tensor_tensor(total2[:], total2[:], square[:, u % 2, :, :], ALU.add).then_inc(summed, 1)

                for u in range(2):
                    rest(0, u)
                with dve.Fori(0, D // GROUP - 1) as r:
                    for u in range(GROUP):
                        channel(r, u)
                for u in range(GROUP):
                    channel(D // GROUP - 1, u, last=True)
                dve.wait_ge(summed, 2 * D + 8)
                n = 0

                def step(ins):
                    nonlocal n
                    ins.then_inc(chain, 1)
                    n += 1
                    dve.wait_ge(chain, n)

                step(dve.tensor_scalar(total[:], total[:], 1.0 / D, None, ALU.mult))
                step(dve.tensor_tensor(total[:], total[:], total[:], ALU.mult))
                step(dve.scalar_tensor_tensor(total[:], total2[:], 1.0 / D, total[:], ALU.mult, ALU.subtract))
                dve.tensor_scalar(total[:], total[:], LN_EPS, None, ALU.add).then_inc(var_ready, 1)
                dve.wait_ge(dev_ready, 1)
                step(dve.reciprocal(total[:], total2[:]))
                for part in range(3):
                    step(dve.tensor_copy(parts[:, :, part, :], total[:]))
                    if part < 2:
                        step(dve.tensor_tensor(total[:], total[:], parts[:, :, part, :], ALU.subtract))
                dve.nop().then_inc(parts_ready, 1)


def stage7_layer1(nc, K, y_d, r_d, x1_d, out, N):
    CB, PAIRS = N // P, 4
    y_v = y_d.rearrange("d (r e) j -> e d r j", e=2)
    r_v = r_d.rearrange("(r e) k j -> (e k) r j", e=2)
    out_v = out.rearrange("(i q p) c -> p i q c", q=CB, p=P)
    with ExitStack() as stack:
        s = Scope(nc, stack, "s7")
        yt = s.sbuf("yt", [P, 2, 2, N])
        rt = s.sbuf("rt", [6, 2, PAIRS // 2, N], BF16)
        x1t = s.sbuf("x1t", [P, 4, 2, N])
        yn = s.sbuf("yn", [P, 2, N])
        high, low = s.sbuf("high", [P, 2, N], FP16), s.sbuf("low", [P, 2, N], FP16)
        gate = s.sbuf("gate", [P, 2, N])
        gated = s.sbuf("gated", [P, 2, N])
        oT = s.sbuf("oT", [P, 4, N])
        ot = s.sbuf("ot", [P, 4, 2, CB, P])
        r_ps = s.psum("r_ps", [P, BANK])
        p_ps = s.psum("p_ps", [P, 2, BANK])
        g_ps = s.psum("g_ps", [P, 2, BANK])
        o_ps = s.psum("o_ps", [P, 2, BANK])
        y_loaded, x_loaded, stored = s.sems("y_loaded", 2), s.sems("x_loaded", 4), s.sems("stored", 4)
        rounded, rest_ready = s.sem("rounded"), s.sem("rest_ready")
        spread, scaled, p_done, g_done, sig, mixed, added, turned, kept = [
            s.sem(n) for n in ("spread", "scaled", "p_done", "g_done", "sig", "mixed", "added", "turned", "kept")]
        ROWS = 2 * PAIRS

        @block_of(nc)
        def _(block):
            @block.sync
            def _(sp):
                with sp.Fori(0, N // ROWS) as r:
                    for n in range(PAIRS):
                        if n % 2 == 0:
                            sp.wait_ge(scaled, r * PAIRS + (n + 2))
                            for e in range(2):
                                sp.dma_start(yt[64 * e:64 * e + 64, n // 2, :, :],
                                             y_v[e, :, bass.ds(r * PAIRS + n, 2), :]).then_inc(y_loaded[n // 2], 16)
                            sp.dma_start(rt[:, n // 2, :, :], r_v[:, bass.ds(r * PAIRS + n, 2), :]).then_inc(y_loaded[n // 2], 16)
                        sp.wait_ge(added, r * ROWS + (2 * n + 2))
                        sp.dma_start(x1t[:, n, :, :], x1_d[:, bass.ds(r * ROWS + 2 * n, 2), :]).then_inc(x_loaded[n], 16)

            @block.tensor
            def _(pe):
                pe.sem_inc(turned, 4)
                pe.sem_inc(p_done, 4)

                def spread_scale(r, n):
                    r, n = r + n // PAIRS, n % PAIRS
                    if n % 2 == 0:
                        pe.wait_ge(y_loaded[n // 2], r * 48 + 48)
                    pe.wait_ge(scaled, r * PAIRS + (n + 4))
                    pe.matmul(r_ps[:, 0:N], K.halves[:], rt[:, n // 2, n % 2, :], start=True, stop=True).then_inc(spread, 1)

                def product(dst, weights, e, n):
                    pe.matmul(dst, weights[:, 0, e, :], high[:, n % 2, :], start=True, stop=False)
                    pe.matmul(dst, weights[:, 1, e, :], high[:, n % 2, :], start=False, stop=False)
                    return pe.matmul(dst, weights[:, 0, e, :], low[:, n % 2, :], start=False, stop=True)

                def project(r, row):
                    n, e = row // 2, row % 2
                    if e == 0:
                        pe.wait_ge(rest_ready, r * PAIRS + (n + 1))
                    pe.wait_ge(mixed, r * ROWS + (row + 1))
                    product(g_ps[:, e, 0:N], K.Wgo, e, n).then_inc(g_done, 1)
                    product(p_ps[:, e, 0:N], K.Wpo, e, n).then_inc(p_done, 1)

                def turn(r, row):
                    pe.wait_ge(kept, r * ROWS + (row + 1))
                    pe.wait_ge(added, r * ROWS + (row + 9))
                    for q in range(CB):
                        last = pe.transpose(o_ps[:, row % 2, q * P:(q + 1) * P], oT[:, row % 4, q * P:(q + 1) * P], K.ident[:])
                    last.then_inc(turned, 1)

                def step(r, row, last=False):
                    if row % 2 == 0 and not (last and row // 2 + 2 >= PAIRS):
                        spread_scale(r, row // 2 + 2)
                    if not (last and row + 2 >= ROWS):
                        project(r, row + 2)
                    turn(r, row)

                spread_scale(0, 0)
                spread_scale(0, 1)
                project(0, 0)
                project(0, 1)
                with pe.Fori(0, N // ROWS - 1) as r:
                    for row in range(ROWS):
                        step(r, row)
                for row in range(ROWS):
                    step(N // ROWS - 1, row, last=True)

            @block.vector
            def _(dve):
                dve.sem_inc(scaled, 4)
                dve.sem_inc(mixed, 2)

                def scale(r, n):
                    dve.wait_ge(spread, r * PAIRS + (n + 1))
                    dve.tensor_tensor(yn[:, n % 2, :], yt[:, n // 2 % 2, n % 2, :], r_ps[:, 0:N], ALU.mult).then_inc(scaled, 1)

                def rest(r, n):
                    dve.wait_ge(rounded, r * PAIRS + (n + 1))
                    dve.tensor_tensor(low[:, n % 2, :], yn[:, n % 2, :], high[:, n % 2, :], ALU.subtract).then_inc(rest_ready, 1)

                def mix(r, row):
                    dve.wait_ge(sig, r * ROWS + (row + 1))
                    dve.wait_ge(p_done, r * ROWS + (row + 5))
                    dve.wait_ge(added, r * ROWS + (row + 7))
                    dve.scalar_tensor_tensor(gated[:, row % 2, :], p_ps[:, row % 2, 0:N], K.po_bias[:], gate[:, row % 2, :],
                                             ALU.add, ALU.mult).then_inc(mixed, 1)

                def step(r, row, last=False):
                    mix(r, row)
                    if not (last and row // 2 + 2 >= PAIRS):
                        (rest if row % 2 else scale)(r, row // 2 + 2)

                for n in range(2):
                    scale(0, n)
                    rest(0, n)
                with dve.Fori(0, N // ROWS - 1) as r:
                    for row in range(ROWS):
                        step(r, row)
                for row in range(ROWS):
                    step(N // ROWS - 1, row, last=True)

            @block.scalar
            def _(act):
                act.sem_inc(kept, 2)

                def keep(r, row):
                    act.wait_ge(turned, r * ROWS + (row + 5))
                    if row % 2 == 0:
                        act.wait_ge(stored[row // 2], r * 16 + 16)
                    act.activation(ot[:, row // 2, row % 2, :, :], o_ps[:, row % 2, 0:N].rearrange("p (q c) -> p q c", c=P),
                                   ACT.Identity).then_inc(kept, 1)
                    if row % 2 == 1:
                        act.wait_ge(kept, r * ROWS + (row + 3))
                        act.dma_start(out_v[:, bass.ds(r * ROWS + row - 1, 2)], ot[:, row // 2, :, :, :]).then_inc(stored[row // 2], 16)

                for n in range(4):
                    act.sem_inc(stored[n], 16)
                def round_high(r, n):
                    act.wait_ge(scaled, r * PAIRS + (n + 5))
                    act.wait_ge(p_done, r * ROWS + (2 * n + 2))
                    act.activation(high[:, n % 2, :], yn[:, n % 2, :], ACT.Identity).then_inc(rounded, 1)

                def open_gate(r, row):
                    act.wait_ge(g_done, r * ROWS + (row + 1))
                    act.wait_ge(mixed, r * ROWS + (row + 1))
                    act.activation(gate[:, row % 2, :], g_ps[:, row % 2, 0:N], ACT.Sigmoid, bias=K.go_bias[:]).then_inc(sig, 1)

                def step(r, row, last=False):
                    if not (last and row + 2 >= ROWS):
                        open_gate(r, row + 2)
                    if row % 2 == 0 and not (last and row // 2 + 2 >= PAIRS):
                        round_high(r, row // 2 + 2)
                    keep(r, row)

                round_high(0, 0)
                round_high(0, 1)
                open_gate(0, 0)
                open_gate(0, 1)
                with act.Fori(0, N // ROWS - 1) as r:
                    for row in range(ROWS):
                        step(r, row)
                for row in range(ROWS):
                    step(N // ROWS - 1, row, last=True)
                for n in range(4):
                    act.wait_ge(stored[n], N // ROWS * 16 + 16)

            @block.gpsimd
            def _(pool):
                pool.sem_inc(added, 8)
                with pool.Fori(0, N // ROWS) as r:
                    for row in range(ROWS):
                        if row % 2 == 0:
                            pool.wait_ge(x_loaded[row // 2], r * 16 + 16)
                        pool.wait_ge(mixed, r * ROWS + (row + 3))
                        pool.wait_ge(turned, r * ROWS + (row + 1))
                        pool.tensor_tensor(oT[:, row % 4, :], gated[:, row % 2, :], x1t[:, row // 2, row % 2, :], ALU.add).then_inc(added, 1)


class Constants:
    pass


def pair_layers(nc, x, W, out):
    N = x.shape[0]
    x_flat = x.rearrange("i j c -> (i j) c")
    out_flat = out.rearrange("i j c -> (i j) c")
    RB = N // P
    a_d = nc.dram_tensor("a_d", [RB, P, 16, N], FP32, kind="Internal").ap()
    b_d = nc.dram_tensor("b_d", [RB, P, 16, N], FP32, kind="Internal").ap()
    z_d = nc.dram_tensor("z_d", [32, N, N], FP16, kind="Internal").ap()
    x1_d = nc.dram_tensor("x1_d", [P, N, N], FP32, kind="Internal").ap()
    h_d = nc.dram_tensor("h_d", [2, RB, P, 64, N], FP32, kind="Internal").ap()
    y_d = nc.dram_tensor("y_d", [64, N, N], FP32, kind="Internal").ap()
    r_d = nc.dram_tensor("r_d", [N, 3, N], BF16, kind="Internal").ap()
    with ExitStack() as stack:
        s = Scope(nc, stack, "k")
        K = Constants()
        K.ident, K.ident_bf = s.sbuf("ident", [P, P]), s.sbuf("ident_bf", [P, P], BF16)
        K.group_mean = s.sbuf("group_mean", [P, P])
        K.select16, K.halves = s.sbuf("select16", [48, 16, P], BF16), s.sbuf("halves", [6, P], BF16)
        K.mean_col = s.sbuf("mean_col", [P, 1])
        K.minus_half = s.sbuf("minus_half", [P, 16])
        K.Wab_high, K.Wab_low = s.sbuf("Wab_high", [P, 64], FP16), s.sbuf("Wab_low", [P, 64], FP16)
        K.bias_ab = s.sbuf("bias_ab", [P, 64])
        K.Wg, K.bg = s.sbuf("Wg", [P, P]), s.sbuf("bg", [P, 1])
        K.Wz, K.z_bias = s.sbuf("Wz", [64, P], FP16), s.sbuf("z_bias", [P, 1])
        K.Wpi, K.Wgi, K.pi_bias, K.gi_bias = s.sbuf("Wpi", [P, P]), s.sbuf("Wgi", [P, P]), s.sbuf("pi_bias", [P, 1]), s.sbuf("gi_bias", [P, 1])
        K.Wpo, K.Wgo, K.po_bias, K.go_bias = s.sbuf("Wpo", [P, 2, 2, P], FP16), s.sbuf("Wgo", [P, 2, 2, P], FP16), s.sbuf("po_bias", [P, 1]), s.sbuf("go_bias", [P, 1])
        K.gn_mean, K.gn_scale, K.gn_shift = s.sbuf("gn_mean", [P, 1]), s.sbuf("gn_scale", [P, 1]), s.sbuf("gn_shift", [P, 1])
        prepare(nc, K, W)
        stage1_statistics(nc, K, x_flat, N)
        stage2_gates(nc, K, x_flat, a_d, b_d, N)
        stage3_triangle(nc, K, a_d, b_d, z_d, N)
        stage4_layer0(nc, K, x_flat, z_d, x1_d, N)
        stage5_project(nc, K, x1_d, W["mask"], h_d, N)
        stage6_triangles(nc, K, h_d, y_d, r_d, N)
        stage7_layer1(nc, K, y_d, r_d, x1_d, out_flat, N)


_WEIGHTS = {
    "Wa1": "L0_conv_Wa1", "ba1": "L0_conv_ba1", "Wa2": "L0_conv_Wa2", "ba2": "L0_conv_ba2",
    "Wb1": "L0_conv_Wb1", "bb1": "L0_conv_bb1", "Wb2": "L0_conv_Wb2", "bb2": "L0_conv_bb2",
    "ln2_g0": "L0_conv_ln2_g", "ln2_b0": "L0_conv_ln2_b", "Wg": "L0_conv_Wg", "bg": "L0_conv_bg",
    "Wz": "L0_conv_Wz", "bz": "L0_conv_bz", "mask": "L1_conv_mask", "ln1_w": "L1_conv_ln1_w",
    "ln1_b": "L1_conv_ln1_b", "pi_w": "L1_conv_pi_w", "pi_b": "L1_conv_pi_b", "gi_w": "L1_conv_gi_w",
    "gi_b": "L1_conv_gi_b", "ln2_w": "L1_conv_ln2_w", "ln2_b": "L1_conv_ln2_b", "po_w": "L1_conv_po_w",
    "po_b": "L1_conv_po_b", "go_w": "L1_conv_go_w", "go_b": "L1_conv_go_b",
}


def kernel(**inputs):
    import numpy as np
    import concourse.bacc as bacc
    from concourse.bass_utils import run_bass_kernel_spmd

    nc = bacc.Bacc("TRN2", target_bir_lowering=False, num_devices=1)
    arrays, weights = {}, {}

    def give(name, array):
        array = np.ascontiguousarray(array)
        arrays[f"in_{name}"] = array
        return nc.dram_tensor(f"in_{name}", array.shape, FP32, kind="ExternalInput").ap()

    x = give("x", inputs["x"][0])
    for short, name in _WEIGHTS.items():
        weights[short] = give(short, inputs[name][0] if short == "mask" else inputs[name])
    out = nc.dram_tensor("out", arrays["in_x"].shape, FP32, kind="ExternalOutput").ap()
    pair_layers(nc, x, weights, out)
    result = run_bass_kernel_spmd(nc, [arrays], core_ids=[0]).results[0]["out"]
    return result[None]
```
